# Optimizing a Trainium2 kernel written in Bass

```python
import numpy as np
import jax
import jax.numpy as jnp

def _softmax(x, axis=-1):
    return jax.nn.softmax(x, axis=axis)

def _gelu(x):
    return jax.nn.gelu(x, approximate=True)

def _silu(x):
    return jax.nn.silu(x)

def _sigmoid(x):
    return jax.nn.sigmoid(x)

def _layernorm(x, axis=-1, eps=1e-05):
    m = jnp.mean(x, axis=axis, keepdims=True)
    v = jnp.var(x, axis=axis, keepdims=True)
    return (x - m) / jnp.sqrt(v + eps)

def _scatter_add(tgt, idx, src, axis=0):
    return tgt.at[idx].add(src)

def _segment_sum(src, seg, n):
    return jax.ops.segment_sum(src, seg, n)
kernel_name = 'mk_audio_tower_d1_tok_audfeat512_r4_67791e'

def setup_inputs(seed: int=0):
    np.random.seed(seed)
    _w = jnp.asarray

    def _rec_inputs():
        import jax
        import jax.numpy as jnp
        _rk = jax.random.key(seed)
        x = -0.000520686 + 1.00062 * jax.random.normal(jax.random.fold_in(_rk, 1), (32, 375, 128), jnp.float32)
        return x
    x = _rec_inputs()

    def _L0_tok_setup():
        import jax, jax.numpy as jnp
        import numpy as np
        D_MODEL = 128
        N_HEADS = 8
        D_FF = 512
        EPS = 1e-05

        def _layernorm(x, g, b):
            mu = jnp.mean(x, axis=-1, keepdims=True)
            var = jnp.mean(jnp.square(x - mu), axis=-1, keepdims=True)
            return (x - mu) * jax.lax.rsqrt(var + EPS) * g + b

        def _forward(x, qkv_w, qkv_b, out_w, out_b, ffn_w1, ffn_b1, ffn_w2, ffn_b2, n1_g, n1_b, n2_g, n2_b, conv_w, conv_b, cn_g, cn_b):
            B, N, C = x.shape
            H, dk = (N_HEADS, C // N_HEADS)
            scale = 1.0 / np.sqrt(dk)
            qkv = (x @ qkv_w + qkv_b).reshape(B, N, 3, H, dk)
            q, k, v = (jnp.moveaxis(qkv, (2, 3), (0, 2))[i] for i in range(3))
            scores = jnp.einsum('bhnd,bhmd->bhnm', q, k) * scale
            M = jnp.max(scores, axis=-1) - jnp.mean(scores, axis=-1)
            n_top = max(1, min(int(N * 0.25), N - 1))
            _, top_idx = jax.lax.top_k(M, n_top)
            bidx = jnp.arange(B)[:, None, None]
            hidx = jnp.arange(H)[None, :, None]
            row_sel = jnp.zeros((B, H, N), bool).at[bidx, hidx, top_idx].set(True)
            attn = jax.nn.softmax(jnp.where(row_sel[..., None], scores, -1000000000.0), axis=-1)
            out = jnp.einsum('bhnm,bhmd->bhnd', attn, v)
            out = out.transpose(0, 2, 1, 3).reshape(B, N, C)
            attn_out = out @ out_w + out_b
            x = _layernorm(x + attn_out, n1_g, n1_b)
            h = jax.nn.gelu(x @ ffn_w1 + ffn_b1, approximate=False)
            ffn_out = h @ ffn_w2 + ffn_b2
            x = _layernorm(x + ffn_out, n2_g, n2_b)
            xc = x.transpose(0, 2, 1)
            xc = jnp.concatenate([xc[..., -1:], xc, xc[..., :1]], axis=-1)
            xc = jax.lax.conv_general_dilated(xc, conv_w, window_strides=(1,), padding='VALID', dimension_numbers=('NCH', 'OIH', 'NCH')) + conv_b[None, :, None]
            neg = jnp.finfo(xc.dtype).min
            xc = jax.lax.reduce_window(xc, neg, jax.lax.max, window_dimensions=(1, 1, 3), window_strides=(1, 1, 2), padding=((0, 0), (0, 0), (1, 1)))
            x = xc.transpose(0, 2, 1)
            x = _layernorm(jax.nn.elu(x), cn_g, cn_b)
            return x
        key = jax.random.key(seed)
        ks = jax.random.split(key, 12)
        B, N, C = (2, 512, D_MODEL)
        s = lambda fi, fo: 1.0 / np.sqrt(fi)
        inp = {'x': jax.random.normal(ks[0], (B, N, C), jnp.float32), 'qkv_w': jax.random.normal(ks[1], (C, 3 * C), jnp.float32) * s(C, 3 * C), 'qkv_b': jnp.zeros((3 * C,), jnp.float32), 'out_w': jax.random.normal(ks[2], (C, C), jnp.float32) * s(C, C), 'out_b': jnp.zeros((C,), jnp.float32), 'ffn_w1': jax.random.normal(ks[3], (C, D_FF), jnp.float32) * s(C, D_FF), 'ffn_b1': jnp.zeros((D_FF,), jnp.float32), 'ffn_w2': jax.random.normal(ks[4], (D_FF, C), jnp.float32) * s(D_FF, C), 'ffn_b2': jnp.zeros((C,), jnp.float32), 'n1_g': jnp.ones((C,), jnp.float32), 'n1_b': jnp.zeros((C,), jnp.float32), 'n2_g': jnp.ones((C,), jnp.float32), 'n2_b': jnp.zeros((C,), jnp.float32), 'conv_w': jax.random.normal(ks[5], (C, C, 3), jnp.float32) * s(3 * C, C), 'conv_b': jnp.zeros((C,), jnp.float32), 'cn_g': jnp.ones((C,), jnp.float32), 'cn_b': jnp.zeros((C,), jnp.float32)}
        return inp
    _L0_tok_all = _L0_tok_setup()
    _L0_tok_in = {k: v for k, v in _L0_tok_all.items() if k in ('qkv_w', 'qkv_b', 'out_w', 'out_b', 'ffn_w1', 'ffn_b1', 'ffn_w2', 'ffn_b2', 'n1_g', 'n1_b', 'n2_g', 'n2_b', 'conv_w', 'conv_b', 'cn_g', 'cn_b')}
    del _L0_tok_all

    def _L0_attn_setup():
        import jax, jax.numpy as jnp
        import numpy as np
        B, N, IN_F, OUT_F, HEAD_D = (4, 1024, 128, 128, 64)
        THRESHOLD_LAMBDA_MIN = 0.001
        key = jax.random.key(seed)
        kx, kq, kk, kv = jax.random.split(key, 4)
        x = jax.random.normal(kx, (B, N, IN_F), dtype=jnp.float32)
        s = 1.0 / np.sqrt(IN_F)
        Wq = jax.random.uniform(kq, (HEAD_D, IN_F), dtype=jnp.float32, minval=-s, maxval=s)
        Wk = jax.random.uniform(kk, (HEAD_D, IN_F), dtype=jnp.float32, minval=-s, maxval=s)
        Wv = jax.random.uniform(kv, (OUT_F, IN_F), dtype=jnp.float32, minval=-s, maxval=s)
        log_lambda = jnp.zeros((1,), dtype=jnp.float32)
        return {'x': x, 'Wq': Wq, 'Wk': Wk, 'Wv': Wv, 'log_lambda': log_lambda}
    _L0_attn_all = _L0_attn_setup()
    _L0_attn_in = {k: v for k, v in _L0_attn_all.items() if k in ('Wq', 'Wk', 'Wv', 'log_lambda')}
    del _L0_attn_all

    def _L0_ffn_setup():
        import jax, jax.numpy as jnp
        import numpy as np
        B, T, D, F, E, K = (8, 256, 128, 512, 8, 2)

        def _moe_forward(x, Wr, br, W1, b1, W2, b2):
            Bx, Tx, Dx = x.shape
            xf = x.reshape(-1, Dx)
            logits = xf @ Wr + br
            probs = jax.nn.softmax(logits, axis=-1)
            vals, idx = jax.lax.top_k(probs, K)
            cw = (jax.nn.one_hot(idx, E, dtype=x.dtype) * vals[..., None]).sum(axis=1)

            def body(acc, params):
                W1e, b1e, W2e, b2e, cwe = params
                h = jax.nn.relu(xf @ W1e + b1e)
                y = h @ W2e + b2e
                return (acc + cwe[:, None] * y, None)
            out, _ = jax.lax.scan(body, jnp.zeros_like(xf), (W1, b1, W2, b2, cw.T))
            return out.reshape(Bx, Tx, Dx)
        key = jax.random.key(seed)
        k0, k1, k2, k3 = jax.random.split(key, 4)
        s_d = 1.0 / np.sqrt(D)
        s_f = 1.0 / np.sqrt(F)
        return {'x': jax.random.normal(k0, (B, T, D), jnp.float32), 'Wr': jax.random.uniform(k1, (D, E), jnp.float32, -s_d, s_d), 'br': jnp.zeros((E,), jnp.float32), 'W1': jax.random.uniform(k2, (E, D, F), jnp.float32, -s_d, s_d), 'b1': jnp.zeros((E, F), jnp.float32), 'W2': jax.random.uniform(k3, (E, F, D), jnp.float32, -s_f, s_f), 'b2': jnp.zeros((E, D), jnp.float32)}
    _L0_ffn_all = _L0_ffn_setup()
    _L0_ffn_in = {k: v for k, v in _L0_ffn_all.items() if k in ('Wr', 'br', 'W1', 'b1', 'W2', 'b2')}
    del _L0_ffn_all
    return {'x': x, 'L0_tok_qkv_w': _L0_tok_in['qkv_w'], 'L0_tok_qkv_b': _L0_tok_in['qkv_b'], 'L0_tok_out_w': _L0_tok_in['out_w'], 'L0_tok_out_b': _L0_tok_in['out_b'], 'L0_tok_ffn_w1': _L0_tok_in['ffn_w1'], 'L0_tok_ffn_b1': _L0_tok_in['ffn_b1'], 'L0_tok_ffn_w2': _L0_tok_in['ffn_w2'], 'L0_tok_ffn_b2': _L0_tok_in['ffn_b2'], 'L0_tok_n1_g': _L0_tok_in['n1_g'], 'L0_tok_n1_b': _L0_tok_in['n1_b'], 'L0_tok_n2_g': _L0_tok_in['n2_g'], 'L0_tok_n2_b': _L0_tok_in['n2_b'], 'L0_tok_conv_w': _L0_tok_in['conv_w'], 'L0_tok_conv_b': _L0_tok_in['conv_b'], 'L0_tok_cn_g': _L0_tok_in['cn_g'], 'L0_tok_cn_b': _L0_tok_in['cn_b'], 'L0_attn_Wq': _L0_attn_in['Wq'], 'L0_attn_Wk': _L0_attn_in['Wk'], 'L0_attn_Wv': _L0_attn_in['Wv'], 'L0_attn_log_lambda': _L0_attn_in['log_lambda'], 'L0_ffn_Wr': _L0_ffn_in['Wr'], 'L0_ffn_br': _L0_ffn_in['br'], 'L0_ffn_W1': _L0_ffn_in['W1'], 'L0_ffn_b1': _L0_ffn_in['b1'], 'L0_ffn_W2': _L0_ffn_in['W2'], 'L0_ffn_b2': _L0_ffn_in['b2']}

def reference(x, L0_tok_qkv_w, L0_tok_qkv_b, L0_tok_out_w, L0_tok_out_b, L0_tok_ffn_w1, L0_tok_ffn_b1, L0_tok_ffn_w2, L0_tok_ffn_b2, L0_tok_n1_g, L0_tok_n1_b, L0_tok_n2_g, L0_tok_n2_b, L0_tok_conv_w, L0_tok_conv_b, L0_tok_cn_g, L0_tok_cn_b, L0_attn_Wq, L0_attn_Wk, L0_attn_Wv, L0_attn_log_lambda, L0_ffn_Wr, L0_ffn_br, L0_ffn_W1, L0_ffn_b1, L0_ffn_W2, L0_ffn_b2):
    import jax
    import jax.numpy as jnp

    def _L0_tok_ref(x, qkv_w, qkv_b, out_w, out_b, ffn_w1, ffn_b1, ffn_w2, ffn_b2, n1_g, n1_b, n2_g, n2_b, conv_w, conv_b, cn_g, cn_b):
        import jax, jax.numpy as jnp
        import numpy as np
        D_MODEL = 128
        N_HEADS = 8
        D_FF = 512
        EPS = 1e-05

        def _layernorm(x, g, b):
            mu = jnp.mean(x, axis=-1, keepdims=True)
            var = jnp.mean(jnp.square(x - mu), axis=-1, keepdims=True)
            return (x - mu) * jax.lax.rsqrt(var + EPS) * g + b

        def _forward(x, qkv_w, qkv_b, out_w, out_b, ffn_w1, ffn_b1, ffn_w2, ffn_b2, n1_g, n1_b, n2_g, n2_b, conv_w, conv_b, cn_g, cn_b):
            B, N, C = x.shape
            H, dk = (N_HEADS, C // N_HEADS)
            scale = 1.0 / np.sqrt(dk)
            qkv = (x @ qkv_w + qkv_b).reshape(B, N, 3, H, dk)
            q, k, v = (jnp.moveaxis(qkv, (2, 3), (0, 2))[i] for i in range(3))
            scores = jnp.einsum('bhnd,bhmd->bhnm', q, k) * scale
            M = jnp.max(scores, axis=-1) - jnp.mean(scores, axis=-1)
            n_top = max(1, min(int(N * 0.25), N - 1))
            _, top_idx = jax.lax.top_k(M, n_top)
            bidx = jnp.arange(B)[:, None, None]
            hidx = jnp.arange(H)[None, :, None]
            row_sel = jnp.zeros((B, H, N), bool).at[bidx, hidx, top_idx].set(True)
            attn = jax.nn.softmax(jnp.where(row_sel[..., None], scores, -1000000000.0), axis=-1)
            out = jnp.einsum('bhnm,bhmd->bhnd', attn, v)
            out = out.transpose(0, 2, 1, 3).reshape(B, N, C)
            attn_out = out @ out_w + out_b
            x = _layernorm(x + attn_out, n1_g, n1_b)
            h = jax.nn.gelu(x @ ffn_w1 + ffn_b1, approximate=False)
            ffn_out = h @ ffn_w2 + ffn_b2
            x = _layernorm(x + ffn_out, n2_g, n2_b)
            xc = x.transpose(0, 2, 1)
            xc = jnp.concatenate([xc[..., -1:], xc, xc[..., :1]], axis=-1)
            xc = jax.lax.conv_general_dilated(xc, conv_w, window_strides=(1,), padding='VALID', dimension_numbers=('NCH', 'OIH', 'NCH')) + conv_b[None, :, None]
            neg = jnp.finfo(xc.dtype).min
            xc = jax.lax.reduce_window(xc, neg, jax.lax.max, window_dimensions=(1, 1, 3), window_strides=(1, 1, 2), padding=((0, 0), (0, 0), (1, 1)))
            x = xc.transpose(0, 2, 1)
            x = _layernorm(jax.nn.elu(x), cn_g, cn_b)
            return x
        return _forward(x, qkv_w, qkv_b, out_w, out_b, ffn_w1, ffn_b1, ffn_w2, ffn_b2, n1_g, n1_b, n2_g, n2_b, conv_w, conv_b, cn_g, cn_b)

    def _L0_attn_ref(x, Wq, Wk, Wv, log_lambda):
        import jax, jax.numpy as jnp
        import numpy as np
        B, N, IN_F, OUT_F, HEAD_D = (4, 1024, 128, 128, 64)
        THRESHOLD_LAMBDA_MIN = 0.001
        Q = jnp.einsum('bni,di->bnd', x, Wq)
        K = jnp.einsum('bni,di->bnd', x, Wk)
        V = jnp.einsum('bni,oi->bno', x, Wv)
        q_sq = jnp.sum(Q * Q, axis=-1)
        k_sq = jnp.sum(K * K, axis=-1)
        cross = jnp.einsum('bnd,bmd->bnm', Q, K)
        dist_sq = jnp.maximum(q_sq[:, :, None] + k_sq[:, None, :] - 2.0 * cross, 0.0)
        lam = jnp.clip(jnp.exp(log_lambda[0]), THRESHOLD_LAMBDA_MIN, None)
        logits = -dist_sq / (2.0 * lam * lam)
        attn = jax.nn.softmax(logits, axis=-1)
        out = jnp.einsum('bnm,bmo->bno', attn, V)
        return out

    def _L0_ffn_ref(x, Wr, br, W1, b1, W2, b2):
        import jax, jax.numpy as jnp
        import numpy as np
        B, T, D, F, E, K = (8, 256, 128, 512, 8, 2)

        def _moe_forward(x, Wr, br, W1, b1, W2, b2):
            Bx, Tx, Dx = x.shape
            xf = x.reshape(-1, Dx)
            logits = xf @ Wr + br
            probs = jax.nn.softmax(logits, axis=-1)
            vals, idx = jax.lax.top_k(probs, K)
            cw = (jax.nn.one_hot(idx, E, dtype=x.dtype) * vals[..., None]).sum(axis=1)

            def body(acc, params):
                W1e, b1e, W2e, b2e, cwe = params
                h = jax.nn.relu(xf @ W1e + b1e)
                y = h @ W2e + b2e
                return (acc + cwe[:, None] * y, None)
            out, _ = jax.lax.scan(body, jnp.zeros_like(xf), (W1, b1, W2, b2, cw.T))
            return out.reshape(Bx, Tx, Dx)
        return _moe_forward(x, Wr, br, W1, b1, W2, b2)
    h = _L0_tok_ref(x, L0_tok_qkv_w, L0_tok_qkv_b, L0_tok_out_w, L0_tok_out_b, L0_tok_ffn_w1, L0_tok_ffn_b1, L0_tok_ffn_w2, L0_tok_ffn_b2, L0_tok_n1_g, L0_tok_n1_b, L0_tok_n2_g, L0_tok_n2_b, L0_tok_conv_w, L0_tok_conv_b, L0_tok_cn_g, L0_tok_cn_b)
    h = h + _L0_attn_ref(_layernorm(h, axis=-1), L0_attn_Wq, L0_attn_Wk, L0_attn_Wv, L0_attn_log_lambda)
    h = h + _L0_ffn_ref(_layernorm(h, axis=-1), L0_ffn_Wr, L0_ffn_br, L0_ffn_W1, L0_ffn_b1, L0_ffn_W2, L0_ffn_b2)
    return h

_drawn_inputs = setup_inputs


def setup_inputs(seed=0):
    import zlib

    import numpy as np

    out = dict(_drawn_inputs(seed))
    spreads = {'L0_tok_qkv_b': (0.0, 0.1),
     'L0_tok_out_b': (0.0, 0.1),
     'L0_tok_ffn_b1': (0.0, 0.1),
     'L0_tok_ffn_b2': (0.0, 0.1),
     'L0_tok_n1_g': (1.0, 0.2),
     'L0_tok_n1_b': (0.0, 0.1),
     'L0_tok_n2_g': (1.0, 0.2),
     'L0_tok_n2_b': (0.0, 0.1),
     'L0_tok_conv_b': (0.0, 0.1),
     'L0_tok_cn_g': (1.0, 0.2),
     'L0_tok_cn_b': (0.0, 0.1),
     'L0_ffn_br': (0.0, 0.1),
     'L0_ffn_b1': (0.0, 0.68),
     'L0_ffn_b2': (0.0, 0.285)}
    factors = {}
    for name, (base, spread) in spreads.items():
        noise = np.random.default_rng([zlib.crc32(name.encode()), seed]).standard_normal(out[name].shape)
        drawn = base * np.exp(spread * noise) if base else spread * noise
        out[name] = jnp.asarray(drawn.astype(out[name].dtype))
    for name, factor in factors.items():
        out[name] = (out[name] * factor).astype(out[name].dtype)
    return out
```

```python
from contextlib import ExitStack

import concourse.bass as bass
import numpy as np
from concourse import mybir

ALU = mybir.AluOpType
ACT = mybir.ActivationFunctionType
AX = mybir.AxisListType
F32 = mybir.dt.float32
BF16 = mybir.dt.bfloat16
U32 = mybir.dt.uint32

B, N, C = 32, 375, 128
CH = 27
H, DK = 8, 16
TOP = max(1, min(int(N * 0.25), N - 1))
S = 96
NT, TP = 3, 125
FF = 512
NF = FF // 128
NP = (N + 1) // 2
PT_, PR = 2, 94
D2 = 64
E = 8
VW = DK + 1
VPAD = 7 * VW + S
OW = 8 * (C + DK)
EPS = 1e-5
BIG = 3.0e38
SELF_SLOT = S - 1

K_ID, K_BM, K_HM, K_TOK, K_ROW, K_M, K_E8, K_END = 0, 128, 128 + 768, 904, 907, 1282, 1284, 1292


def later(b):
    return not (isinstance(b, int) and b == 0)


def shape_constants():
    k = np.zeros((128, K_END), np.float32)
    p = np.arange(128)
    k[:, K_ID:K_ID + 128] = np.eye(128)
    k[:, K_BM:K_BM + 768] = (p[:, None] // DK == np.arange(768)[None] // S)
    k[:, K_HM:K_HM + 8] = (p[:, None] // DK == np.arange(8)[None])
    k[:, K_TOK:K_TOK + 3] = p[:, None] + TP * np.arange(3)[None]
    k[:, K_ROW:K_ROW + N] = np.arange(N)[None]
    k[:, K_M] = p == SELF_SLOT
    k[:, K_M + 1] = p != SELF_SLOT
    k[:, K_E8:K_E8 + 8] = np.arange(8)[None]
    return k


def audio_tower(nc, a, out):
    with ExitStack() as ctx:
        def sb(name, shape, dt=F32):
            return ctx.enter_context(nc.sbuf_tensor(name, shape, dt))

        def sem(name):
            return ctx.enter_context(nc.semaphore(name))

        idx_dram = nc.dram_tensor("top_idx_scratch", [2 * 128, S], F32, kind="Internal").ap()
        max_dram = nc.dram_tensor("top_max_scratch", [3, 2 * 128, S], BF16, kind="Internal").ap()

        kc = sb("shape_consts", [128, K_END])
        ident = kc[:, K_ID:K_ID + 128]
        wqkv = sb("wqkv", [128, 3 * C])
        bqkT = sb("bqkT", [128, 2])
        bqv_bc = sb("bqv_bc", [128, 2 * C])
        wo = sb("wo", [128, C])
        bo_bc = sb("bo_bc", [128, C])
        w1 = sb("w1", [128, FF])
        b1 = sb("b1", [128, NF])
        w2 = sb("w2", [128, NF, C])
        vecs = sb("vecs", [128, 6])
        cw = sb("conv_w", [128, 3, C])
        cng_bc = sb("cng_bc", [128, C])
        cnb_bc = sb("cnb_bc", [128, C])
        wqq = sb("wqq", [128, 2 * D2])
        wkk = sb("wkk", [128, 2 * D2])
        wv2 = sb("wv2", [128, C])
        lam = sb("lam", [128, 4])
        epsc = sb("epsc", [128, NT])
        euler = sb("euler", [128, 1])
        wr = sb("wr", [128, E])
        br_bc = sb("br_bc", [128, E])
        mw1 = sb("mw1", [128, E, FF])
        mb1 = sb("mb1", [128, E * NF])
        mw2 = sb("mw2", [128, E, NF, C])
        mb2 = sb("mb2", [E, C])
        mean_w = sb("mean_w", [128, S])
        ones_bf = sb("ones_bf", [3, 128], BF16)
        ones_f = sb("ones_f", [128, PR])
        mhalf = sb("mhalf", [128, NT])

        maxes = sb("maxes", [128, NT, B * H])
        xa = sb("xa", [128, NT, C])
        xTa = sb("xTa", [128, N])
        qTa = [sb(f"qTa{u}", [128, N]) for u in range(2)]
        kTa = sb("kTa", [128, N])
        ksum = sb("ksum", [128, 2])
        kpad = [sb(f"kpad{u}", [128, H, N]) for u in range(2)]
        mrow = sb("mrow", [128, N])
        mwork = sb("mwork", [128, N])
        top_v = sb("top_v", [128, S])
        top_i = sb("top_i", [128, S], U32)
        top_if = sb("top_if", [128, S])
        top_p = [sb(f"top_p{k}", [128, S], BF16) for k in range(3)]
        top_r = sb("top_r", [128, S])
        idx_col = sb("idx_col", [S, B * H])

        x = sb("x", [128, NT, C])
        xb = sb("xb", [128, NT, C])
        idx_bc = sb("idx_bc", [128, H * S])
        negmax = sb("negmax", [3, H * S], BF16)
        xT = sb("xT", [128, N])
        kT = sb("kT", [128, N])
        kTc = sb("kTc", [128, N])
        ksum_b = sb("ksum_b", [128, 2])
        qrow = sb("qrow", [128, NT, C])
        v = sb("v", [128, NT, VPAD + 1])
        pick = sb("pick", [128, NT, H * S])
        place = sb("place", [S, H, N])
        qsel = sb("qsel", [128, H * S])
        ex = sb("ex", [128, NT, H * S])
        rden = sb("rden", [S, H])
        onorm = sb("onorm", [S, H, DK])
        vmw = sb("vmw", [S, H, DK])
        opad = sb("opad", [S, OW])
        attnT = sb("attnT", [128, N])
        r1 = sb("r1", [128, NT, C])
        st = sb("st", [128, NT, 6])
        mv = sb("mv", [128, NT, 2])
        veps = sb("veps", [128, NT])
        rstd = sb("rstd", [128, NT])
        xn = sb("xn", [128, NT, C])
        x1T = sb("x1T", [128, N])
        hT = sb("hT", [128, NF, N])
        yT = sb("yT", [128, N])
        xn2 = sb("xn2", [128, NT, C])
        x2p = sb("x2p", [128, N + 2])
        cp = sb("cp", [128, N + 2])
        mx = sb("mx", [128, NP])
        emn = sb("emn", [128, NP])
        el = sb("el", [128, NP])
        xn3 = sb("xn3", [128, PT_, C])
        hrow = sb("hrow", [128, PT_, C])
        hn = sb("hn", [128, PT_, C])
        hnT = sb("hnT", [128, NP])
        qa = sb("qa", [128, NP])
        ka = sb("ka", [128, NP])
        kk = sb("kk", [128, NP])
        v2 = sb("v2", [128, PT_, C])
        d2 = sb("d2", [128, PT_, NP])
        dmin = sb("dmin", [128, PT_])
        dbias = sb("dbias", [128, PT_])
        e2 = sb("e2", [128, PT_, NP])
        rs2 = sb("rs2", [128, PT_])
        rr2 = sb("rr2", [128, PT_])
        e2T = sb("e2T", [128, PT_, NP])
        h2 = sb("h2", [128, PT_, C])
        xn4 = sb("xn4", [128, PT_, C])
        lg = sb("lg", [128, PT_, E])
        m8 = sb("m8", [128, PT_, 8])
        i8 = sb("i8", [128, PT_, 8], U32)
        i8f = sb("i8f", [128, PT_, 8])
        nm1 = sb("nm1", [128, PT_])
        elg = sb("elg", [128, PT_, E])
        e12 = sb("e12", [128, PT_, 2])
        rse = sb("rse", [128, PT_])
        rre = sb("rre", [128, PT_])
        p12 = sb("p12", [128, PT_, 2])
        gate = sb("gate", [128, PT_, E])
        gateA = sb("gateA", [128, PT_, E])
        gateT = sb("gateT", [E, NP])
        h2nT = sb("h2nT", [128, NP])
        gate_m = sb("gate_m", [128, PT_, E])
        acc = sb("acc", [128, PT_, C])
        mh = [sb(f"mh{u}", [128, NF, NP]) for u in range(2)]
        ostage = sb("ostage", [128, PT_, C])

        ps = ctx.enter_context(nc.psum_tensor("ps", [128, 8, 512], F32))

        s_w = sem("s_weights_loaded")
        s_set = sem("s_constants_set")
        s_lam = sem("s_lambda")
        s_alone = sem("s_carries_a_wait")
        s_e = sem("s_euler")
        A = {n: sem("A_" + n) for n in (
            "x_loaded x_turned xT k_proj kT_ready q_proj qT_ready mean_ready kpad_ready scores maxed".split())}
        T = {n: sem("T_" + n) for n in "turned rows idx_ready idx_turned idx_col stored chain".split()}
        names = ("x_loaded idx_loaded nm_loaded x_turned xT k_proj kT kTc qv_proj q_rows v_rows pick place gathered qsel "
                 "s0 s1 s2 e0 e1 e2 av vmean on scattered attnT oproj xb aggr1 rstd1 xn1 x1_turned x1T "
                 "f0 f1 f2 f3 g0 g1 g2 g3 ffn2 yT y_turned aggr2 rstd2 xn2 x2_turned x2T conv cp mx emn el "
                 "el_turned aggr3 rstd3 hrow aggr4 rstd4 hn hn_turned hnT qk_proj v2_proj qa ka v2 dist dclip e2x e2_turned e2T "
                 "av2 h2 aggr5 rstd5 xn4 h2n_turned h2nT router lg elg gate gate_turned gateT bias2 acc_start "
                 "out_ready out_stored").split()
        Bs = {n: sem("B_" + n) for n in names}
        m_h = [sem("M_hidden_act"), sem("M_hidden_dve")]
        m_ra = sem("M_relu_act")
        m_rd = sem("M_relu_dve")
        m_y = sem("M_y")
        m_acc = sem("M_acc")
        dch = sem("dve_chain")
        dchA = sem("dve_chain_A")
        pch = sem("pool_chain")

        loads = [
            (kc[:], a["consts"]), (wqkv[:], a["qkv_w"]), (bqkT[:], a["qk_bT"]),
            (bqv_bc[:, 0:C], a["qkv_b"][:, 0:C].to_broadcast([128, C])),
            (bqv_bc[:, C:2 * C], a["qkv_b"][:, 2 * C:3 * C].to_broadcast([128, C])),
            (wo[:], a["out_w"]), (bo_bc[:], a["out_b"].to_broadcast([128, C])),
            (w1[:], a["ffn_w1"]), (b1[:], a["ffn_b1"]),
            (w2[:], a["ffn_w2"].rearrange("(f p) c -> p f c", p=128)), (vecs[:], a["vecs"]),
            (cw[:], a["conv_w"]),
            (cng_bc[:], a["cn_g"].to_broadcast([128, C])), (cnb_bc[:], a["cn_b"].to_broadcast([128, C])),
            (wqq[:, 0:D2], a["WqT"]), (wqq[:, D2:], a["WqT"]), (wkk[:, 0:D2], a["WkT"]), (wkk[:, D2:], a["WkT"]),
            (wv2[:], a["WvT"]), (lam[:, 0:1], a["log_lambda"].to_broadcast([128, 1])),
            (wr[:], a["Wr"]), (br_bc[:], a["br"].to_broadcast([128, E])),
            (mw1[:], a["W1"].rearrange("e p f -> p e f")), (mb1[:], a["mb1"]),
            (mw2[:], a["W2"].rearrange("e (f p) c -> p e f c", p=128)), (mb2[:], a["b2"]),
        ]
        NSET = 10
        xd = a["x"].rearrange("b (t p) c -> b p t c", p=TP)
        od = out.rearrange("b (t p) c -> b p t c", p=PR)

        block = ctx.enter_context(nc.Block())

        @block.sync
        def _(sp):
            for dst, src in loads:
                sp.dma_start(dst, src).then_inc(s_w, 16)
            sp.dma_start(xa[0:TP], xd[0]).then_inc(A["x_loaded"], 16)
            with sp.Fori(1, B) as i:
                sp.wait_ge(s_set, NSET)
                sp.wait_ge(A["x_turned"], i)
                sp.dma_start(xa[0:TP], xd[bass.ds(i, 1)].rearrange("b p t c -> (b p) t c")).then_inc(A["x_loaded"], 16)
            for g in range(2):
                sp.wait_ge(T["idx_ready"], g + 1)
                sp.dma_start(idx_dram[128 * g:128 * g + 128], top_if[:]).then_inc(T["stored"], 16)
                for k in range(3):
                    sp.dma_start(max_dram[k, 128 * g:128 * g + 128], top_p[k][:]).then_inc(T["stored"], 16)
            sp.wait_ge(T["stored"], 2 * 4 * 16)
            idx_flat = idx_dram.rearrange("(b h) s -> b (h s)", h=H)
            max_flat = max_dram.rearrange("k (b h) s -> k b (h s)", h=H)

            def batch_loads(i):
                if later(i):
                    sp.wait_ge(s_set, NSET)
                    sp.wait_ge(Bs["pick"], i)
                sp.dma_start(idx_bc[0:TP], idx_flat[bass.ds(i, 1)].to_broadcast([TP, H * S])).then_inc(Bs["idx_loaded"], 16)
                if later(i):
                    sp.wait_ge(s_set, NSET)
                    sp.wait_ge(Bs["s2"], i)
                sp.dma_start(negmax[:], max_flat[:, bass.ds(i, 1)].rearrange("k b s -> k (b s)")).then_inc(Bs["nm_loaded"], 16)
                if later(i):
                    sp.wait_ge(s_set, NSET)
                    sp.wait_ge(Bs["xb"], i)
                    sp.wait_ge(Bs["x_turned"], i)
                sp.dma_start(x[0:TP], xd[bass.ds(i, 1)].rearrange("b p t c -> (b p) t c")).then_inc(Bs["x_loaded"], 16)

            batch_loads(0)
            with sp.Fori(1, B) as i:
                batch_loads(i)
            sp.wait_ge(Bs["out_stored"], 16 * B)

        @block.tensor
        def _(pe):
            mm = nc.tensor.matmul
            tr = nc.tensor.transpose

            def a_project(b, u):
                pe.wait_ge(A["x_loaded"], 16 * (b + 1))
                if later(b):
                    pe.wait_ge(A["kT_ready"], b)
                for t in range(NT):
                    last = tr(ps[:, 6, TP * t:TP * t + TP], xa[0:TP, t, :], ident[0:TP, 0:TP])
                last.then_inc(A["x_turned"], 1)
                if later(b):
                    pe.wait_ge(A["qT_ready"], b)
                pe.wait_ge(A["xT"], b + 1)
                mm(ps[:, 7, 0:N], wqkv[:, 0:C], xTa[:], start=True, stop=True).then_inc(A["q_proj"], 1)
                mm(ps[:, 6, 0:N], wqkv[:, C:2 * C], xTa[:], start=True, stop=True).then_inc(A["k_proj"], 1)

            def a_scores(b, u, first=False):
                pe.wait_ge(A["kpad_ready"], b + 1)
                pe.wait_ge(A["qT_ready"], b + 1)
                for n in range(12):
                    hp, t = n // 3, n % 3
                    if not (first and n < 3):
                        pe.wait_ge(A["maxed"], 12 * b + n - 2)
                    for k in range(2):
                        last = mm(ps[0:TP, 2 * (n % 3) + k, 0:N], qTa[u][:, TP * t:TP * t + TP],
                                  kpad[u][:, 2 * hp + k, :], start=True, stop=True)
                    last.then_inc(A["scores"], 1)

            pe.wait_ge(s_w, 16 * len(loads))
            pe.wait_ge(s_set, NSET)
            a_project(0, 0)
            a_project(1, 1)
            a_scores(0, 0, first=True)
            with pe.Fori(1, B // 2) as j:
                a_project(2 * j, 0)
                a_scores(2 * j - 1, 1)
                a_project(2 * j + 1, 1)
                a_scores(2 * j, 0)
            a_scores(B - 1, 1)

            for g in range(2):
                pe.wait_ge(A["maxed"], 12 * B)
                if g:
                    pe.wait_ge(T["rows"], 1)
                else:
                    pe.wait_ge(A["kT_ready"], B)
                for t in range(NT):
                    last = tr(ps[:, 6, TP * t:TP * t + TP], maxes[0:TP, t, 128 * g:128 * g + 128], ident[0:TP, 0:TP])
                last.then_inc(T["turned"], 1)
            for g in range(2):
                pe.wait_ge(T["idx_ready"], g + 1)
                if g:
                    pe.wait_ge(T["idx_col"], 1)
                tr(ps[0:S, 7, 0:128], top_if[:], ident).then_inc(T["idx_turned"], 1)
            pe.wait_ge(T["idx_col"], 2)

            W = Bs

            def experts(b):
                def hidden(e):
                    for half in range(2):
                        if later(b) or e:
                            pe.wait_ge((m_ra, m_rd)[half], 2 * (E * b + e))
                        for k in range(2):
                            f = 2 * half + k
                            last = mm(ps[:, 6 + half, 256 * k:256 * k + NP], mw1[:, e, 128 * f:128 * f + 128], h2nT[:],
                                      start=True, stop=True)
                        last.then_inc(m_h[half], 1)

                def down(e):
                    pe.wait_ge(m_ra, 2 * (E * b + e + 1))
                    pe.wait_ge(m_rd, 2 * (E * b + e + 1))
                    if later(b) or e:
                        pe.wait_ge(m_acc, E * b + e)
                    for t in range(PT_):
                        for f in range(NF):
                            last = mm(ps[0:PR, 5, C * t:C * t + C],
                                      mh[e % 2][:, f, PR * t:PR * t + PR], mw2[:, e, f, :],
                                      start=(f == 0), stop=(f == NF - 1))
                    last.then_inc(m_y, 1)

                hidden(0)
                for e in range(E):
                    if e + 1 < E:
                        hidden(e + 1)
                    down(e)
                    yield

            def batch(i, filler):
                pe.wait_ge(W["x_loaded"], 16 * (i + 1))
                if later(i):
                    pe.wait_ge(W["gateT"], i)
                for t in range(NT):
                    last = tr(ps[:, 4, TP * t:TP * t + TP], x[0:TP, t, :], ident[0:TP, 0:TP])
                last.then_inc(W["x_turned"], 1)
                pe.wait_ge(W["xT"], i + 1)
                mm(ps[:, 2, 0:N], wqkv[:, C:2 * C], xT[:], start=True, stop=True).then_inc(W["k_proj"], 1)
                for t in range(NT):
                    for k, w in ((0, wqkv[:, 0:C]), (1, wqkv[:, 2 * C:3 * C])):
                        last = mm(ps[0:TP, t // 2, 256 * (t % 2) + 128 * k:256 * (t % 2) + 128 * k + 128],
                                  xT[:, TP * t:TP * t + TP], w, start=True, stop=True)
                last.then_inc(W["qv_proj"], 1)
                filler()
                if later(i):
                    pe.wait_ge(W["acc_start"], i)
                pe.wait_ge(W["kT"], i + 1)
                pe.wait_ge(W["q_rows"], i + 1)
                pe.wait_ge(W["pick"], i + 1)
                for half in range(2):
                    for t in range(NT):
                        last = mm(ps[:, 2 + half, 0:384], qrow[0:TP, t, :], pick[0:TP, t, 384 * half:384 * half + 384],
                                  start=(t == 0), stop=(t == NT - 1))
                last.then_inc(W["gathered"], 1)
                filler()
                pe.wait_ge(W["qsel"], i + 1)
                pe.wait_ge(W["kTc"], i + 1)
                pe.wait_ge(W["v_rows"], i + 1)
                pe.wait_ge(W["nm_loaded"], 16 * (i + 1))
                for t in range(NT):
                    if t == 2:
                        pe.wait_ge(W["e0"], i + 1)
                    for half in range(2):
                        bank = ps[0:TP, 2 * (t % 2) + half, 0:384]
                        mm(bank, kTc[:, TP * t:TP * t + TP], qsel[:, 384 * half:384 * half + 384], start=True, stop=False)
                        last = mm(bank, ones_bf[0:3, 0:TP], negmax[:, 384 * half:384 * half + 384], start=False, stop=True)
                    last.then_inc(W[f"s{t}"], 1)
                for t in range(NT):
                    last = mm(ps[0:S, 4, 0:H * VW], mean_w[0:TP, :], v[0:TP, t, 0:H * VW], start=(t == 0), stop=(t == NT - 1))
                last.then_inc(W["vmean"], 1)
                filler()
                pe.wait_ge(W["e1"], i + 1)
                pe.wait_ge(W["e2"], i + 1)
                for h in range(H):
                    for t in range(NT):
                        last = mm(ps[0:S, 2 + h // 4, S * (h % 4):S * (h % 4) + S], ex[0:TP, t, S * h:S * h + S],
                                  v[0:TP, t, VW * h:VW * h + S], start=(t == 0), stop=(t == NT - 1))
                last.then_inc(W["av"], 1)
                filler()
                pe.wait_ge(W["on"], i + 1)
                pe.wait_ge(W["place"], i + 1)
                for h in range(H):
                    last = mm(ps[:, 0, 0:N], opad[:, C * h:C * h + C], place[:, h, :], start=(h == 0), stop=(h == H - 1))
                last.then_inc(W["scattered"], 1)
                pe.wait_ge(W["attnT"], i + 1)
                for t in range(NT):
                    last = mm(ps[0:TP, 4, 128 * t:128 * t + 128], attnT[:, TP * t:TP * t + TP], wo[:], start=True, stop=True)
                last.then_inc(W["oproj"], 1)
                filler()
                pe.wait_ge(W["xn1"], i + 1)
                for t in range(NT):
                    last = tr(ps[:, 2, TP * t:TP * t + TP], xn[0:TP, t, :], ident[0:TP, 0:TP])
                last.then_inc(W["x1_turned"], 1)
                pe.wait_ge(W["x1T"], i + 1)
                for f, bank in enumerate((0, 1, 2, 3)):
                    mm(ps[:, bank, 0:N], w1[:, 128 * f:128 * f + 128], x1T[:], start=True, stop=True).then_inc(W[f"f{f}"], 1)
                for f in range(NF):
                    pe.wait_ge(W[f"g{f}"], i + 1)
                    last = mm(ps[:, 4, 0:N], w2[:, f, :], hT[:, f, :], start=(f == 0), stop=(f == NF - 1))
                last.then_inc(W["ffn2"], 1)
                filler()
                pe.wait_ge(W["yT"], i + 1)
                for t in range(NT):
                    last = tr(ps[0:TP, 0, 128 * t:128 * t + 128], yT[:, TP * t:TP * t + TP], ident)
                last.then_inc(W["y_turned"], 1)
                filler()
                pe.wait_ge(W["xn2"], i + 1)
                for t in range(NT):
                    last = tr(ps[:, 1, TP * t:TP * t + TP], xn2[0:TP, t, :], ident[0:TP, 0:TP])
                last.then_inc(W["x2_turned"], 1)
                pe.wait_ge(W["x2T"], i + 1)
                for k in range(3):
                    last = mm(ps[:, 2, 0:N], cw[:, k, :], x2p[:, k:k + N], start=(k == 0), stop=(k == 2))
                last.then_inc(W["conv"], 1)
                filler()
                pe.wait_ge(W["el"], i + 1)
                for t in range(PT_):
                    last = tr(ps[0:PR, 4, 128 * t:128 * t + 128], el[:, PR * t:PR * t + PR], ident)
                last.then_inc(W["el_turned"], 1)
                pe.wait_ge(W["hn"], i + 1)
                for t in range(PT_):
                    last = tr(ps[:, 0, PR * t:PR * t + PR], hn[0:PR, t, :], ident[0:PR, 0:PR])
                last.then_inc(W["hn_turned"], 1)
                pe.wait_ge(W["hnT"], i + 1)
                mm(ps[:, 2, 0:NP], wqq[:], hnT[:], start=True, stop=True)
                mm(ps[:, 2, 256:256 + NP], wkk[:], hnT[:], start=True, stop=True).then_inc(W["qk_proj"], 1)
                for t in range(PT_):
                    last = mm(ps[0:PR, 3, 128 * t:128 * t + 128], hnT[:, PR * t:PR * t + PR], wv2[:], start=True, stop=True)
                last.then_inc(W["v2_proj"], 1)
                pe.wait_ge(W["qa"], i + 1)
                pe.wait_ge(W["ka"], i + 1)
                for t in range(PT_):
                    o = ps[0:PR, 4, NP * t:NP * t + NP]
                    mm(o, qa[:, PR * t:PR * t + PR], ka[:], start=True, stop=False)
                    last = mm(o, ones_f[D2:128, :], kk[D2:128, :], start=False, stop=True)
                last.then_inc(W["dist"], 1)
                pe.wait_ge(W["e2x"], i + 1)
                for m in range(PT_):
                    for t in range(PT_):
                        last = tr(ps[0:PR, 1, NP * m + PR * t:NP * m + PR * t + PR], e2[0:PR, t, PR * m:PR * m + PR],
                                  ident[0:PR, 0:PR])
                last.then_inc(W["e2_turned"], 1)
                pe.wait_ge(W["e2T"], i + 1)
                pe.wait_ge(W["v2"], i + 1)
                for t in range(PT_):
                    for m in range(PT_):
                        last = mm(ps[0:PR, 2, 128 * t:128 * t + 128], e2T[0:PR, m, PR * t:PR * t + PR], v2[0:PR, m, :],
                                  start=(m == 0), stop=(m == PT_ - 1))
                last.then_inc(W["av2"], 1)
                pe.wait_ge(W["xn4"], i + 1)
                for t in range(PT_):
                    last = tr(ps[:, 0, PR * t:PR * t + PR], xn4[0:PR, t, :], ident[0:PR, 0:PR])
                last.then_inc(W["h2n_turned"], 1)
                pe.wait_ge(W["h2nT"], i + 1)
                for t in range(PT_):
                    last = mm(ps[0:PR, 4, E * t:E * t + E], h2nT[:, PR * t:PR * t + PR], wr[:], start=True, stop=True)
                last.then_inc(W["router"], 1)
                pe.wait_ge(W["gate"], i + 1)
                for t in range(PT_):
                    last = tr(ps[0:E, 4, 64 + PR * t:64 + PR * t + PR], gate[0:PR, t, :], ident[0:PR, 0:PR])
                last.then_inc(W["gate_turned"], 1)
                pe.wait_ge(W["gateT"], i + 1)
                for t in range(PT_):
                    last = mm(ps[0:PR, 3, 128 * t:128 * t + 128], gateT[:, PR * t:PR * t + PR], mb2[:], start=True, stop=True)
                last.then_inc(W["bias2"], 1)

            batch(0, lambda: None)
            ex_steps = experts(0)
            batch(1, lambda: next(ex_steps))
            with pe.Fori(2, B) as i:
                ex_steps = experts(i - 1)
                batch(i, lambda: next(ex_steps))
            for _ in experts(B - 1):
                pass

        @block.scalar
        def _(act):
            fn = nc.scalar.activation
            act.wait_ge(s_w, 16 * len(loads))
            act.wait_ge(s_set, NSET)

            def a_evac(b, u):
                act.wait_ge(A["x_turned"], b + 1)
                if later(b):
                    act.wait_ge(A["k_proj"], b)
                fn(xTa[:], ps[:, 6, 0:N], ACT.Copy).then_inc(A["xT"], 1)
                act.wait_ge(A["q_proj"], b + 1)
                if u is not None:
                    act.wait_ge(A["scores"], 12 * (b - 1))
                fn(qTa[b % 2 if u is None else u][:], ps[:, 7, 0:N], ACT.Identity, bias=bqkT[:, 0:1]).then_inc(A["qT_ready"], 1)
                act.wait_ge(A["k_proj"], b + 1)
                if later(b):
                    act.wait_ge(A["kpad_ready"], b)
                fn(kTa[:], ps[:, 6, 0:N], ACT.Identity, bias=bqkT[:, 1:2], accum_out=ksum[:, 0:1]).then_inc(A["kT_ready"], 1)

            a_evac(0, None)
            a_evac(1, None)
            with act.Fori(1, B // 2) as j:
                a_evac(2 * j, 0)
                a_evac(2 * j + 1, 1)

            W = Bs

            def relus(b):
                for e in range(E):
                    act.wait_ge(m_h[0], E * b + e + 1)
                    if e >= 2:
                        act.wait_ge(m_y, E * b + e - 1)
                    for f in range(2):
                        fn(mh[e % 2][:, f, :], ps[:, 6, 256 * f:256 * f + NP], ACT.Relu,
                           bias=mb1[:, NF * e + f:NF * e + f + 1]).then_inc(m_ra, 1)
                    yield

            def batch(i, filler):
                act.wait_ge(W["x_turned"], i + 1)
                fn(xT[:], ps[:, 4, 0:N], ACT.Copy).then_inc(W["xT"], 1)
                act.wait_ge(W["k_proj"], i + 1)
                fn(kT[:], ps[:, 2, 0:N], ACT.Identity, bias=bqkT[:, 1:2], accum_out=ksum_b[:, 0:1]).then_inc(W["kT"], 1)
                filler()
                filler()
                for t in range(NT):
                    act.wait_ge(W[f"s{t}"], i + 1)
                    fn(ex[0:TP, t, :].rearrange("p (a s) -> p a s", a=2), ps[0:TP, 2 * (t % 2):2 * (t % 2) + 2, 0:384],
                       ACT.Exp, scale=1.0 / float(np.sqrt(DK))).then_inc(W[f"e{t}"], 1)
                filler()
                filler()
                act.wait_ge(W["scattered"], i + 1)
                fn(attnT[:], ps[:, 0, 0:N], ACT.Copy).then_inc(W["attnT"], 1)
                filler()
                act.wait_ge(W["x1_turned"], i + 1)
                fn(x1T[:], ps[:, 2, 0:N], ACT.Identity, bias=vecs[:, 2:3], scale=vecs[:, 1:2]).then_inc(W["x1T"], 1)
                for f in range(NF):
                    act.wait_ge(W[f"f{f}"], i + 1)
                    fn(hT[:, f, :], ps[:, f, 0:N], ACT.Gelu, bias=b1[:, f:f + 1]).then_inc(W[f"g{f}"], 1)
                filler()
                filler()
                act.wait_ge(W["x2_turned"], i + 1)
                fn(x2p[:, 1:N + 1], ps[:, 1, 0:N], ACT.Identity, bias=vecs[:, 4:5], scale=vecs[:, 3:4])
                fn(x2p[:, 0:1], ps[:, 1, N - 1:N], ACT.Identity, bias=vecs[:, 4:5], scale=vecs[:, 3:4])
                fn(x2p[:, N + 1:N + 2], ps[:, 1, 0:1], ACT.Identity, bias=vecs[:, 4:5], scale=vecs[:, 3:4]).then_inc(W["x2T"], 1)
                act.wait_ge(W["conv"], i + 1)
                fn(cp[:, 1:N + 1], ps[:, 2, 0:N], ACT.Identity, bias=vecs[:, 5:6]).then_inc(W["cp"], 1)
                filler()
                act.wait_ge(W["mx"], i + 1)
                fn(emn[:], el[:], ACT.Exp).then_inc(W["emn"], 1)
                act.wait_ge(W["hn_turned"], i + 1)
                fn(hnT[:], ps[:, 0, 0:NP], ACT.Copy).then_inc(W["hnT"], 1)
                act.wait_ge(W["qk_proj"], i + 1)
                fn(qa[0:D2, :], ps[0:D2, 2, 0:NP], ACT.Copy)
                fn(qa[D2:128, :], ps[D2:128, 2, 0:NP], ACT.Square).then_inc(W["qa"], 1)
                fn(ka[0:D2, :], ps[0:D2, 2, 256:256 + NP], ACT.Copy, scale=-2.0)
                fn(kk[D2:128, :], ps[D2:128, 2, 256:256 + NP], ACT.Square).then_inc(W["ka"], 1)
                act.wait_ge(W["v2_proj"], i + 1)
                fn(v2[0:PR], ps[0:PR, 3, 0:256].rearrange("p (t c) -> p t c", t=PT_), ACT.Copy).then_inc(W["v2"], 1)
                act.wait_ge(W["dclip"], i + 1)
                for t in range(PT_):
                    last = fn(e2[0:PR, t, :], d2[0:PR, t, :], ACT.Exp, scale=lam[0:PR, 3:4], bias=dbias[0:PR, t:t + 1],
                              accum_out=rs2[0:PR, t:t + 1])
                last.then_inc(W["e2x"], 1)
                act.wait_ge(W["e2_turned"], i + 1)
                fn(e2T[0:PR].rearrange("p m n -> p (m n)"), ps[0:PR, 1, 0:PT_ * NP], ACT.Copy).then_inc(W["e2T"], 1)
                act.wait_ge(W["h2n_turned"], i + 1)
                for half in range(2):
                    if later(i):
                        act.wait_ge(m_h[half], E * i)
                fn(h2nT[:], ps[:, 0, 0:NP], ACT.Copy).then_inc(W["h2nT"], 1)
                act.wait_ge(W["lg"], i + 1)
                for t in range(PT_):
                    last = fn(elg[0:PR, t, :], lg[0:PR, t, :], ACT.Exp, bias=nm1[0:PR, t:t + 1], accum_out=rse[0:PR, t:t + 1])
                    last = fn(e12[0:PR, t, :], m8[0:PR, t, 0:2], ACT.Exp, bias=nm1[0:PR, t:t + 1])
                last.then_inc(W["elg"], 1)
                act.wait_ge(W["gate_turned"], i + 1)
                fn(gateT[:], ps[0:E, 4, 64:64 + NP], ACT.Copy).then_inc(W["gateT"], 1)

            def store(i):
                act.wait_ge(W["out_ready"], i + 1)
                act.dma_start(od[bass.ds(i, 1)].rearrange("b p t c -> (b p) t c"), ostage[0:PR]).then_inc(W["out_stored"], 16)

            batch(0, lambda: None)
            steps = relus(0)
            batch(1, lambda: next(steps))
            store(0)
            with act.Fori(2, B) as i:
                steps = relus(i - 1)
                batch(i, lambda: next(steps))
                store(i - 1)
            for _ in relus(B - 1):
                pass
            store(B - 1)

        @block.gpsimd
        def _(pool):
            g = nc.gpsimd
            g.memset(mean_w[:], 1.0 / N).then_inc(s_set, 1)
            g.memset(ones_bf[:], 1.0).then_inc(s_set, 1)
            g.memset(ones_f[:], 1.0).then_inc(s_set, 1)
            g.memset(mhalf[:], -0.5).then_inc(s_set, 1)
            g.memset(opad[:], 0.0).then_inc(s_set, 1)
            g.memset(cp[:], -BIG).then_inc(s_set, 1)
            g.memset(ka[:], 1.0).then_inc(s_set, 1)
            g.memset(v[:], 0.0).then_inc(s_set, 1)
            pool.wait_ge(s_set, 8)
            for t in range(NT):
                last = g.memset(v[:, t, 0:H * VW].rearrange("p (h c) -> p h c", c=VW)[:, :, DK:VW], 1.0)
            last.then_inc(s_set, 1)
            g.memset(epsc[:], EPS).then_inc(s_e, 1)
            g.memset(euler[:], float(np.e)).then_inc(s_e, 1)
            pool.wait_ge(s_w, 16 * len(loads))
            pool.wait_ge(s_e, 2)
            g.tensor_tensor(lam[:, 1:2], euler[:], lam[:, 0:1], ALU.pow).then_inc(s_lam, 1)

            def spread(b, u, kp):
                pool.wait_ge(A["mean_ready"], b + 1)
                if u is not None:
                    pool.wait_ge(A["scores"], 12 * (b - 1))
                    pool.sem_inc(s_alone, 1)
                for h in range(H):
                    last = g.tensor_scalar(kp[:, h, :], kTa[:], ksum[:, 1:2], kc[:, K_HM + h:K_HM + h + 1], ALU.add, ALU.mult)
                last.then_inc(A["kpad_ready"], 1)

            spread(0, None, kpad[0])
            spread(1, None, kpad[1])
            with pool.Fori(1, B // 2) as j:
                spread(2 * j, 0, kpad[0])
                spread(2 * j + 1, 1, kpad[1])

            with pool.Fori(0, B) as i:
                for n, (k, rows) in enumerate(((1, TP), (2, TP), (3, PR), (4, PR), (5, PR))):
                    nt = NT if k < 3 else PT_
                    pool.wait_ge(Bs[f"aggr{k}"], i + 1)
                    g.tensor_tensor(veps[0:rows, 0:nt], mv[0:rows, 0:nt, 1], epsc[0:rows, 0:nt], ALU.add).then_inc(pch, 1)
                    pool.wait_ge(pch, 5 * i + n + 1)
                    g.tensor_tensor(rstd[0:rows, 0:nt], veps[0:rows, 0:nt], mhalf[0:rows, 0:nt], ALU.pow).then_inc(Bs[f"rstd{k}"], 1)

        @block.vector
        def _(dve):
            vv = nc.vector
            dve.wait_ge(s_w, 16 * len(loads))
            cnt = [0]

            def setup(ins):
                cnt[0] += 1
                ins.then_inc(T["chain"], 1)
                dve.wait_ge(T["chain"], cnt[0])

            dve.wait_ge(s_lam, 1)
            setup(vv.tensor_scalar(lam[:, 1:2], lam[:, 1:2], 0.001, None, ALU.max))
            setup(vv.tensor_tensor(lam[:, 2:3], lam[:, 1:2], lam[:, 1:2], ALU.mult))
            setup(vv.tensor_scalar(lam[:, 1:2], lam[:, 2:3], 2.0, None, ALU.mult))
            setup(vv.reciprocal(lam[:, 2:3], lam[:, 1:2]))
            vv.tensor_scalar(lam[:, 3:4], lam[:, 2:3], -1.0, None, ALU.mult).then_inc(s_set, 1)
            dve.wait_ge(s_set, NSET)

            def a_batch(b):
                dve.wait_ge(A["kT_ready"], b + 1)
                vv.tensor_scalar(ksum[:, 1:2], ksum[:, 0:1], -1.0 / N, None, ALU.mult).then_inc(A["mean_ready"], 1)

            def a_max(b, n, last_half=None):
                hp, t = n // 3, n % 3
                dve.wait_ge(A["scores"], 12 * b + n + 1)
                vv.tensor_reduce(maxes[0:TP, t, bass.ds(H * b + 2 * hp, 2)], ps[0:TP, 2 * (n % 3):2 * (n % 3) + 2, 0:N],
                                 AX.X, ALU.max).then_inc(A["maxed"], 1)

            a_batch(0)
            a_batch(1)
            for n in range(12):
                a_max(0, n)
            with dve.Fori(1, B // 2) as j:
                a_batch(2 * j)
                for n in range(12):
                    a_max(2 * j - 1, n)
                a_batch(2 * j + 1)
                for n in range(12):
                    a_max(2 * j, n)
            for n in range(12):
                a_max(B - 1, n)

            for gr in range(2):
                dve.wait_ge(T["turned"], gr + 1)
                if gr:
                    dve.wait_ge(T["stored"], 4 * 16)
                    dve.wait_ge(T["idx_turned"], 1)
                vv.tensor_copy(mrow[:], ps[:, 6, 0:N]).then_inc(T["rows"], 1)
                dve.wait_ge(T["rows"], gr + 1)
                src = mrow
                for r in range(S // 8):
                    t8 = top_v[:, 8 * r:8 * r + 8]
                    setup(vv.max(t8, src[:]))
                    setup(vv.max_index(top_i[:, 8 * r:8 * r + 8], t8, src[:]))
                    if r < S // 8 - 1:
                        dst = mwork if src is mrow else mrow
                        setup(vv.match_replace(dst[:], t8, src[:], -BIG))
                        src = dst
                setup(vv.tensor_copy(top_if[:], top_i[:]))
                setup(vv.memset(top_if[:, TOP:S], -1.0))
                setup(vv.memset(top_v[:, TOP:S], 0.0))
                setup(vv.tensor_scalar(top_r[:], top_v[:], -1.0, None, ALU.mult))
                setup(vv.tensor_copy(top_p[0][:], top_r[:]))
                setup(vv.tensor_tensor(top_v[:], top_r[:], top_p[0][:], ALU.subtract))
                setup(vv.tensor_copy(top_p[1][:], top_v[:]))
                setup(vv.tensor_tensor(top_r[:], top_v[:], top_p[1][:], ALU.subtract))
                vv.tensor_copy(top_p[2][:], top_r[:]).then_inc(T["idx_ready"], 1)
                if gr == 0:
                    dve.wait_ge(T["idx_turned"], 1)
                    vv.tensor_copy(idx_col[:, 0:128], ps[0:S, 7, 0:128]).then_inc(T["idx_col"], 1)
            dve.wait_ge(T["idx_turned"], 2)
            vv.tensor_copy(idx_col[:, 128:256], ps[0:S, 7, 0:128]).then_inc(T["idx_col"], 1)
            dve.wait_ge(T["idx_col"], 2)

            W = Bs

            def relus_and_sums(b):
                def relu(e):
                    dve.wait_ge(m_h[1], E * b + e + 1)
                    if e >= 2:
                        dve.wait_ge(m_y, E * b + e - 1)
                    for f in range(2):
                        vv.tensor_scalar(mh[e % 2][:, 2 + f, :], ps[:, 7, 256 * f:256 * f + NP],
                                         mb1[:, NF * e + 2 + f:NF * e + 3 + f], 0.0, ALU.add, ALU.max).then_inc(m_rd, 1)

                def add(e):
                    dve.wait_ge(m_y, E * b + e + 1)
                    if e == 0:
                        dve.wait_ge(W["acc_start"], b + 1)
                    else:
                        dve.wait_ge(m_acc, E * b + e)
                    for t in range(PT_):
                        last = vv.scalar_tensor_tensor(
                            acc[0:PR, t, :], ps[0:PR, 5, C * t:C * t + C],
                            gate_m[0:PR, t, e:e + 1], acc[0:PR, t, :], ALU.mult, ALU.add)
                    last.then_inc(m_acc, 1)

                relu(0)
                for e in range(E):
                    if e + 1 < E:
                        relu(e + 1)
                    add(e)
                    yield
                dve.wait_ge(m_acc, E * (b + 1))
                if later(b):
                    dve.wait_ge(W["out_stored"], 16 * b)
                vv.tensor_copy(ostage[0:PR], acc[0:PR]).then_inc(W["out_ready"], 1)
                yield

            def batch(i, filler):
                k = [0]

                def link(ins, alone=False):
                    k[0] += 1
                    ins.then_inc(dch, 1)
                    dve.wait_ge(dch, i * CH + k[0])
                    if alone:
                        dve.sem_inc(s_alone, 1)

                def norm(src, dst, rows, nt, n, stats_ready=None):
                    for t in range(nt):
                        last = vv.bn_stats(st[0:rows, t, :], src(t))
                    link(last, alone=True)
                    for t in range(nt):
                        last = vv.bn_aggr(mv[0:rows, t, :], st[0:rows, t, :])
                    last.then_inc(W[f"aggr{n}"], 1)
                    dve.wait_ge(W[f"aggr{n}"], i + 1)
                    dve.wait_ge(W[f"rstd{n}"], i + 1)
                    for t in range(nt):
                        last = vv.tensor_scalar(dst(t), src(t), mv[0:rows, t, 0:1], rstd[0:rows, t:t + 1],
                                                ALU.subtract, ALU.mult)
                    return last

                dve.wait_ge(W["idx_loaded"], 16 * (i + 1))
                if later(i):
                    dve.wait_ge(W["gathered"], i)
                for t in range(NT):
                    last = vv.tensor_scalar(pick[0:TP, t, :], idx_bc[0:TP, :], kc[0:TP, K_TOK + t:K_TOK + t + 1], None, ALU.is_equal)
                last.then_inc(W["pick"], 1)
                if later(i):
                    dve.wait_ge(W["scattered"], i)
                vv.tensor_scalar(place[:, 0, :], kc[0:S, K_ROW:K_ROW + N], idx_col[:, bass.ds(H * i, 1)],
                                 kc[0:S, K_M:K_M + 1], ALU.is_equal, ALU.max)
                for h in range(1, H):
                    last = vv.tensor_scalar(place[:, h, :], kc[0:S, K_ROW:K_ROW + N], idx_col[:, bass.ds(H * i + h, 1)],
                                            None, ALU.is_equal)
                last.then_inc(W["place"], 1)
                dve.wait_ge(W["kT"], i + 1)
                link(vv.tensor_scalar(ksum_b[:, 1:2], ksum_b[:, 0:1], -1.0 / N, None, ALU.mult))
                vv.tensor_scalar(kTc[:], kT[:], ksum_b[:, 1:2], None, ALU.add).then_inc(W["kTc"], 1)
                dve.wait_ge(W["qv_proj"], i + 1)
                qv = ps[0:TP, 0:2, :].rearrange("p a c -> p (a c)")[:, 0:256 * NT].rearrange("p (t c) -> p t c", t=NT)
                vv.tensor_tensor(qrow[0:TP], qv[:, :, 0:C], bqv_bc[0:TP, None, 0:C].to_broadcast([TP, NT, C]), ALU.add).then_inc(W["q_rows"], 1)
                for t in range(NT):
                    last = vv.tensor_tensor(v[0:TP, t, 0:H * VW].rearrange("p (h c) -> p h c", c=VW)[:, :, 0:DK],
                                            qv[:, t, C:2 * C].rearrange("p (h c) -> p h c", c=DK),
                                            bqv_bc[0:TP, C:2 * C].rearrange("p (h c) -> p h c", c=DK), ALU.add)
                last.then_inc(W["v_rows"], 1)
                dve.wait_ge(W["x_loaded"], 16 * (i + 1))
                vv.tensor_tensor(xb[0:TP], x[0:TP], bo_bc[0:TP, None, :].to_broadcast([TP, NT, C]), ALU.add).then_inc(W["xb"], 1)
                filler()
                dve.wait_ge(W["gathered"], i + 1)
                vv.tensor_tensor(qsel[:].rearrange("p (a s) -> p a s", a=2), ps[:, 2:4, 0:384],
                                 kc[:, K_BM:K_BM + 768].rearrange("p (a s) -> p a s", a=2), ALU.mult).then_inc(W["qsel"], 1)
                filler()
                dve.wait_ge(W["vmean"], i + 1)
                vm = ps[0:S, 4, 0:H * VW].rearrange("p (h c) -> p h c", c=VW)[:, :, 0:DK]
                vv.tensor_scalar(vmw[:], vm, kc[0:S, K_M + 1:K_M + 2], None, ALU.mult)
                link(vv.tensor_scalar(opad[:, 0:C].rearrange("p (h c) -> p h c", c=DK), vm, kc[0:S, K_M:K_M + 1], None, ALU.mult))
                filler()
                dve.wait_ge(W["av"], i + 1)
                av = ps[0:S, 2:4, 0:384].rearrange("p a (h c) -> p a h c", c=S)
                link(vv.reciprocal(rden[:].rearrange("p (a h) -> p a h", a=2)[:, :, :, None], av[:, :, :, DK:VW]))
                for half in range(2):
                    last = vv.tensor_tensor(onorm[:, 4 * half:4 * half + 4, :], av[:, half, :, 0:DK],
                                            rden[:, 4 * half:4 * half + 4, None].to_broadcast([S, 4, DK]), ALU.mult)
                link(last)
                vv.tensor_tensor(opad[:].rearrange("p (h c) -> p h c", c=C + DK)[:, :, 0:DK], onorm[:], vmw[:],
                                 ALU.subtract).then_inc(W["on"], 1)
                filler()
                dve.wait_ge(W["oproj"], i + 1)
                dve.wait_ge(W["xb"], i + 1)
                link(vv.tensor_tensor(r1[0:TP].rearrange("p t c -> p (t c)"), ps[0:TP, 4, 0:NT * C],
                                      xb[0:TP].rearrange("p t c -> p (t c)"), ALU.add))
                norm(lambda t: r1[0:TP, t, :], lambda t: xn[0:TP, t, :], TP, NT, 1).then_inc(W["xn1"], 1)
                filler()
                dve.wait_ge(W["ffn2"], i + 1)
                vv.scalar_tensor_tensor(yT[:], ps[:, 4, 0:N], vecs[:, 0:1], x1T[:], ALU.add, ALU.add).then_inc(W["yT"], 1)
                filler()
                dve.wait_ge(W["y_turned"], i + 1)
                norm(lambda t: ps[0:TP, 0, C * t:C * t + C], lambda t: xn2[0:TP, t, :], TP, NT, 2).then_inc(W["xn2"], 1)
                filler()
                dve.wait_ge(W["cp"], i + 1)
                link(vv.tensor_tensor(mx[:], cp[:, 0:2 * NP:2], cp[:, 1:2 * NP:2], ALU.max))
                link(vv.tensor_tensor(mx[:], mx[:], cp[:, 2:2 * NP + 1:2], ALU.max))
                vv.tensor_scalar(el[:], mx[:], 0.0, None, ALU.min).then_inc(W["mx"], 1)
                filler()
                filler()
                dve.wait_ge(W["emn"], i + 1)
                link(vv.tensor_scalar(emn[:], emn[:], -1.0, None, ALU.add))
                vv.scalar_tensor_tensor(el[:], mx[:], 0.0, emn[:], ALU.max, ALU.add).then_inc(W["el"], 1)
                dve.wait_ge(W["el_turned"], i + 1)
                link(norm(lambda t: ps[0:PR, 4, C * t:C * t + C], lambda t: xn3[0:PR, t, :], PR, PT_, 3))
                link(vv.tensor_tensor(xn3[0:PR], xn3[0:PR], cng_bc[0:PR, None, :].to_broadcast([PR, PT_, C]), ALU.mult))
                link(vv.tensor_tensor(hrow[0:PR], xn3[0:PR], cnb_bc[0:PR, None, :].to_broadcast([PR, PT_, C]), ALU.add))
                norm(lambda t: hrow[0:PR, t, :], lambda t: hn[0:PR, t, :], PR, PT_, 4).then_inc(W["hn"], 1)
                dve.wait_ge(W["dist"], i + 1)
                link(vv.tensor_scalar(d2[0:PR].rearrange("p t m -> p (t m)"), ps[0:PR, 4, 0:PT_ * NP], 0.0, None, ALU.max))
                link(vv.tensor_reduce(dmin[0:PR], d2[0:PR], AX.X, ALU.min))
                vv.tensor_scalar(dbias[0:PR], dmin[0:PR], lam[0:PR, 2:3], None, ALU.mult).then_inc(W["dclip"], 1)
                dve.wait_ge(W["e2x"], i + 1)
                link(vv.reciprocal(rr2[0:PR], rs2[0:PR]))
                dve.wait_ge(W["av2"], i + 1)
                for t in range(PT_):
                    last = vv.scalar_tensor_tensor(h2[0:PR, t, :], ps[0:PR, 2, C * t:C * t + C], rr2[0:PR, t:t + 1],
                                                   hrow[0:PR, t, :], ALU.mult, ALU.add)
                link(last)
                norm(lambda t: h2[0:PR, t, :], lambda t: xn4[0:PR, t, :], PR, PT_, 5).then_inc(W["xn4"], 1)
                dve.wait_ge(W["router"], i + 1)
                logits = vv.tensor_tensor(lg[0:PR], ps[0:PR, 4, 0:PT_ * E].rearrange("p (t e) -> p t e", t=PT_),
                                           br_bc[0:PR, None, :].to_broadcast([PR, PT_, E]), ALU.add)
                link(logits, alone=True)
                for t in range(PT_):
                    last = vv.max(m8[0:PR, t, :], lg[0:PR, t, :])
                link(last)
                vv.tensor_scalar(nm1[0:PR], m8[0:PR, :, 0], -1.0, None, ALU.mult).then_inc(W["lg"], 1)
                for t in range(PT_):
                    last = vv.max_index(i8[0:PR, t, :], m8[0:PR, t, :], lg[0:PR, t, :])
                link(last)
                link(vv.tensor_copy(i8f[0:PR], i8[0:PR]))
                dve.wait_ge(W["elg"], i + 1)
                link(vv.reciprocal(rre[0:PR], rse[0:PR]))
                link(vv.tensor_tensor(p12[0:PR], e12[0:PR], rre[0:PR, :, None].to_broadcast([PR, PT_, 2]), ALU.mult))
                for t in range(PT_):
                    vv.tensor_scalar(gateA[0:PR, t, :], kc[0:PR, K_E8:K_E8 + E], i8f[0:PR, t, 0:1], p12[0:PR, t, 0:1],
                                     ALU.is_equal, ALU.mult)
                    last = vv.tensor_scalar(gate[0:PR, t, :], kc[0:PR, K_E8:K_E8 + E], i8f[0:PR, t, 1:2], p12[0:PR, t, 1:2],
                                            ALU.is_equal, ALU.mult)
                link(last)
                vv.tensor_tensor(gate[0:PR], gate[0:PR], gateA[0:PR], ALU.add).then_inc(W["gate"], 1)
                dve.wait_ge(W["gate"], i + 1)
                vv.tensor_copy(gate_m[0:PR], gate[0:PR])
                dve.wait_ge(W["bias2"], i + 1)
                vv.tensor_tensor(acc[0:PR].rearrange("p t c -> p (t c)"), ps[0:PR, 3, 0:PT_ * C],
                                 h2[0:PR].rearrange("p t c -> p (t c)"), ALU.add).then_inc(W["acc_start"], 1)
                assert k[0] == CH, k[0]

            batch(0, lambda: None)
            steps = relus_and_sums(0)
            batch(1, lambda: next(steps))
            with dve.Fori(2, B) as i:
                steps = relus_and_sums(i - 1)
                batch(i, lambda: next(steps))
            for _ in relus_and_sums(B - 1):
                pass


def kernel(**inputs):
    import numpy as _np
    import concourse.bacc as _bacc
    from concourse import mybir as _mybir
    from concourse.bass_utils import run_bass_kernel_spmd as _run

    w = {k.split("_", 1)[1]: _np.asarray(v) for k, v in inputs.items() if k != "x"}
    tok = {k[4:]: v for k, v in w.items() if k.startswith("tok_")}
    att = {k[5:]: v for k, v in w.items() if k.startswith("attn_")}
    moe = {k[4:]: v for k, v in w.items() if k.startswith("ffn_")}
    laid = {
        "x": _np.asarray(inputs["x"]),
        "consts": shape_constants(),
        "qkv_w": tok["qkv_w"],
        "qkv_b": tok["qkv_b"].reshape(1, -1),
        "qk_bT": tok["qkv_b"][:2 * C].reshape(2, C).T,
        "out_w": tok["out_w"],
        "out_b": tok["out_b"].reshape(1, -1),
        "ffn_w1": tok["ffn_w1"],
        "ffn_b1": tok["ffn_b1"].reshape(NF, 128).T,
        "ffn_w2": tok["ffn_w2"],
        "vecs": _np.stack([tok[n] for n in ("ffn_b2", "n1_g", "n1_b", "n2_g", "n2_b", "conv_b")], axis=1),
        "conv_w": tok["conv_w"].transpose(1, 2, 0),
        "cn_g": tok["cn_g"].reshape(1, -1),
        "cn_b": tok["cn_b"].reshape(1, -1),
        "WqT": att["Wq"].T,
        "WkT": att["Wk"].T,
        "WvT": att["Wv"].T,
        "log_lambda": att["log_lambda"].reshape(1, 1),
        "Wr": moe["Wr"],
        "br": moe["br"].reshape(1, -1),
        "W1": moe["W1"],
        "mb1": moe["b1"].reshape(E * NF, 128).T,
        "W2": moe["W2"],
        "b2": moe["b2"],
    }
    nc = _bacc.Bacc("TRN2", target_bir_lowering=False, num_devices=1)
    arrays, aps = {}, {}
    for name, value in laid.items():
        value = _np.ascontiguousarray(value)
        arrays[f"in_{name}"] = value
        aps[name] = nc.dram_tensor(f"in_{name}", value.shape, _mybir.dt.from_np(value.dtype), kind="ExternalInput").ap()
    out = nc.dram_tensor("out_0", (B, NP, C), _mybir.dt.float32, kind="ExternalOutput").ap()
    audio_tower(nc, aps, out)
    r = _run(nc, [arrays], core_ids=[0])
    return r.results[0]["out_0"]
```

```python
from contextlib import ExitStack

import concourse.bass as bass
import numpy as np
from concourse import mybir

ALU = mybir.AluOpType
ACT = mybir.ActivationFunctionType
AX = mybir.AxisListType
F32 = mybir.dt.float32
BF16 = mybir.dt.bfloat16
F32R = mybir.dt.float32r
U32 = mybir.dt.uint32

B, N, C = 32, 375, 128
CF, CK = 9, 21
ATTEND_SLOTS = (0, 2, 3, 4, 5, 6, 7, 12, 14)
SLOTS = 18
H, DK = 8, 16
TOP = max(1, min(int(N * 0.25), N - 1))
S = 96
NE = N + 1
Q_PART = (0, 0, 0, 1, 1, 2)
K_PART = (0, 1, 2, 0, 1, 0)
NC6 = len(Q_PART)
NT, TP = 3, 125
FF = 512
NF = FF // 128
NP = (N + 1) // 2
PT_, PR = 2, 94
D2 = 64
E = 8
VW = DK + 1
VPAD = 7 * VW + S
OW = 8 * (C + DK)
EPS = 1e-5
BIG = 3.0e38
SELF_SLOT = S - 1

K_ID, K_BM, K_TOK, K_ROW, K_M, K_E8, K_END = 0, 128, 896, 900, 1276, 1278, 1286


def later(b):
    return not (isinstance(b, int) and b == 0)


def pipeline(attend=None, rest=None, experts=None):
    for slot in range(SLOTS):
        if rest:
            next(rest, None)
        if experts:
            next(experts, None)
        if attend and slot in ATTEND_SLOTS:
            next(attend, None)


def all_batches(eng, attend, rest, experts):
    pipeline(attend(0))
    pipeline(attend(1), rest(0))
    pipeline(attend(2), rest(1), experts(0))
    with eng.Fori(2, B - 1) as i:
        pipeline(attend(i + 1), rest(i), experts(i - 1))
    pipeline(None, rest(B - 1), experts(B - 2))
    pipeline(None, None, experts(B - 1))


def shape_constants():
    k = np.zeros((128, K_END), np.float32)
    p = np.arange(128)
    k[:, K_ID:K_ID + 128] = np.eye(128)
    k[:, K_BM:K_BM + 768] = (p[:, None] // DK == np.arange(768)[None] // S)
    k[:, K_TOK:K_TOK + 3] = p[:, None] + TP * np.arange(3)[None]
    k[:, K_ROW:K_ROW + NE] = np.arange(NE)[None]
    k[:, K_M] = p == SELF_SLOT
    k[:, K_M + 1] = p != SELF_SLOT
    k[:, K_E8:K_E8 + 8] = np.arange(8)[None]
    return k


def audio_tower(nc, a, out):
    with ExitStack() as ctx:
        def sb(name, shape, dt=F32):
            return ctx.enter_context(nc.sbuf_tensor(name, shape, dt))

        def sem(name):
            return ctx.enter_context(nc.semaphore(name))

        idx_dram = nc.dram_tensor("top_idx_scratch", [2 * 128, S], F32, kind="Internal").ap()
        part_dram = nc.dram_tensor("qk_parts_scratch", [B, 6, C, NE], BF16, kind="Internal").ap()
        gate_dram = nc.dram_tensor("gate_scratch", [B, E * NP], F32, kind="Internal").ap()
        max_dram = nc.dram_tensor("top_max_scratch", [3, 2 * 128, S], BF16, kind="Internal").ap()

        kc = sb("shape_consts", [128, K_END])
        ident = kc[:, K_ID:K_ID + 128]
        wqkv = sb("wqkv", [128, 3 * C])
        bqkT = sb("bqkT", [128, 2])
        bqv_bc = sb("bqv_bc", [128, 2 * C])
        wo = sb("wo", [128, C])
        bo_bc = sb("bo_bc", [128, C])
        w1 = sb("w1", [128, FF])
        b1 = sb("b1", [128, NF])
        w2 = sb("w2", [128, NF, C])
        vecs = sb("vecs", [128, 6])
        cw = sb("conv_w", [128, 3, C])
        cng_bc = sb("cng_bc", [128, C])
        cnb_bc = sb("cnb_bc", [128, C])
        wqq = sb("wqq", [128, 2 * D2])
        wkk = sb("wkk", [128, 2 * D2])
        wv2 = sb("wv2", [128, C])
        lam = sb("lam", [128, 4])
        euler = sb("euler", [128, 1])
        wr = sb("wr", [128, E])
        br_bc = sb("br_bc", [128, E])
        mw1 = sb("mw1", [128, E, FF])
        mb1 = sb("mb1", [128, E * NF])
        mw2 = sb("mw2", [128, E, NF, C])
        mb2 = sb("mb2", [E, C])
        mean_w = sb("mean_w", [128, S])
        ones_bf = sb("ones_bf", [128, 128], BF16)
        ones_f = sb("ones_f", [128, PR])
        mhalf = sb("mhalf", [128, NT])

        maxes = sb("maxes", [128, NT, B * H])
        xa = sb("xa", [128, NT, C])
        xTa = sb("xTa", [128, N])
        qTa = sb("qTa", [128, N])
        kTa = sb("kTa", [128, N])
        kca = sb("kca", [128, N])
        ksum = sb("ksum", [128, 2])
        rem = [sb(f"rem{u}", [128, N]) for u in range(2)]
        parts = [sb(f"parts{u}", [128, 3, NE], BF16) for u in range(2)]
        gate_bc = sb("gate_bc", [128, E, NP])
        qstack = [gate_bc[0:NC6 * DK].bitcast(BF16), sb("qstack1", [NC6 * DK, H, NE], BF16)]
        kstack = [sb(f"kstack{u}", [NC6 * DK, H, NE], BF16) for u in range(2)]
        mrow = sb("mrow", [128, N])
        mwork = sb("mwork", [128, N])
        top_v = sb("top_v", [128, S])
        top_i = sb("top_i", [128, S], U32)
        top_if = sb("top_if", [128, S])
        top_p = [sb(f"top_p{k}", [128, S], BF16) for k in range(3)]
        top_r = sb("top_r", [128, S])
        idx_col = sb("idx_col", [S, B * H])

        x = sb("x", [128, NT, C])
        xb = sb("xb", [128, NT, C])
        idx_bc = sb("idx_bc", [128, H * S])
        negmax = sb("negmax", [128, H * S], BF16)
        xT = sb("xT", [128, N])
        kT = sb("kT", [128, N])
        kTc = sb("kTc", [128, N])
        ksum_b = sb("ksum_b", [128, 2])
        qrow = sb("qrow", [128, NT, C])
        q_hi = sb("q_hi", [128, NT, C], F32R)
        q_lo = sb("q_lo", [128, NT, C], F32R)
        v = sb("v", [128, NT, VPAD + 1])
        pick = sb("pick", [128, NT, H * S], F32R)
        place = sb("place", [S, H, NE], F32R)
        qsel = sb("qsel", [128, H * S])
        ex = sb("ex", [128, NT, H * S])
        rden = sb("rden", [S, H])
        onorm = sb("onorm", [S, H, DK])
        vmw = sb("vmw", [S, H, DK])
        on_all = sb("on_all", [S, H, DK])
        self_row = sb("self_row", [S, C])
        opad = [sb(f"opad{u}", [S, OW], F32R) for u in range(2)]
        attnT = sb("attnT", [128, N])
        r1 = sb("r1", [128, NT, C])
        st = [sb(f"st{u}", [128, NT, 6]) for u in range(2)]
        mv = [sb(f"mv{u}", [128, NT, 2]) for u in range(2)]
        veps = [sb(f"veps{u}", [128, NT]) for u in range(2)]
        rstd = [sb(f"rstd{u}", [128, NT]) for u in range(2)]
        xn = sb("xn", [128, NT, C])
        x1T = sb("x1T", [128, N])
        hT = sb("hT", [128, NF, N])
        yT = sb("yT", [128, N])
        xn2 = sb("xn2", [128, NT, C])
        x2p = sb("x2p", [128, N + 2])
        cp = sb("cp", [128, N + 2])
        mx = sb("mx", [128, NP])
        emn = sb("emn", [128, NP])
        el = sb("el", [128, NP])
        xn3 = sb("xn3", [128, PT_, C])
        hrow = sb("hrow", [128, PT_, C])
        hn = sb("hn", [128, PT_, C])
        hnT = sb("hnT", [128, NP])
        qa = sb("qa", [128, NP])
        ka = sb("ka", [128, NP])
        kk = sb("kk", [128, NP])
        v2 = sb("v2", [128, PT_, C])
        d2 = sb("d2", [128, PT_, NP])
        dmin = sb("dmin", [128, PT_])
        dbias = sb("dbias", [128, PT_])
        e2 = sb("e2", [128, PT_, NP])
        rs2 = sb("rs2", [128, PT_])
        rr2 = sb("rr2", [128, PT_])
        e2T = sb("e2T", [128, PT_, NP])
        h2 = sb("h2", [128, PT_, C])
        xn4 = sb("xn4", [128, PT_, C])
        lg = sb("lg", [128, PT_, E])
        m8 = sb("m8", [128, PT_, 8])
        i8 = sb("i8", [128, PT_, 8], U32)
        i8f = sb("i8f", [128, PT_, 8])
        nm1 = sb("nm1", [128, PT_])
        elg = sb("elg", [128, PT_, E])
        e12 = sb("e12", [128, PT_, 2])
        rse = sb("rse", [128, PT_])
        rre = sb("rre", [128, PT_])
        p12 = sb("p12", [128, PT_, 2])
        h2nT = sb("h2nT", [128, NP])
        gate = sb("gate", [128, PT_, E])
        gateB = sb("gateB", [128, PT_, E])
        gateA = sb("gateA", [128, PT_, E])
        gateT = sb("gateT", [E, NP])
        h2nT_m = sb("h2nT_m", [128, NP])
        h2_m = sb("h2_m", [128, PT_, C])
        moeT = sb("moeT", [128, NP])
        mh = [sb(f"mh{u}", [128, NF, NP]) for u in range(2)]
        ostage = sb("ostage", [128, PT_, C])

        ps = ctx.enter_context(nc.psum_tensor("ps", [128, 8, 512], F32))

        s_w0 = sem("s_weights_of_phase_A_loaded")
        s_w = sem("s_weights_loaded")
        s_set = sem("s_constants_set")
        s_lam = sem("s_lambda")
        s_alone = sem("s_carries_a_wait")
        s_e = sem("s_euler")
        A = {n: sem("A_" + n) for n in (
            "x_loaded x_turned xT k_proj kT_ready q_proj qT_ready mean_ready kc_ready q1 q2 k1 k2 qrem krem q3 k3 "
            "q_out k_out stacked0 stacked1 scores maxed".split())}
        T = {n: sem("T_" + n) for n in "turned rows idx_ready idx_turned idx_col stored chain".split()}
        names = ("x_loaded idx_loaded nm_loaded x_turned xT k_proj kT kTc qv_proj q_rows q_hi q_lo v_rows pick place gathered qsel "
                 "s0 s1 s2 e0 e1 e2 av vmean on scattered attnT oproj xb aggr1 rstd1 xn1 x1_turned x1T "
                 "f0 f1 f2 f3 g0 g1 g2 g3 ffn2 yT y_turned aggr2 rstd2 xn2 x2_turned x2T conv cp mx emn el "
                 "el_turned aggr3 rstd3 hrow aggr4 rstd4 hn hn_turned hnT qk_proj v2_proj qa ka v2 dist dclip e2x e2_turned e2T "
                 "av2 h2 aggr5 rstd5 xn4 h2n_turned h2nT router lg elg gate gate_turned gateT bias2 gate_out gates0 gates1 h2_kept h2_held moeT out_turned "
                 "veps1 veps2 veps3 veps4 veps5 h2nT_m out_ready out_stored").split()
        Bs = {n: sem("B_" + n) for n in names}
        m_h = [sem("M_hidden01"), sem("M_hidden23")]
        m_relu = sem("M_relu")
        m_y = sem("M_y")
        m_gated = sem("M_gated")
        chain_f = sem("dve_chain_attention")
        chain_k = sem("dve_chain_rest")

        loads = [
            (kc[:], a["consts"]), (wqkv[:], a["qkv_w"]), (bqkT[:], a["qk_bT"]),
            (lam[:, 0:1], a["log_lambda"].to_broadcast([128, 1])),
            (bqv_bc[:, 0:C], a["qkv_b"][:, 0:C].to_broadcast([128, C])),
            (bqv_bc[:, C:2 * C], a["qkv_b"][:, 2 * C:3 * C].to_broadcast([128, C])),
            (wo[:], a["out_w"]), (bo_bc[:], a["out_b"].to_broadcast([128, C])),
            (w1[:], a["ffn_w1"]), (b1[:], a["ffn_b1"]),
            (w2[:], a["ffn_w2"].rearrange("(f p) c -> p f c", p=128)), (vecs[:], a["vecs"]),
            (cw[:], a["conv_w"]),
            (cng_bc[:], a["cn_g"].to_broadcast([128, C])), (cnb_bc[:], a["cn_b"].to_broadcast([128, C])),
            (wqq[:, 0:D2], a["WqT"]), (wqq[:, D2:], a["WqT"]), (wkk[:, 0:D2], a["WkT"]), (wkk[:, D2:], a["WkT"]),
            (wv2[:], a["WvT"]),
            (wr[:], a["Wr"]), (br_bc[:], a["br"].to_broadcast([128, E])),
            (mw1[:], a["W1"].rearrange("e p f -> p e f")), (mb1[:], a["mb1"]),
            (mw2[:], a["W2"].rearrange("e (f p) c -> p e f c", p=128)), (mb2[:], a["b2"]),
        ]
        EARLY = 4
        NSET = 14
        xd = a["x"].rearrange("b (t p) c -> b p t c", p=TP)
        od = out.rearrange("b (t p) c -> b p t c", p=PR)

        block = ctx.enter_context(nc.Block())

        @block.sync
        def _(sp):
            for dst, src in loads[:EARLY]:
                sp.dma_start(dst, src).then_inc(s_w0, 16)

            def x_load(b):
                if later(b):
                    sp.wait_ge(A["x_turned"], b)
                    sp.sem_inc(s_alone, 1)
                sp.dma_start(xa[0:TP], xd[bass.ds(b, 1)].rearrange("b p t c -> (b p) t c")).then_inc(A["x_loaded"], 16)

            def parts_out(b):
                for u, n in ((0, "q"), (1, "k")):
                    sp.wait_ge(A[n + "3"], b + 1)
                    sp.sem_inc(s_alone, 1)
                    sp.dma_start(part_dram[bass.ds(b, 1), 3 * u:3 * u + 3].rearrange("b k p n -> p (b k) n"),
                                 parts[u][:]).then_inc(A[n + "_out"], 16)

            def stack_in(b, u):
                if not isinstance(b, int) or b >= 2:
                    sp.wait_ge(A["scores"], 8 * (b - 1))
                    sp.sem_inc(s_alone, 1)
                sp.wait_ge(A["q_out"], 16 * (b + 1))
                sp.wait_ge(A["k_out"], 16 * (b + 1))
                sp.sem_inc(s_alone, 1)
                for stack, which, base in ((qstack, Q_PART, 0), (kstack, K_PART, 3)):
                    for c in range(NC6):
                        sp.dma_start(stack[u][DK * c:DK * c + DK],
                                     part_dram[bass.ds(b, 1), base + which[c]].rearrange("b (h d) n -> (b d) h n", d=DK)
                                     ).then_inc(A[f"stacked{u}"], 16)

            x_load(0)
            x_load(1)
            for dst, src in loads[EARLY:]:
                sp.dma_start(dst, src).then_inc(s_w, 16)
            parts_out(0)
            x_load(2)
            parts_out(1)
            stack_in(0, 0)
            for b in range(2):
                stack_in(b + 1, (b + 1) % 2)
                x_load(b + 3)
                parts_out(b + 2)
            with sp.Fori(1, B // 2 - 2) as j:
                for u in range(2):
                    stack_in(2 * j + 1 + u, 1 - u)
                    x_load(2 * j + 3 + u)
                    parts_out(2 * j + 2 + u)
            for b in range(B - 4, B - 1):
                stack_in(b + 1, (b + 1) % 2)
                if b + 3 < B:
                    x_load(b + 3)
                if b + 2 < B:
                    parts_out(b + 2)
            for g in range(2):
                sp.wait_ge(T["idx_ready"], g + 1)
                sp.dma_start(idx_dram[128 * g:128 * g + 128], top_if[:]).then_inc(T["stored"], 16)
                for k in range(3):
                    sp.dma_start(max_dram[k, 128 * g:128 * g + 128], top_p[k][:]).then_inc(T["stored"], 16)
            sp.wait_ge(T["stored"], 2 * 4 * 16)
            idx_flat = idx_dram.rearrange("(b h) s -> b (h s)", h=H)
            max_flat = max_dram.rearrange("k (b h) s -> k b (h s)", h=H)

            def batch_loads(i):
                if later(i):
                    sp.wait_ge(s_set, NSET)
                    sp.wait_ge(Bs["pick"], i)
                sp.dma_start(idx_bc[0:TP], idx_flat[bass.ds(i, 1)].to_broadcast([TP, H * S])).then_inc(Bs["idx_loaded"], 16)
                if later(i):
                    sp.wait_ge(s_set, NSET)
                    sp.wait_ge(Bs["s2"], i)
                sp.dma_start(negmax[0:3], max_flat[:, bass.ds(i, 1)].rearrange("k b s -> k (b s)")).then_inc(Bs["nm_loaded"], 16)
                if later(i):
                    sp.wait_ge(s_set, NSET)
                    sp.wait_ge(Bs["xb"], i)
                    sp.wait_ge(Bs["x_turned"], i)
                sp.dma_start(x[0:TP], xd[bass.ds(i, 1)].rearrange("b p t c -> (b p) t c")).then_inc(Bs["x_loaded"], 16)

            def gates_move(i):
                sp.wait_ge(Bs["gateT"], i + 1)
                sp.sem_inc(s_alone, 1)
                sp.dma_start(gate_dram[bass.ds(i, 1)].rearrange("b (e n) -> (b e) n", e=E), gateT[:]).then_inc(Bs["gate_out"], 16)
                sp.wait_ge(Bs["gate_out"], 16 * (i + 1))
                sp.sem_inc(s_alone, 1)
                for half in range(2):
                    if later(i):
                        sp.wait_ge(m_gated, E * i - 4 * (1 - half))
                        sp.sem_inc(s_alone, 1)
                    sp.dma_start(gate_bc[:, 4 * half:4 * half + 4].rearrange("p e n -> p (e n)"),
                                 gate_dram[bass.ds(i, 1), 4 * half * NP:4 * (half + 1) * NP].to_broadcast([128, 4 * NP])
                                 ).then_inc(Bs[f"gates{half}"], 16)

            batch_loads(0)
            batch_loads(1)
            batch_loads(2)
            gates_move(0)
            with sp.Fori(1, B - 2) as i:
                batch_loads(i + 2)
                gates_move(i)
            gates_move(B - 2)
            gates_move(B - 1)
            sp.wait_ge(Bs["out_stored"], 16 * B)

        @block.tensor
        def _(pe):
            mm = nc.tensor.matmul
            tr = nc.tensor.transpose

            def a_project(b):
                pe.wait_ge(A["x_loaded"], 16 * (b + 1))
                if later(b):
                    pe.wait_ge(A["kT_ready"], b)
                for t in range(NT):
                    last = tr(ps[:, 6, TP * t:TP * t + TP], xa[0:TP, t, :], ident[0:TP, 0:TP])
                last.then_inc(A["x_turned"], 1)
                yield
                if later(b):
                    pe.wait_ge(A["qT_ready"], b)
                pe.wait_ge(A["xT"], b + 1)
                mm(ps[:, 7, 0:N], wqkv[:, 0:C], xTa[:], start=True, stop=True).then_inc(A["q_proj"], 1)
                yield
                mm(ps[:, 6, 0:N], wqkv[:, C:2 * C], xTa[:], start=True, stop=True).then_inc(A["k_proj"], 1)
                yield

            def a_scores(b, u, ahead=None):
                pe.wait_ge(A[f"stacked{u}"], 16 * NC6 * (b - u + 2))
                for n in range(H):
                    if later(b) or n >= 2:
                        pe.wait_ge(A["maxed"], 8 * b + n - 1)
                    for t in range(NT):
                        last = mm(ps[0:TP, 3 * (n % 2) + t, 0:N], qstack[u][:, n, TP * t:TP * t + TP],
                                  kstack[u][:, n, 0:N], start=True, stop=True)
                    last.then_inc(A["scores"], 1)
                    if ahead and n in (0, 1, 3):
                        next(ahead)

            pe.wait_ge(s_w0, 16 * EARLY)
            pe.wait_ge(s_set, NSET)
            for b in range(2):
                for _ in a_project(b):
                    pass
            for b in range(2):
                a_scores(b, b, a_project(b + 2))
            with pe.Fori(1, B // 2 - 1) as j:
                for u in range(2):
                    a_scores(2 * j + u, u, a_project(2 * j + u + 2))
            a_scores(B - 2, 0)
            a_scores(B - 1, 1)

            for g in range(2):
                pe.wait_ge(A["maxed"], 8 * B)
                if g:
                    pe.wait_ge(T["rows"], 1)
                else:
                    pe.wait_ge(A["kT_ready"], B)
                for t in range(NT):
                    last = tr(ps[:, 6, TP * t:TP * t + TP], maxes[0:TP, t, 128 * g:128 * g + 128], ident[0:TP, 0:TP])
                last.then_inc(T["turned"], 1)
            for g in range(2):
                pe.wait_ge(T["idx_ready"], g + 1)
                if g:
                    pe.wait_ge(T["idx_col"], 1)
                tr(ps[0:S, 7, 0:128], top_if[:], ident).then_inc(T["idx_turned"], 1)
            pe.wait_ge(T["idx_col"], 2)
            pe.wait_ge(s_w, 16 * (len(loads) - EARLY))

            W = Bs

            def attend(b):
                pe.wait_ge(W["x_loaded"], 16 * (b + 1))
                if later(b):
                    pe.wait_ge(W["attnT"], b)
                for t in range(NT):
                    last = tr(ps[:, 2, TP * t:TP * t + TP], x[0:TP, t, :], ident[0:TP, 0:TP])
                last.then_inc(W["x_turned"], 1)
                yield
                if later(b):
                    pe.wait_ge(W["xn1"], b)
                pe.wait_ge(W["xT"], b + 1)
                mm(ps[:, 2, 0:N], wqkv[:, C:2 * C], xT[:], start=True, stop=True).then_inc(W["k_proj"], 1)
                for t in range(NT):
                    for k, w in ((0, wqkv[:, 0:C]), (1, wqkv[:, 2 * C:3 * C])):
                        last = mm(ps[0:TP, t // 2, 256 * (t % 2) + 128 * k:256 * (t % 2) + 128 * k + 128],
                                  xT[:, TP * t:TP * t + TP], w, start=True, stop=True)
                last.then_inc(W["qv_proj"], 1)
                yield
                pe.wait_ge(W["q_hi"], b + 1)
                pe.wait_ge(W["q_lo"], b + 1)
                pe.wait_ge(W["v_rows"], b + 1)
                pe.wait_ge(W["pick"], b + 1)
                for half in range(2):
                    for t in range(NT):
                        for part, q in enumerate((q_hi, q_lo)):
                            last = mm(ps[:, half, 0:384], q[0:TP, t, :], pick[0:TP, t, 384 * half:384 * half + 384],
                                      start=(t == 0 and part == 0), stop=(t == NT - 1 and part == 1))
                last.then_inc(W["gathered"], 1)
                yield
                pe.wait_ge(W["qsel"], b + 1)
                pe.wait_ge(W["kTc"], b + 1)
                pe.wait_ge(W["nm_loaded"], 16 * (b + 1))
                for t in range(NT):
                    if t:
                        pe.wait_ge(W[f"e{t - 1}"], b + 1)
                    for half in range(2):
                        bank = ps[0:TP, half, 0:384]
                        mm(bank, kTc[:, TP * t:TP * t + TP], qsel[:, 384 * half:384 * half + 384], start=True, stop=False)
                        last = mm(bank, ones_bf[:, 0:TP], negmax[:, 384 * half:384 * half + 384], start=False, stop=True)
                    last.then_inc(W[f"s{t}"], 1)
                    if t == 0:
                        for k in range(NT):
                            last = mm(ps[0:S, 2, 0:H * VW], mean_w[0:TP, :], v[0:TP, k, 0:H * VW], start=(k == 0), stop=(k == NT - 1))
                        last.then_inc(W["vmean"], 1)
                    yield
                pe.wait_ge(W["e2"], b + 1)
                for h in range(H):
                    for t in range(NT):
                        last = mm(ps[0:S, h // 4, S * (h % 4):S * (h % 4) + S], ex[0:TP, t, S * h:S * h + S],
                                  v[0:TP, t, VW * h:VW * h + S], start=(t == 0), stop=(t == NT - 1))
                last.then_inc(W["av"], 1)
                yield
                pe.wait_ge(W["on"], b + 1)
                pe.wait_ge(W["place"], b + 1)
                for h in range(H):
                    for part in range(2):
                        last = mm(ps[:, 2, 0:NE], opad[part][:, C * h:C * h + C], place[:, h, :],
                                  start=(h == 0 and part == 0), stop=(h == H - 1 and part == 1))
                last.then_inc(W["scattered"], 1)
                yield
                pe.wait_ge(W["attnT"], b + 1)
                for t in range(NT):
                    last = mm(ps[0:TP, 0, 128 * t:128 * t + 128], attnT[:, TP * t:TP * t + TP], wo[:], start=True, stop=True)
                last.then_inc(W["oproj"], 1)
                yield

            def rest(i):
                pe.wait_ge(W["xn1"], i + 1)
                if later(i):
                    pe.wait_ge(W["gateT"], i)
                for t in range(NT):
                    last = tr(ps[:, 3, TP * t:TP * t + TP], xn[0:TP, t, :], ident[0:TP, 0:TP])
                last.then_inc(W["x1_turned"], 1)
                yield
                pe.wait_ge(W["x1T"], i + 1)
                for f in range(NF):
                    if f >= 2:
                        pe.wait_ge(W[f"g{f - 2}"], i + 1)
                    mm(ps[:, 4 - f % 2, 0:N], w1[:, 128 * f:128 * f + 128], x1T[:], start=True, stop=True).then_inc(W[f"f{f}"], 1)
                    if f % 2:
                        yield
                for f in range(NF):
                    pe.wait_ge(W[f"g{max(f, 2)}"], i + 1)
                    last = mm(ps[:, 4, 0:N], w2[:, f, :], hT[:, f, :], start=(f == 0), stop=(f == NF - 1))
                last.then_inc(W["ffn2"], 1)
                yield
                pe.wait_ge(W["yT"], i + 1)
                for t in range(NT):
                    last = tr(ps[0:TP, 3, 128 * t:128 * t + 128], yT[:, TP * t:TP * t + TP], ident)
                last.then_inc(W["y_turned"], 1)
                yield
                pe.wait_ge(W["xn2"], i + 1)
                for t in range(NT):
                    last = tr(ps[:, 4, TP * t:TP * t + TP], xn2[0:TP, t, :], ident[0:TP, 0:TP])
                last.then_inc(W["x2_turned"], 1)
                yield
                pe.wait_ge(W["x2T"], i + 1)
                for k in range(3):
                    last = mm(ps[:, 3, 0:N], cw[:, k, :], x2p[:, k:k + N], start=(k == 0), stop=(k == 2))
                last.then_inc(W["conv"], 1)
                yield
                pe.wait_ge(W["el"], i + 1)
                for t in range(PT_):
                    last = tr(ps[0:PR, 4, 128 * t:128 * t + 128], el[:, PR * t:PR * t + PR], ident)
                last.then_inc(W["el_turned"], 1)
                yield
                pe.wait_ge(W["hn"], i + 1)
                for t in range(PT_):
                    last = tr(ps[:, 3, PR * t:PR * t + PR], hn[0:PR, t, :], ident[0:PR, 0:PR])
                last.then_inc(W["hn_turned"], 1)
                yield
                pe.wait_ge(W["hnT"], i + 1)
                mm(ps[:, 4, 0:NP], wqq[:], hnT[:], start=True, stop=True)
                mm(ps[:, 4, 256:256 + NP], wkk[:], hnT[:], start=True, stop=True).then_inc(W["qk_proj"], 1)
                for t in range(PT_):
                    last = mm(ps[0:PR, 3, 128 * t:128 * t + 128], hnT[:, PR * t:PR * t + PR], wv2[:], start=True, stop=True)
                last.then_inc(W["v2_proj"], 1)
                yield
                pe.wait_ge(W["qa"], i + 1)
                pe.wait_ge(W["ka"], i + 1)
                for t in range(PT_):
                    o = ps[0:PR, 4, NP * t:NP * t + NP]
                    mm(o, qa[:, PR * t:PR * t + PR], ka[:], start=True, stop=False)
                    last = mm(o, ones_f[D2:128, :], kk[D2:128, :], start=False, stop=True)
                last.then_inc(W["dist"], 1)
                yield
                pe.wait_ge(W["e2x"], i + 1)
                pe.wait_ge(W["v2"], i + 1)
                for m in range(PT_):
                    for t in range(PT_):
                        last = tr(ps[0:PR, 3, NP * m + PR * t:NP * m + PR * t + PR], e2[0:PR, t, PR * m:PR * m + PR],
                                  ident[0:PR, 0:PR])
                last.then_inc(W["e2_turned"], 1)
                yield
                pe.wait_ge(W["e2T"], i + 1)
                for t in range(PT_):
                    for m in range(PT_):
                        last = mm(ps[0:PR, 4, 128 * t:128 * t + 128], e2T[0:PR, m, PR * t:PR * t + PR], v2[0:PR, m, :],
                                  start=(m == 0), stop=(m == PT_ - 1))
                last.then_inc(W["av2"], 1)
                yield
                pe.wait_ge(W["xn4"], i + 1)
                for t in range(PT_):
                    last = tr(ps[:, 3, PR * t:PR * t + PR], xn4[0:PR, t, :], ident[0:PR, 0:PR])
                last.then_inc(W["h2n_turned"], 1)
                yield
                pe.wait_ge(W["h2nT"], i + 1)
                for t in range(PT_):
                    last = mm(ps[0:PR, 4, E * t:E * t + E], h2nT[:, PR * t:PR * t + PR], wr[:], start=True, stop=True)
                last.then_inc(W["router"], 1)
                yield
                pe.wait_ge(W["gate"], i + 1)
                for t in range(PT_):
                    last = tr(ps[0:E, 3, PR * t:PR * t + PR], gate[0:PR, t, :], ident[0:PR, 0:PR])
                last.then_inc(W["gate_turned"], 1)
                yield

            def turn_out(b):
                pe.wait_ge(W["moeT"], b + 1)
                for t in range(PT_):
                    last = tr(ps[0:PR, 5, 256 + C * t:256 + C * t + C], moeT[:, PR * t:PR * t + PR], ident)
                last.then_inc(W["out_turned"], 1)

            def experts(b):
                def hidden(e):
                    if e == 0:
                        pe.wait_ge(W["h2nT_m"], b + 1)
                    for half in range(2):
                        if later(b) or e:
                            pe.wait_ge(m_relu, NF * (E * b + e) - 2 * (1 - half))
                        for k in range(2):
                            f = 2 * half + k
                            last = mm(ps[:, 6 + half, 256 * k:256 * k + NP], mw1[:, e, 128 * f:128 * f + 128], h2nT_m[:],
                                      start=True, stop=True)
                        last.then_inc(m_h[half], 1)

                def down(e):
                    if e == 0:
                        pe.wait_ge(W["gateT"], b + 1)
                        if later(b):
                            pe.wait_ge(W["out_ready"], b)
                        mm(ps[:, 5, 0:NP], mb2[:], gateT[:], start=True, stop=False).then_inc(W["bias2"], 1)
                    pe.wait_ge(m_gated, E * b + e + 1)
                    for f in range(NF):
                        last = mm(ps[:, 5, 0:NP], mw2[:, e, f, :], mh[e % 2][:, f, :],
                                  start=False, stop=(e == E - 1 and f == NF - 1))
                    last.then_inc(m_y, 1)

                hidden(0)
                if later(b):
                    turn_out(b - 1)
                yield
                for e in range(E):
                    if e + 1 < E:
                        hidden(e + 1)
                    yield
                    down(e)
                    yield

            all_batches(pe, attend, rest, experts)
            turn_out(B - 1)

        @block.scalar
        def _(act):
            fn = nc.scalar.activation
            act.wait_ge(s_w0, 16 * EARLY)
            act.wait_ge(s_set, NSET)

            def a_evac(b):
                act.wait_ge(A["x_turned"], b + 1)
                if later(b):
                    act.wait_ge(A["k_proj"], b)
                fn(xTa[:], ps[:, 6, 0:N], ACT.Copy).then_inc(A["xT"], 1)
                act.wait_ge(A["q_proj"], b + 1)
                if later(b):
                    act.wait_ge(A["qrem"], b)
                    act.wait_ge(A["q_out"], 16 * b)
                fn(qTa[:], ps[:, 7, 0:N], ACT.Identity, bias=bqkT[:, 0:1])
                fn(parts[0][:, 0, 0:N], ps[:, 7, 0:N], ACT.Identity, bias=bqkT[:, 0:1]).then_inc(A["qT_ready"], 1)
                act.wait_ge(A["k_proj"], b + 1)
                if later(b):
                    act.wait_ge(A["kc_ready"], b)
                fn(kTa[:], ps[:, 6, 0:N], ACT.Identity, bias=bqkT[:, 1:2], accum_out=ksum[:, 0:1]).then_inc(A["kT_ready"], 1)
                act.wait_ge(A["mean_ready"], b + 1)
                if later(b):
                    act.wait_ge(A["krem"], b)
                    act.wait_ge(A["k_out"], 16 * b)
                fn(kca[:], kTa[:], ACT.Identity, bias=ksum[:, 1:2])
                fn(parts[1][:, 0, 0:N], kTa[:], ACT.Identity, bias=ksum[:, 1:2]).then_inc(A["kc_ready"], 1)
                for u, n in ((0, "q"), (1, "k")):
                    act.wait_ge(A[n + "rem"], b + 1)
                    fn(parts[u][:, 1, 0:N], rem[u][:], ACT.Copy).then_inc(A[n + "2"], 1)

            a_evac(0)
            with act.Fori(1, B) as b:
                a_evac(b)
            act.wait_ge(s_w, 16 * (len(loads) - EARLY))

            W = Bs

            def attend(b):
                act.wait_ge(W["x_turned"], b + 1)
                fn(xT[:], ps[:, 2, 0:N], ACT.Copy).then_inc(W["xT"], 1)
                yield
                act.wait_ge(W["k_proj"], b + 1)
                fn(kT[:], ps[:, 2, 0:N], ACT.Identity, bias=bqkT[:, 1:2], accum_out=ksum_b[:, 0:1]).then_inc(W["kT"], 1)
                act.wait_ge(W["q_rows"], b + 1)
                fn(q_hi[0:TP], qrow[0:TP], ACT.Copy).then_inc(W["q_hi"], 1)
                yield
                yield
                for t in range(NT):
                    act.wait_ge(W[f"s{t}"], b + 1)
                    fn(ex[0:TP, t, :].rearrange("p (a s) -> p a s", a=2), ps[0:TP, 0:2, 0:384],
                       ACT.Exp, scale=1.0 / float(np.sqrt(DK))).then_inc(W[f"e{t}"], 1)
                    yield
                yield
                act.wait_ge(W["scattered"], b + 1)
                fn(attnT[:], ps[:, 2, 0:N], ACT.Copy).then_inc(W["attnT"], 1)
                yield

            def rest(i):
                act.wait_ge(W["x1_turned"], i + 1)
                fn(x1T[:], ps[:, 3, 0:N], ACT.Identity, bias=vecs[:, 2:3], scale=vecs[:, 1:2]).then_inc(W["x1T"], 1)
                yield
                for f in range(NF):
                    act.wait_ge(W[f"f{f}"], i + 1)
                    fn(hT[:, f, :], ps[:, 4 - f % 2, 0:N], ACT.Gelu, bias=b1[:, f:f + 1]).then_inc(W[f"g{f}"], 1)
                    if f % 2:
                        yield
                yield
                yield
                act.wait_ge(W["x2_turned"], i + 1)
                fn(x2p[:, 1:N + 1], ps[:, 4, 0:N], ACT.Identity, bias=vecs[:, 4:5], scale=vecs[:, 3:4])
                fn(x2p[:, 0:1], ps[:, 4, N - 1:N], ACT.Identity, bias=vecs[:, 4:5], scale=vecs[:, 3:4])
                fn(x2p[:, N + 1:N + 2], ps[:, 4, 0:1], ACT.Identity, bias=vecs[:, 4:5], scale=vecs[:, 3:4]).then_inc(W["x2T"], 1)
                yield
                act.wait_ge(W["conv"], i + 1)
                fn(cp[:, 1:N + 1], ps[:, 3, 0:N], ACT.Identity, bias=vecs[:, 5:6]).then_inc(W["cp"], 1)
                act.wait_ge(W["mx"], i + 1)
                fn(emn[:], el[:], ACT.Exp).then_inc(W["emn"], 1)
                yield
                yield
                act.wait_ge(W["hn_turned"], i + 1)
                fn(hnT[:], ps[:, 3, 0:NP], ACT.Copy).then_inc(W["hnT"], 1)
                yield
                act.wait_ge(W["qk_proj"], i + 1)
                fn(qa[0:D2, :], ps[0:D2, 4, 0:NP], ACT.Copy)
                fn(qa[D2:128, :], ps[D2:128, 4, 0:NP], ACT.Square).then_inc(W["qa"], 1)
                fn(ka[0:D2, :], ps[0:D2, 4, 256:256 + NP], ACT.Copy, scale=-2.0)
                fn(kk[D2:128, :], ps[D2:128, 4, 256:256 + NP], ACT.Square).then_inc(W["ka"], 1)
                act.wait_ge(W["v2_proj"], i + 1)
                fn(v2[0:PR], ps[0:PR, 3, 0:256].rearrange("p (t c) -> p t c", t=PT_), ACT.Copy).then_inc(W["v2"], 1)
                yield
                act.wait_ge(W["dclip"], i + 1)
                for t in range(PT_):
                    last = fn(e2[0:PR, t, :], d2[0:PR, t, :], ACT.Exp, scale=lam[0:PR, 3:4], bias=dbias[0:PR, t:t + 1],
                              accum_out=rs2[0:PR, t:t + 1])
                last.then_inc(W["e2x"], 1)
                yield
                act.wait_ge(W["e2_turned"], i + 1)
                fn(e2T[0:PR].rearrange("p m n -> p (m n)"), ps[0:PR, 3, 0:PT_ * NP], ACT.Copy).then_inc(W["e2T"], 1)
                yield
                yield
                act.wait_ge(W["h2n_turned"], i + 1)
                if later(i):
                    act.wait_ge(W["h2nT_m"], i)
                fn(h2nT[:], ps[:, 3, 0:NP], ACT.Copy).then_inc(W["h2nT"], 1)
                yield
                act.wait_ge(W["lg"], i + 1)
                for t in range(PT_):
                    last = fn(elg[0:PR, t, :], lg[0:PR, t, :], ACT.Exp, bias=nm1[0:PR, t:t + 1], accum_out=rse[0:PR, t:t + 1])
                    last = fn(e12[0:PR, t, :], m8[0:PR, t, 0:2], ACT.Exp, bias=nm1[0:PR, t:t + 1])
                last.then_inc(W["elg"], 1)
                yield
                act.wait_ge(W["gate_turned"], i + 1)
                if later(i):
                    act.wait_ge(W["bias2"], i)
                    act.wait_ge(W["gate_out"], 16 * i)
                fn(gateT[:], ps[0:E, 3, 0:NP], ACT.Copy).then_inc(W["gateT"], 1)
                yield

            def store(b):
                act.wait_ge(W["out_ready"], b + 1)
                act.dma_start(od[bass.ds(b, 1)].rearrange("b p t c -> (b p) t c"), ostage[0:PR]).then_inc(W["out_stored"], 16)

            def experts(b):
                def relu(e):
                    if e >= 2:
                        act.wait_ge(m_y, E * b + e - 1)
                    for f in range(NF):
                        if f % 2 == 0:
                            act.wait_ge(m_h[f // 2], E * b + e + 1)
                        fn(mh[e % 2][:, f, :], ps[:, 6 + f // 2, 256 * (f % 2):256 * (f % 2) + NP], ACT.Relu,
                           bias=mb1[:, NF * e + f:NF * e + f + 1]).then_inc(m_relu, 1)

                relu(0)
                if later(b):
                    store(b - 1)
                yield
                for e in range(E):
                    if e + 1 < E:
                        relu(e + 1)
                    yield
                    yield
                act.wait_ge(m_y, E * (b + 1))
                if later(b):
                    act.wait_ge(W["out_turned"], b)
                fn(moeT[:], ps[:, 5, 0:NP], ACT.Copy).then_inc(W["moeT"], 1)
                yield

            all_batches(act, attend, rest, experts)
            store(B - 1)

        @block.gpsimd
        def _(pool):
            g = nc.gpsimd
            g.memset(mean_w[:], 1.0 / N).then_inc(s_set, 1)
            g.memset(ones_bf[:], 1.0).then_inc(s_set, 1)
            g.memset(ones_f[:], 1.0).then_inc(s_set, 1)
            g.memset(mhalf[:], -0.5).then_inc(s_set, 1)
            for u in range(2):
                g.memset(parts[u][:], 0.0).then_inc(s_set, 1)
            g.memset(negmax[:], 0.0).then_inc(s_set, 1)
            g.memset(opad[0][:].bitcast(F32), 0.0).then_inc(s_set, 1)
            g.memset(opad[1][:].bitcast(F32), 0.0).then_inc(s_set, 1)
            g.memset(cp[:], -BIG).then_inc(s_set, 1)
            g.memset(ka[:], 1.0).then_inc(s_set, 1)
            g.memset(v[:], 0.0).then_inc(s_set, 1)
            pool.wait_ge(s_set, 12)
            for t in range(NT):
                last = g.memset(v[:, t, 0:H * VW].rearrange("p (h c) -> p h c", c=VW)[:, :, DK:VW], 1.0)
            last.then_inc(s_set, 1)
            g.memset(euler[:], float(np.e)).then_inc(s_e, 1)
            pool.wait_ge(s_w0, 16 * EARLY)
            pool.wait_ge(s_e, 1)
            g.tensor_tensor(lam[:, 1:2], euler[:], lam[:, 0:1], ALU.pow).then_inc(s_lam, 1)

            def split(b):
                for u, n, whole, ready in ((0, "q", qTa, "qT_ready"), (1, "k", kca, "kc_ready")):
                    pool.wait_ge(A[ready], b + 1)
                    if later(b):
                        pool.wait_ge(A[n + "3"], b)
                    g.tensor_tensor(rem[u][:], whole[:], parts[u][:, 0, 0:N], ALU.subtract).then_inc(A[n + "rem"], 1)
                for u, n in ((0, "q"), (1, "k")):
                    pool.wait_ge(A[n + "2"], b + 1)
                    g.tensor_tensor(parts[u][:, 2, 0:N], rem[u][:], parts[u][:, 1, 0:N], ALU.subtract).then_inc(A[n + "3"], 1)

            split(0)
            with pool.Fori(1, B) as b:
                split(b)

            def root(k, u, b, rows, nt):
                pool.wait_ge(Bs[f"veps{k}"], b + 1)
                g.tensor_tensor(rstd[u][0:rows, 0:nt], veps[u][0:rows, 0:nt], mhalf[0:rows, 0:nt], ALU.pow).then_inc(Bs[f"rstd{k}"], 1)

            def attend(b):
                yield
                pool.wait_ge(Bs["q_hi"], b + 1)
                g.tensor_tensor(q_lo[0:TP].rearrange("p t c -> p (t c)"), qrow[0:TP].rearrange("p t c -> p (t c)"),
                                q_hi[0:TP].bitcast(F32).rearrange("p t c -> p (t c)"), ALU.subtract).then_inc(Bs["q_lo"], 1)
                for _ in range(7):
                    yield
                root(1, 0, b, TP, NT)
                yield

            def rest(i):
                for slot in range(SLOTS):
                    if slot == 4:
                        root(2, 1, i, TP, NT)
                    if slot == 7:
                        root(3, 1, i, PR, PT_)
                        root(4, 1, i, PR, PT_)
                    if slot == 12:
                        root(5, 1, i, PR, PT_)
                    if slot == 17:
                        pool.wait_ge(Bs["h2nT"], i + 1)
                        if later(i):
                            for half in range(2):
                                pool.wait_ge(m_h[half], E * i)
                        pool.sem_inc(s_alone, 1)
                        g.tensor_copy(h2nT_m[:], h2nT[:]).then_inc(Bs["h2nT_m"], 1)
                    yield

            def experts(b):
                def weigh(e):
                    pool.wait_ge(m_relu, NF * (E * b + e + 1))
                    if e % 4 == 0:
                        pool.wait_ge(Bs[f"gates{e // 4}"], 16 * (b + 1))
                    g.tensor_tensor(mh[e % 2][:], mh[e % 2][:], gate_bc[:, e, None, :].to_broadcast([128, NF, NP]),
                                    ALU.mult).then_inc(m_gated, 1)

                weigh(0)
                yield
                for e in range(E):
                    if e + 1 < E:
                        weigh(e + 1)
                    yield
                    yield

            all_batches(pool, attend, rest, experts)

        @block.vector
        def _(dve):
            vv = nc.vector
            dve.wait_ge(s_w0, 16 * EARLY)
            cnt = [0]

            def setup(ins):
                cnt[0] += 1
                ins.then_inc(T["chain"], 1)
                dve.wait_ge(T["chain"], cnt[0])

            dve.wait_ge(s_lam, 1)
            setup(vv.tensor_scalar(lam[:, 1:2], lam[:, 1:2], 0.001, None, ALU.max))
            setup(vv.tensor_tensor(lam[:, 2:3], lam[:, 1:2], lam[:, 1:2], ALU.mult))
            setup(vv.tensor_scalar(lam[:, 1:2], lam[:, 2:3], 2.0, None, ALU.mult))
            setup(vv.reciprocal(lam[:, 2:3], lam[:, 1:2]))
            vv.tensor_scalar(lam[:, 3:4], lam[:, 2:3], -1.0, None, ALU.mult).then_inc(s_set, 1)
            dve.wait_ge(s_set, NSET)

            def a_batch(b):
                dve.wait_ge(A["kT_ready"], b + 1)
                vv.tensor_scalar(ksum[:, 1:2], ksum[:, 0:1], -1.0 / N, None, ALU.mult).then_inc(A["mean_ready"], 1)

            def a_max(b, ahead=None):
                for n in range(H):
                    if ahead is not None and n == 5:
                        a_batch(ahead)
                    dve.wait_ge(A["scores"], 8 * b + n + 1)
                    vv.tensor_reduce(maxes[0:TP, :, bass.ds(H * b + n, 1)].rearrange("p t k -> p (t k)"),
                                     ps[0:TP, 3 * (n % 2):3 * (n % 2) + 3, 0:N], AX.X, ALU.max).then_inc(A["maxed"], 1)

            a_batch(0)
            a_batch(1)
            a_max(0, 2)
            with dve.Fori(1, B - 2) as b:
                a_max(b, b + 2)
            a_max(B - 2)
            a_max(B - 1)

            for gr in range(2):
                dve.wait_ge(T["turned"], gr + 1)
                if gr:
                    dve.wait_ge(T["stored"], 4 * 16)
                    dve.wait_ge(T["idx_turned"], 1)
                vv.tensor_copy(mrow[:], ps[:, 6, 0:N]).then_inc(T["rows"], 1)
                dve.wait_ge(T["rows"], gr + 1)
                src = mrow
                for r in range(S // 8):
                    t8 = top_v[:, 8 * r:8 * r + 8]
                    setup(vv.max(t8, src[:]))
                    setup(vv.max_index(top_i[:, 8 * r:8 * r + 8], t8, src[:]))
                    if r < S // 8 - 1:
                        dst = mwork if src is mrow else mrow
                        setup(vv.match_replace(dst[:], t8, src[:], -BIG))
                        src = dst
                setup(vv.tensor_copy(top_if[:], top_i[:]))
                setup(vv.memset(top_if[:, TOP:S], -1.0))
                setup(vv.memset(top_v[:, TOP:S], 0.0))
                setup(vv.tensor_scalar(top_r[:], top_v[:], -1.0, None, ALU.mult))
                setup(vv.tensor_copy(top_p[0][:], top_r[:]))
                setup(vv.tensor_tensor(top_v[:], top_r[:], top_p[0][:], ALU.subtract))
                setup(vv.tensor_copy(top_p[1][:], top_v[:]))
                setup(vv.tensor_tensor(top_r[:], top_v[:], top_p[1][:], ALU.subtract))
                vv.tensor_copy(top_p[2][:], top_r[:]).then_inc(T["idx_ready"], 1)
                if gr == 0:
                    dve.wait_ge(T["idx_turned"], 1)
                    vv.tensor_copy(idx_col[:, 0:128], ps[0:S, 7, 0:128]).then_inc(T["idx_col"], 1)
            dve.wait_ge(T["idx_turned"], 2)
            vv.tensor_copy(idx_col[:, 128:256], ps[0:S, 7, 0:128]).then_inc(T["idx_col"], 1)
            dve.wait_ge(T["idx_col"], 2)
            dve.wait_ge(s_w, 16 * (len(loads) - EARLY))

            W = Bs

            def chained(b, sem_, per):
                k = [0]

                def link(ins, alone=False):
                    k[0] += 1
                    ins.then_inc(sem_, 1)
                    dve.wait_ge(sem_, b * per + k[0])
                    if alone:
                        dve.sem_inc(s_alone, 1)

                return link, k

            def norm(b, link, u, src, dst, rows, nt, n):
                for t in range(nt):
                    last = vv.bn_stats(st[u][0:rows, t, :], src(t))
                link(last, alone=True)
                for t in range(nt):
                    last = vv.bn_aggr(mv[u][0:rows, t, :], st[u][0:rows, t, :])
                last.then_inc(W[f"aggr{n}"], 1)
                dve.wait_ge(W[f"aggr{n}"], b + 1)
                vv.tensor_scalar(veps[u][0:rows, 0:nt], mv[u][0:rows, 0:nt, 1], EPS, None, ALU.add).then_inc(W[f"veps{n}"], 1)
                dve.wait_ge(W[f"rstd{n}"], b + 1)
                for t in range(nt):
                    last = vv.tensor_scalar(dst(t), src(t), mv[u][0:rows, t, 0:1], rstd[u][0:rows, t:t + 1],
                                            ALU.subtract, ALU.mult)
                return last

            def attend(b):
                link, k = chained(b, chain_f, CF)
                dve.wait_ge(W["idx_loaded"], 16 * (b + 1))
                if later(b):
                    dve.wait_ge(W["gathered"], b)
                for t in range(NT):
                    last = vv.tensor_scalar(pick[0:TP, t, :], idx_bc[0:TP, :], kc[0:TP, K_TOK + t:K_TOK + t + 1], None, ALU.is_equal)
                last.then_inc(W["pick"], 1)
                yield
                dve.wait_ge(W["qv_proj"], b + 1)
                qv = ps[0:TP, 0:2, :].rearrange("p a c -> p (a c)")[:, 0:256 * NT].rearrange("p (t c) -> p t c", t=NT)
                vv.tensor_tensor(qrow[0:TP], qv[:, :, 0:C], bqv_bc[0:TP, None, 0:C].to_broadcast([TP, NT, C]), ALU.add).then_inc(W["q_rows"], 1)
                for t in range(NT):
                    last = vv.tensor_tensor(v[0:TP, t, 0:H * VW].rearrange("p (h c) -> p h c", c=VW)[:, :, 0:DK],
                                            qv[:, t, C:2 * C].rearrange("p (h c) -> p h c", c=DK),
                                            bqv_bc[0:TP, C:2 * C].rearrange("p (h c) -> p h c", c=DK), ALU.add)
                last.then_inc(W["v_rows"], 1)
                dve.wait_ge(W["kT"], b + 1)
                link(vv.tensor_scalar(ksum_b[:, 1:2], ksum_b[:, 0:1], -1.0 / N, None, ALU.mult))
                vv.tensor_scalar(kTc[:], kT[:], ksum_b[:, 1:2], None, ALU.add).then_inc(W["kTc"], 1)
                yield
                dve.wait_ge(W["gathered"], b + 1)
                vv.tensor_tensor(qsel[:].rearrange("p (a s) -> p a s", a=2), ps[:, 0:2, 0:384],
                                 kc[:, K_BM:K_BM + 768].rearrange("p (a s) -> p a s", a=2), ALU.mult).then_inc(W["qsel"], 1)
                dve.wait_ge(W["x_loaded"], 16 * (b + 1))
                vv.tensor_tensor(xb[0:TP], x[0:TP], bo_bc[0:TP, None, :].to_broadcast([TP, NT, C]), ALU.add).then_inc(W["xb"], 1)
                yield
                dve.wait_ge(W["vmean"], b + 1)
                vm = ps[0:S, 2, 0:H * VW].rearrange("p (h c) -> p h c", c=VW)[:, :, 0:DK]
                if later(b):
                    dve.wait_ge(W["scattered"], b)
                vv.tensor_scalar(vmw[:], vm, kc[0:S, K_M + 1:K_M + 2], None, ALU.mult)
                link(vv.tensor_scalar(self_row[:].rearrange("p (h c) -> p h c", c=DK), vm, kc[0:S, K_M:K_M + 1], None, ALU.mult))
                link(vv.tensor_copy(opad[0][:, 0:C], self_row[:]))
                vv.tensor_tensor(opad[1][:, 0:C], self_row[:], opad[0][:, 0:C].bitcast(F32), ALU.subtract)
                yield
                vv.tensor_scalar(place[:, 0, :], kc[0:S, K_ROW:K_ROW + NE], idx_col[:, bass.ds(H * b, 1)],
                                 kc[0:S, K_M:K_M + 1], ALU.is_equal, ALU.max)
                for h in range(1, 4):
                    vv.tensor_scalar(place[:, h, :], kc[0:S, K_ROW:K_ROW + NE], idx_col[:, bass.ds(H * b + h, 1)],
                                     None, ALU.is_equal)
                yield
                for h in range(4, H):
                    last = vv.tensor_scalar(place[:, h, :], kc[0:S, K_ROW:K_ROW + NE], idx_col[:, bass.ds(H * b + h, 1)],
                                            None, ALU.is_equal)
                last.then_inc(W["place"], 1)
                yield
                dve.wait_ge(W["av"], b + 1)
                av = ps[0:S, 0:2, 0:384].rearrange("p a (h c) -> p a h c", c=S)
                link(vv.reciprocal(rden[:].rearrange("p (a h) -> p a h", a=2)[:, :, :, None], av[:, :, :, DK:VW]))
                for half in range(2):
                    last = vv.tensor_tensor(onorm[:, 4 * half:4 * half + 4, :], av[:, half, :, 0:DK],
                                            rden[:, 4 * half:4 * half + 4, None].to_broadcast([S, 4, DK]), ALU.mult)
                link(last)
                link(vv.tensor_tensor(on_all[:], onorm[:], vmw[:], ALU.subtract))
                hi, lo = (o[:].rearrange("p (h c) -> p h c", c=C + DK)[:, :, 0:DK] for o in opad)
                link(vv.tensor_copy(hi, on_all[:]))
                vv.tensor_tensor(lo, on_all[:], hi.bitcast(F32), ALU.subtract).then_inc(W["on"], 1)
                yield
                yield
                dve.wait_ge(W["oproj"], b + 1)
                dve.wait_ge(W["xb"], b + 1)
                link(vv.tensor_tensor(r1[0:TP].rearrange("p t c -> p (t c)"), ps[0:TP, 0, 0:NT * C],
                                      xb[0:TP].rearrange("p t c -> p (t c)"), ALU.add))
                if later(b):
                    dve.wait_ge(W["x1_turned"], b)
                norm(b, link, 0, lambda t: r1[0:TP, t, :], lambda t: xn[0:TP, t, :], TP, NT, 1).then_inc(W["xn1"], 1)
                assert k[0] == CF, ("CF", k[0])
                yield

            def rest(i):
                link, k = chained(i, chain_k, CK)
                yield
                yield
                yield
                dve.wait_ge(W["ffn2"], i + 1)
                vv.scalar_tensor_tensor(yT[:], ps[:, 4, 0:N], vecs[:, 0:1], x1T[:], ALU.add, ALU.add).then_inc(W["yT"], 1)
                yield
                dve.wait_ge(W["y_turned"], i + 1)
                norm(i, link, 1, lambda t: ps[0:TP, 3, C * t:C * t + C], lambda t: xn2[0:TP, t, :], TP, NT, 2).then_inc(W["xn2"], 1)
                yield
                yield
                dve.wait_ge(W["cp"], i + 1)
                link(vv.tensor_tensor(mx[:], cp[:, 0:2 * NP:2], cp[:, 1:2 * NP:2], ALU.max))
                link(vv.tensor_tensor(mx[:], mx[:], cp[:, 2:2 * NP + 1:2], ALU.max))
                vv.tensor_scalar(el[:], mx[:], 0.0, None, ALU.min).then_inc(W["mx"], 1)
                dve.wait_ge(W["emn"], i + 1)
                link(vv.tensor_scalar(emn[:], emn[:], -1.0, None, ALU.add))
                vv.scalar_tensor_tensor(el[:], mx[:], 0.0, emn[:], ALU.max, ALU.add).then_inc(W["el"], 1)
                yield
                dve.wait_ge(W["el_turned"], i + 1)
                link(norm(i, link, 1, lambda t: ps[0:PR, 4, C * t:C * t + C], lambda t: xn3[0:PR, t, :], PR, PT_, 3))
                link(vv.tensor_tensor(xn3[0:PR], xn3[0:PR], cng_bc[0:PR, None, :].to_broadcast([PR, PT_, C]), ALU.mult))
                link(vv.tensor_tensor(hrow[0:PR], xn3[0:PR], cnb_bc[0:PR, None, :].to_broadcast([PR, PT_, C]), ALU.add))
                norm(i, link, 1, lambda t: hrow[0:PR, t, :], lambda t: hn[0:PR, t, :], PR, PT_, 4).then_inc(W["hn"], 1)
                yield
                yield
                yield
                dve.wait_ge(W["dist"], i + 1)
                link(vv.tensor_scalar(d2[0:PR].rearrange("p t m -> p (t m)"), ps[0:PR, 4, 0:PT_ * NP], 0.0, None, ALU.max))
                link(vv.tensor_reduce(dmin[0:PR], d2[0:PR], AX.X, ALU.min))
                vv.tensor_scalar(dbias[0:PR], dmin[0:PR], lam[0:PR, 2:3], None, ALU.mult).then_inc(W["dclip"], 1)
                yield
                dve.wait_ge(W["e2x"], i + 1)
                link(vv.reciprocal(rr2[0:PR], rs2[0:PR]))
                yield
                dve.wait_ge(W["av2"], i + 1)
                for t in range(PT_):
                    last = vv.scalar_tensor_tensor(h2[0:PR, t, :], ps[0:PR, 4, C * t:C * t + C], rr2[0:PR, t:t + 1],
                                                   hrow[0:PR, t, :], ALU.mult, ALU.add)
                link(last)
                norm(i, link, 1, lambda t: h2[0:PR, t, :], lambda t: xn4[0:PR, t, :], PR, PT_, 5).then_inc(W["xn4"], 1)
                yield
                yield
                dve.wait_ge(W["router"], i + 1)
                logits = vv.tensor_tensor(lg[0:PR], ps[0:PR, 4, 0:PT_ * E].rearrange("p (t e) -> p t e", t=PT_),
                                          br_bc[0:PR, None, :].to_broadcast([PR, PT_, E]), ALU.add)
                link(logits, alone=True)
                for t in range(PT_):
                    last = vv.max(m8[0:PR, t, :], lg[0:PR, t, :])
                link(last)
                vv.tensor_scalar(nm1[0:PR], m8[0:PR, :, 0], -1.0, None, ALU.mult).then_inc(W["lg"], 1)
                for t in range(PT_):
                    last = vv.max_index(i8[0:PR, t, :], m8[0:PR, t, :], lg[0:PR, t, :])
                link(last)
                link(vv.tensor_copy(i8f[0:PR], i8[0:PR]))
                dve.wait_ge(W["elg"], i + 1)
                link(vv.reciprocal(rre[0:PR], rse[0:PR]))
                link(vv.tensor_tensor(p12[0:PR], e12[0:PR], rre[0:PR, :, None].to_broadcast([PR, PT_, 2]), ALU.mult))
                for t in range(PT_):
                    vv.tensor_scalar(gateA[0:PR, t, :], kc[0:PR, K_E8:K_E8 + E], i8f[0:PR, t, 0:1], p12[0:PR, t, 0:1],
                                     ALU.is_equal, ALU.mult)
                    last = vv.tensor_scalar(gateB[0:PR, t, :], kc[0:PR, K_E8:K_E8 + E], i8f[0:PR, t, 1:2], p12[0:PR, t, 1:2],
                                            ALU.is_equal, ALU.mult)
                link(last)
                vv.tensor_tensor(gate[0:PR], gateB[0:PR], gateA[0:PR], ALU.add).then_inc(W["gate"], 1)
                yield
                yield
                yield
                if later(i):
                    dve.wait_ge(W["h2_kept"], i)
                    if not isinstance(i, int) or i >= 2:
                        dve.wait_ge(W["out_stored"], 16 * (i - 1))
                    vv.tensor_copy(ostage[0:PR], h2_m[0:PR]).then_inc(W["h2_held"], 1)
                    dve.wait_ge(W["h2_held"], i)
                vv.tensor_copy(h2_m[0:PR], h2[0:PR]).then_inc(W["h2_kept"], 1)
                assert k[0] == CK, ("CK", k[0])
                yield

            def finish(b):
                dve.wait_ge(W["out_turned"], b + 1)
                dve.wait_ge(W["h2_held"], b + 1)
                vv.tensor_tensor(ostage[0:PR].rearrange("p t c -> p (t c)"), ps[0:PR, 5, 256:256 + PT_ * C],
                                 ostage[0:PR].rearrange("p t c -> p (t c)"), ALU.add).then_inc(W["out_ready"], 1)

            def experts(b):
                if later(b):
                    finish(b - 1)
                yield

            all_batches(dve, attend, rest, experts)
            dve.wait_ge(W["h2_kept"], B)
            dve.wait_ge(W["out_stored"], 16 * (B - 1))
            vv.tensor_copy(ostage[0:PR], h2_m[0:PR]).then_inc(W["h2_held"], 1)
            finish(B - 1)


def kernel(**inputs):
    import numpy as _np
    import concourse.bacc as _bacc
    from concourse import mybir as _mybir
    from concourse.bass_utils import run_bass_kernel_spmd as _run

    w = {k.split("_", 1)[1]: _np.asarray(v) for k, v in inputs.items() if k != "x"}
    tok = {k[4:]: v for k, v in w.items() if k.startswith("tok_")}
    att = {k[5:]: v for k, v in w.items() if k.startswith("attn_")}
    moe = {k[4:]: v for k, v in w.items() if k.startswith("ffn_")}
    laid = {
        "x": _np.asarray(inputs["x"]),
        "consts": shape_constants(),
        "qkv_w": tok["qkv_w"],
        "qkv_b": tok["qkv_b"].reshape(1, -1),
        "qk_bT": tok["qkv_b"][:2 * C].reshape(2, C).T,
        "out_w": tok["out_w"],
        "out_b": tok["out_b"].reshape(1, -1),
        "ffn_w1": tok["ffn_w1"],
        "ffn_b1": tok["ffn_b1"].reshape(NF, 128).T,
        "ffn_w2": tok["ffn_w2"],
        "vecs": _np.stack([tok[n] for n in ("ffn_b2", "n1_g", "n1_b", "n2_g", "n2_b", "conv_b")], axis=1),
        "conv_w": tok["conv_w"].transpose(1, 2, 0),
        "cn_g": tok["cn_g"].reshape(1, -1),
        "cn_b": tok["cn_b"].reshape(1, -1),
        "WqT": att["Wq"].T,
        "WkT": att["Wk"].T,
        "WvT": att["Wv"].T,
        "log_lambda": att["log_lambda"].reshape(1, 1),
        "Wr": moe["Wr"],
        "br": moe["br"].reshape(1, -1),
        "W1": moe["W1"],
        "mb1": moe["b1"].reshape(E * NF, 128).T,
        "W2": moe["W2"],
        "b2": moe["b2"],
    }
    nc = _bacc.Bacc("TRN2", target_bir_lowering=False, num_devices=1)
    arrays, aps = {}, {}
    for name, value in laid.items():
        value = _np.ascontiguousarray(value)
        arrays[f"in_{name}"] = value
        aps[name] = nc.dram_tensor(f"in_{name}", value.shape, _mybir.dt.from_np(value.dtype), kind="ExternalInput").ap()
    out = nc.dram_tensor("out_0", (B, NP, C), _mybir.dt.float32, kind="ExternalOutput").ap()
    audio_tower(nc, aps, out)
    r = _run(nc, [arrays], core_ids=[0])
    return r.results[0]["out_0"]
```

```python
from contextlib import ExitStack

import concourse.bass as bass
import numpy as np
from concourse import mybir

ALU = mybir.AluOpType
ACT = mybir.ActivationFunctionType
AX = mybir.AxisListType
F32 = mybir.dt.float32
BF16 = mybir.dt.bfloat16
F32R = mybir.dt.float32r
U32 = mybir.dt.uint32

B, N, C = 32, 375, 128
CF, CK = 8, 20
ORDER = "KM KPM KF KM KMMFM KF KMMM KFM KM KFM KFM K KGMG K Q K M G KMM KK"
H, DK = 8, 16
TOP = max(1, min(int(N * 0.25), N - 1))
S = 96
NE = N + 1
Q_PART = (0, 0, 0, 1, 1, 2)
K_PART = (0, 1, 2, 0, 1, 0)
NC6 = len(Q_PART)
NT, TP = 3, 125
FF = 512
NF = FF // 128
NP = (N + 1) // 2
PT_, PR = 2, 94
D2 = 64
E = 8
VW = DK + 1
VPAD = 7 * VW + S
OW = 8 * (C + DK)
EPS = 1e-5
BIG = 3.0e38
SELF_SLOT = S - 1

K_ID, K_BM, K_TOK, K_ROW, K_M, K_E8, K_END = 0, 128, 896, 900, 1276, 1278, 1286


def later(b):
    return not (isinstance(b, int) and b == 0)


def pipeline(pick=None, split=None, head=None, tail=None, rest=None, experts=None):
    streams = {"P": pick, "Q": split, "G": head, "F": tail, "K": rest, "M": experts}
    for step in ORDER.replace(" ", ""):
        if streams[step]:
            next(streams[step], None)


def all_batches(eng, pick, split, head, tail, rest, experts, second=None, chosen=None):
    pipeline(pick(0), split(0), head(0))
    pipeline(pick(1), split(1), head(1), tail(0), None, second)
    if chosen:
        chosen()
    pipeline(pick(2), split(2), head(2), tail(1), rest(0))
    pipeline(pick(3), split(3), head(3), tail(2), rest(1), experts(0))
    with eng.Fori(2, B - 2) as i:
        pipeline(pick(i + 2), split(i + 2), head(i + 2), tail(i + 1), rest(i), experts(i - 1))
    pipeline(None, None, None, tail(B - 1), rest(B - 2), experts(B - 3))
    pipeline(None, None, None, None, rest(B - 1), experts(B - 2))
    pipeline(None, None, None, None, None, experts(B - 1))


def no_steps(b):
    return iter(())


def shape_constants():
    k = np.zeros((128, K_END), np.float32)
    p = np.arange(128)
    k[:, K_ID:K_ID + 128] = np.eye(128)
    k[:, K_BM:K_BM + 768] = (p[:, None] // DK == np.arange(768)[None] // S)
    k[:, K_TOK:K_TOK + 3] = p[:, None] + TP * np.arange(3)[None]
    k[:, K_ROW:K_ROW + NE] = np.arange(NE)[None]
    k[:, K_M] = p == SELF_SLOT
    k[:, K_M + 1] = p != SELF_SLOT
    k[:, K_E8:K_E8 + 8] = np.arange(8)[None]
    return k


def audio_tower(nc, a, out):
    with ExitStack() as ctx:
        def sb(name, shape, dt=F32):
            return ctx.enter_context(nc.sbuf_tensor(name, shape, dt))

        def sem(name):
            return ctx.enter_context(nc.semaphore(name))

        idx_dram = nc.dram_tensor("top_idx_scratch", [2 * 128, S], F32, kind="Internal").ap()
        part_dram = nc.dram_tensor("qk_parts_scratch", [B, 6, C, NE], BF16, kind="Internal").ap()
        gate_dram = nc.dram_tensor("gate_scratch", [B, E * NP], F32, kind="Internal").ap()
        max_dram = nc.dram_tensor("top_max_scratch", [2 * 128, S], F32, kind="Internal").ap()

        kc = sb("shape_consts", [128, K_END])
        ident = kc[:, K_ID:K_ID + 128]
        wqkv = sb("wqkv", [128, 3 * C])
        bqkT = sb("bqkT", [128, 2])
        bqv_bc = sb("bqv_bc", [128, 2 * C])
        wo = sb("wo", [128, C])
        bo_bc = sb("bo_bc", [128, C])
        w1 = sb("w1", [128, FF])
        b1 = sb("b1", [128, NF])
        w2 = sb("w2", [128, NF, C])
        vecs = sb("vecs", [128, 6])
        cw = sb("conv_w", [128, 3, C])
        cng_bc = sb("cng_bc", [128, C])
        cnb_bc = sb("cnb_bc", [128, C])
        wqq = sb("wqq", [128, 2 * D2])
        wkk = sb("wkk", [128, 2 * D2])
        wv2 = sb("wv2", [128, C])
        lam = sb("lam", [128, 4])
        euler = sb("euler", [128, 1])
        wr = sb("wr", [128, E])
        br_bc = sb("br_bc", [128, E])
        mw1 = sb("mw1", [128, E, FF])
        mb1 = sb("mb1", [128, E * NF])
        mw2 = sb("mw2", [128, E, NF, C])
        mb2 = sb("mb2", [E, C])
        mean_w = sb("mean_w", [128, S])
        ones_f = sb("ones_f", [128, PR])
        mhalf = sb("mhalf", [128, NT])

        maxes = sb("maxes", [128, NT, B * H])
        xa = sb("xa", [128, NT, C])
        xTa = sb("xTa", [128, N])
        qTa = sb("qTa", [128, N])
        kTa = sb("kTa", [128, N])
        kca = sb("kca", [128, N])
        ksum = sb("ksum", [128, 2])
        rem = [sb(f"rem{u}", [128, N]) for u in range(2)]
        parts = [sb(f"parts{u}", [128, 3, NE], BF16) for u in range(2)]
        gate_bc = sb("gate_bc", [128, E, NP])
        qstack = [gate_bc[0:NC6 * DK].bitcast(BF16), sb("qstack1", [NC6 * DK, H, NE], BF16)]
        kstack = [sb(f"kstack{u}", [NC6 * DK, H, NE], BF16) for u in range(2)]
        mrow = sb("mrow", [128, N])
        mwork = sb("mwork", [128, N])
        top_v = sb("top_v", [128, S])
        top_i = sb("top_i", [128, S], U32)
        top_if = sb("top_if", [128, S])
        top_r = sb("top_r", [128, S])
        idx_col = sb("idx_col", [S, B * H])

        x = sb("x", [128, NT, C])
        xb = sb("xb", [128, NT, C])
        idx_bc = sb("idx_bc", [128, H * S])
        xT = sb("xT", [128, N])
        kT = sb("kT", [128, N])
        kTc = [sb(f"kTc{u}", [128, N]) for u in range(2)]
        xsum = sb("xsum", [128, 1])
        xmean = sb("xmean", [128, S])
        ksum_b = sb("ksum_b", [128, 2])
        qrow = sb("qrow", [128, NT, C])
        q_hi = sb("q_hi", [128, NT, C], F32R)
        q_lo = sb("q_lo", [128, NT, C], F32R)
        v = sb("v", [128, NT, VPAD + 1])
        pick = sb("pick", [128, NT, H * S], F32R)
        place = sb("place", [S, H, NE], F32R)
        qsel = sb("qsel", [128, H * S])
        ex = sb("ex", [128, NT, H * S])
        rden = sb("rden", [S, H])
        onorm = sb("onorm", [S, H, DK])
        vmw = sb("vmw", [S, H, DK])
        on_all = sb("on_all", [S, H, DK])
        vrow = sb("vrow", [S, C])
        self_row = sb("self_row", [S, C])
        opad = [sb(f"opad{u}", [S, OW], F32R) for u in range(2)]
        attnT = sb("attnT", [128, N])
        r1 = sb("r1", [128, NT, C])
        st = [sb(f"st{u}", [128, NT, 6]) for u in range(2)]
        mv = [sb(f"mv{u}", [128, NT, 2]) for u in range(2)]
        veps = [sb(f"veps{u}", [128, NT]) for u in range(2)]
        rstd = [sb(f"rstd{u}", [128, NT]) for u in range(2)]
        xn = sb("xn", [128, NT, C])
        x1T = sb("x1T", [128, N])
        hT = sb("hT", [128, NF, N])
        yT = sb("yT", [128, N])
        xn2 = sb("xn2", [128, NT, C])
        x2p = sb("x2p", [128, N + 2])
        cp = sb("cp", [128, N + 2])
        mx = sb("mx", [128, NP])
        emn = sb("emn", [128, NP])
        el = sb("el", [128, NP])
        xn3 = sb("xn3", [128, PT_, C])
        hrow = sb("hrow", [128, PT_, C])
        hn = sb("hn", [128, PT_, C])
        hnT = sb("hnT", [128, NP])
        qa = sb("qa", [128, NP])
        ka = sb("ka", [128, NP])
        kk = sb("kk", [128, NP])
        v2 = sb("v2", [128, PT_, C])
        d2 = sb("d2", [128, PT_, NP])
        dmin = sb("dmin", [128, PT_])
        dbias = sb("dbias", [128, PT_])
        e2 = sb("e2", [128, PT_, NP])
        rs2 = sb("rs2", [128, PT_])
        rr2 = sb("rr2", [128, PT_])
        e2T = sb("e2T", [128, PT_, NP])
        h2 = sb("h2", [128, PT_, C])
        xn4 = sb("xn4", [128, PT_, C])
        lg = sb("lg", [128, PT_, E])
        m8 = sb("m8", [128, PT_, 8])
        i8 = sb("i8", [128, PT_, 8], U32)
        i8f = sb("i8f", [128, PT_, 8])
        lgd = sb("lgd", [128, PT_, E + 2])
        elg = sb("elg", [128, PT_, E + 2])
        rse = sb("rse", [128, PT_])
        rre = sb("rre", [128, PT_])
        p12 = sb("p12", [128, PT_, 2])
        h2nT = sb("h2nT", [128, NP])
        gate = sb("gate", [128, PT_, E])
        gateB = sb("gateB", [128, PT_, E])
        gateA = sb("gateA", [128, PT_, E])
        gateT = sb("gateT", [E, NP])
        h2nT_m = sb("h2nT_m", [128, NP])
        h2_m = sb("h2_m", [128, PT_, C])
        moeT = sb("moeT", [128, NP])
        unused = sb("unused", [128, 2])
        mh = [sb(f"mh{u}", [128, NF, NP]) for u in range(2)]
        ostage = sb("ostage", [128, PT_, C])

        ps = ctx.enter_context(nc.psum_tensor("ps", [128, 8, 512], F32))

        s_w0 = sem("s_weights_of_phase_A_loaded")
        s_w = sem("s_weights_loaded")
        s_set = sem("s_constants_set")
        s_lam = sem("s_lambda")
        s_alone = sem("s_carries_a_wait")
        s_e = sem("s_euler")
        A = {n: sem("A_" + n) for n in (
            "x_loaded x_turned xT k_proj kT_ready q_proj qT_ready mean_ready kc_ready q1 q2 k1 k2 qrem krem q3 k3 "
            "q_out k_out stacked0 stacked1 scores maxed".split())}
        T = {n: sem("T_" + n) for n in "turned rows idx_ready idx_turned idx_col stored chain".split()}
        names = ("x_loaded idx_loaded nm_loaded x_turned xT k_proj kT kTc qv_proj q_rows q_hi q_lo v_rows pick place gathered qsel "
                 "s0 s1 s2 e0 e1 e2 av vmean on scattered attnT oproj xb aggr1 rstd1 xn1 x1_turned x1T "
                 "f0 f1 f2 f3 g0 g1 g2 g3 ffn2 yT y_turned aggr2 rstd2 xn2 x2_turned x2T x2_edges conv cp mx emn el "
                 "el_turned aggr3 rstd3 hrow aggr4 rstd4 hn hn_turned hnT qk_proj v2_proj qa ka v2 dist dclip e2x e2_turned e2T "
                 "av2 h2 aggr5 rstd5 xn4 h2n_turned h2nT router lg elg gate gate_turned gateT bias2 gate_out gates0 gates1 h2_kept h2_held moeT out_turned "
                 "r1 kmean xmean veps1 veps2 veps3 veps4 veps5 h2nT_m out_ready out_stored").split()
        Bs = {n: sem("B_" + n) for n in names}
        m_h = [sem("M_hidden01"), sem("M_hidden23")]
        m_relu = sem("M_relu")
        m_y = sem("M_y")
        m_gated = sem("M_gated")
        chain_f = sem("dve_chain_attention")
        chain_k = sem("dve_chain_rest")

        loads = [
            (kc[:], a["consts"]), (wqkv[:], a["qkv_w"]), (bqkT[:], a["qk_bT"]),
            (lam[:, 0:1], a["log_lambda"].to_broadcast([128, 1])),
            (bqv_bc[:, 0:C], a["qkv_b"][:, 0:C].to_broadcast([128, C])),
            (bqv_bc[:, C:2 * C], a["qkv_b"][:, 2 * C:3 * C].to_broadcast([128, C])),
            (wo[:], a["out_w"]), (bo_bc[:], a["out_b"].to_broadcast([128, C])),
            (w1[:], a["ffn_w1"]), (b1[:], a["ffn_b1"]),
            (w2[:], a["ffn_w2"].rearrange("(f p) c -> p f c", p=128)), (vecs[:], a["vecs"]),
            (cw[:], a["conv_w"]),
            (cng_bc[:], a["cn_g"].to_broadcast([128, C])), (cnb_bc[:], a["cn_b"].to_broadcast([128, C])),
            (wqq[:, 0:D2], a["WqT"]), (wqq[:, D2:], a["WqT"]), (wkk[:, 0:D2], a["WkT"]), (wkk[:, D2:], a["WkT"]),
            (wv2[:], a["WvT"]),
            (wr[:], a["Wr"]), (br_bc[:], a["br"].to_broadcast([128, E])),
            (mw1[:], a["W1"].rearrange("e p f -> p e f")), (mb1[:], a["mb1"]),
            (mw2[:], a["W2"].rearrange("e (f p) c -> p e f c", p=128)), (mb2[:], a["b2"]),
        ]
        EARLY = 4
        NSET = 17
        xd = a["x"].rearrange("b (t p) c -> b p t c", p=TP)
        od = out.rearrange("b (t p) c -> b p t c", p=PR)

        block = ctx.enter_context(nc.Block())

        @block.sync
        def _(sp):
            for dst, src in loads[:EARLY]:
                sp.dma_start(dst, src).then_inc(s_w0, 16)

            def x_load(b):
                if later(b):
                    sp.wait_ge(A["x_turned"], b)
                    sp.sem_inc(s_alone, 1)
                sp.dma_start(xa[0:TP], xd[bass.ds(b, 1)].rearrange("b p t c -> (b p) t c")).then_inc(A["x_loaded"], 16)

            def parts_out(b):
                for u, n in ((0, "q"), (1, "k")):
                    sp.wait_ge(A[n + "3"], b + 1)
                    sp.sem_inc(s_alone, 1)
                    sp.dma_start(part_dram[bass.ds(b, 1), 3 * u:3 * u + 3].rearrange("b k p n -> p (b k) n"),
                                 parts[u][:]).then_inc(A[n + "_out"], 16)

            def stack_in(b, u):
                if not isinstance(b, int) or b >= 2:
                    sp.wait_ge(A["scores"], 8 * (b - 1))
                    sp.sem_inc(s_alone, 1)
                sp.wait_ge(A["q_out"], 16 * (b + 1))
                sp.wait_ge(A["k_out"], 16 * (b + 1))
                sp.sem_inc(s_alone, 1)
                for stack, which, base in ((qstack, Q_PART, 0), (kstack, K_PART, 3)):
                    for c in range(NC6):
                        sp.dma_start(stack[u][DK * c:DK * c + DK],
                                     part_dram[bass.ds(b, 1), base + which[c]].rearrange("b (h d) n -> (b d) h n", d=DK)
                                     ).then_inc(A[f"stacked{u}"], 16)

            x_load(0)
            x_load(1)
            parts_out(0)
            x_load(2)
            parts_out(1)
            stack_in(0, 0)
            for b in range(2):
                stack_in(b + 1, (b + 1) % 2)
                x_load(b + 3)
                parts_out(b + 2)
            with sp.Fori(1, B // 2 - 2) as j:
                for u in range(2):
                    stack_in(2 * j + 1 + u, 1 - u)
                    x_load(2 * j + 3 + u)
                    parts_out(2 * j + 2 + u)
            for b in range(B - 4, B - 1):
                stack_in(b + 1, (b + 1) % 2)
                if b + 3 < B:
                    x_load(b + 3)
                if b + 2 < B:
                    parts_out(b + 2)
            for dst, src in loads[EARLY:]:
                sp.dma_start(dst, src).then_inc(s_w, 16)

            def chosen_out(g):
                sp.wait_ge(T["idx_ready"], g + 1)
                sp.dma_start(idx_dram[128 * g:128 * g + 128], top_if[:]).then_inc(T["stored"], 16)
                sp.dma_start(max_dram[128 * g:128 * g + 128], top_r[:]).then_inc(T["stored"], 16)
                sp.wait_ge(T["stored"], 2 * 16 * (g + 1))

            chosen_out(0)
            idx_flat = idx_dram.rearrange("(b h) s -> b (h s)", h=H)
            max_flat = max_dram.rearrange("(b h) s -> b (h s)", h=H)

            def batch_loads(i):
                if later(i):
                    sp.wait_ge(s_set, NSET)
                    sp.wait_ge(Bs["pick"], i)
                sp.dma_start(idx_bc[0:TP], idx_flat[bass.ds(i, 1)].to_broadcast([TP, H * S])).then_inc(Bs["idx_loaded"], 16)
                if later(i):
                    sp.wait_ge(s_set, NSET)
                    sp.wait_ge(Bs["xb"], i)
                    sp.wait_ge(Bs["x_turned"], i)
                sp.dma_start(x[0:TP], xd[bass.ds(i, 1)].rearrange("b p t c -> (b p) t c")).then_inc(Bs["x_loaded"], 16)
                if later(i):
                    sp.wait_ge(s_set, NSET)
                    sp.wait_ge(Bs["s2"], i)
                for half, row in ((0, 64), (1, 0)):
                    sp.dma_start(qsel[row:row + 1, 384 * half:384 * half + 384],
                                 max_flat[bass.ds(i, 1), 384 * half:384 * half + 384]).then_inc(Bs["nm_loaded"], 16)

            def gates_move(i):
                sp.wait_ge(Bs["gateT"], i + 1)
                sp.sem_inc(s_alone, 1)
                sp.dma_start(gate_dram[bass.ds(i, 1)].rearrange("b (e n) -> (b e) n", e=E), gateT[:]).then_inc(Bs["gate_out"], 16)
                sp.wait_ge(Bs["gate_out"], 16 * (i + 1))
                sp.sem_inc(s_alone, 1)
                for half in range(2):
                    if later(i):
                        sp.wait_ge(m_gated, E * i - 4 * (1 - half))
                        sp.sem_inc(s_alone, 1)
                    sp.dma_start(gate_bc[:, 4 * half:4 * half + 4].rearrange("p e n -> p (e n)"),
                                 gate_dram[bass.ds(i, 1), 4 * half * NP:4 * (half + 1) * NP].to_broadcast([128, 4 * NP])
                                 ).then_inc(Bs[f"gates{half}"], 16)

            batch_loads(0)
            batch_loads(1)
            batch_loads(2)
            chosen_out(1)
            gates_move(0)
            with sp.Fori(1, B - 2) as i:
                batch_loads(i + 2)
                gates_move(i)
            gates_move(B - 2)
            gates_move(B - 1)
            sp.wait_ge(Bs["out_stored"], 16 * B)

        @block.tensor
        def _(pe):
            mm = nc.tensor.matmul
            tr = nc.tensor.transpose

            def a_project(b):
                pe.wait_ge(A["x_loaded"], 16 * (b + 1))
                if later(b):
                    pe.wait_ge(A["kT_ready"], b)
                for t in range(NT):
                    last = tr(ps[:, 6, TP * t:TP * t + TP], xa[0:TP, t, :], ident[0:TP, 0:TP])
                last.then_inc(A["x_turned"], 1)
                yield
                pe.wait_ge(A["xT"], b + 1)
                mm(ps[:, 6, 0:N], wqkv[:, C:2 * C], xTa[:], start=True, stop=True).then_inc(A["k_proj"], 1)
                yield
                if later(b):
                    pe.wait_ge(A["qT_ready"], b)
                mm(ps[:, 7, 0:N], wqkv[:, 0:C], xTa[:], start=True, stop=True).then_inc(A["q_proj"], 1)
                yield

            def a_scores(b, u, ahead=None):
                pe.wait_ge(A[f"stacked{u}"], 16 * NC6 * (b - u + 2))
                for n in range(H):
                    if later(b) or n >= 2:
                        pe.wait_ge(A["maxed"], 8 * b + n - 1)
                    for t in range(NT):
                        last = mm(ps[0:TP, 3 * (n % 2) + t, 0:N], qstack[u][:, n, TP * t:TP * t + TP],
                                  kstack[u][:, n, 0:N], start=True, stop=True)
                    last.then_inc(A["scores"], 1)
                    if ahead and n in (0, 1, 2):
                        next(ahead)

            pe.wait_ge(s_w0, 16 * EARLY)
            pe.wait_ge(s_set, NSET)
            for b in range(2):
                for _ in a_project(b):
                    pass
            for b in range(2):
                a_scores(b, b, a_project(b + 2))
            with pe.Fori(1, B // 2 - 1) as j:
                for u in range(2):
                    a_scores(2 * j + u, u, a_project(2 * j + u + 2))
            a_scores(B - 2, 0)
            a_scores(B - 1, 1)

            for g in range(2):
                pe.wait_ge(A["maxed"], 8 * B)
                if g:
                    pe.wait_ge(T["rows"], 1)
                else:
                    pe.wait_ge(A["kT_ready"], B)
                for t in range(NT):
                    last = tr(ps[:, 6, TP * t:TP * t + TP], maxes[0:TP, t, 128 * g:128 * g + 128], ident[0:TP, 0:TP])
                last.then_inc(T["turned"], 1)

            def columns(g):
                pe.wait_ge(T["idx_ready"], g + 1)
                if g:
                    pe.wait_ge(T["idx_col"], 1)
                tr(ps[0:S, 7, 0:128], top_if[:], ident).then_inc(T["idx_turned"], 1)

            columns(0)
            pe.wait_ge(T["idx_col"], 1)
            pe.wait_ge(s_w, 16 * (len(loads) - EARLY))

            W = Bs

            def head(b):
                pe.wait_ge(W["x_loaded"], 16 * (b + 1))
                if later(b):
                    pe.wait_ge(W["attnT"], b)
                for t in range(NT):
                    last = tr(ps[:, 2, TP * t:TP * t + TP], x[0:TP, t, :], ident[0:TP, 0:TP])
                last.then_inc(W["x_turned"], 1)
                yield
                if later(b):
                    pe.wait_ge(W["r1"], b)
                pe.wait_ge(W["xT"], b + 1)
                mm(ps[:, 2, 0:N], wqkv[:, C:2 * C], xT[:], start=True, stop=True).then_inc(W["k_proj"], 1)
                for t in range(NT):
                    for k, w in ((0, wqkv[:, 0:C]), (1, wqkv[:, 2 * C:3 * C])):
                        last = mm(ps[0:TP, t // 2, 256 * (t % 2) + 128 * k:256 * (t % 2) + 128 * k + 128],
                                  xT[:, TP * t:TP * t + TP], w, start=True, stop=True)
                last.then_inc(W["qv_proj"], 1)
                yield
                pe.wait_ge(W["q_hi"], b + 1)
                pe.wait_ge(W["q_lo"], b + 1)
                pe.wait_ge(W["v_rows"], b + 1)
                pe.wait_ge(W["pick"], b + 1)
                for half in range(2):
                    for t in range(NT):
                        for part, q in enumerate((q_hi, q_lo)):
                            last = mm(ps[:, half, 0:384], q[0:TP, t, :], pick[0:TP, t, 384 * half:384 * half + 384],
                                      start=(t == 0 and part == 0), stop=(t == NT - 1 and part == 1))
                last.then_inc(W["gathered"], 1)
                yield

            def tail(b):
                pe.wait_ge(W["qsel"], b + 1)
                pe.wait_ge(W["kTc"], b + 1)
                pe.wait_ge(W["nm_loaded"], 32 * (b + 1))
                for t in range(NT):
                    if t:
                        pe.wait_ge(W[f"e{t - 1}"], b + 1)
                    for half in range(2):
                        bank = ps[0:TP, half, 0:384]
                        last = mm(bank, kTc[half][:, TP * t:TP * t + TP], qsel[:, 384 * half:384 * half + 384], start=True, stop=True)
                    last.then_inc(W[f"s{t}"], 1)
                    if t == 0:
                        pe.wait_ge(W["xmean"], b + 1)
                        mm(ps[0:S, 2, 0:C], xmean[:], wqkv[:, 2 * C:3 * C], start=True, stop=True).then_inc(W["vmean"], 1)
                    yield
                pe.wait_ge(W["e2"], b + 1)
                for h in range(H):
                    for t in range(NT):
                        last = mm(ps[0:S, h // 4, S * (h % 4):S * (h % 4) + S], ex[0:TP, t, S * h:S * h + S],
                                  v[0:TP, t, VW * h:VW * h + S], start=(t == 0), stop=(t == NT - 1))
                last.then_inc(W["av"], 1)
                yield
                pe.wait_ge(W["on"], b + 1)
                pe.wait_ge(W["place"], b + 1)
                for h in range(H):
                    for part in range(2):
                        last = mm(ps[:, 2, 0:NE], opad[part][:, C * h:C * h + C], place[:, h, :],
                                  start=(h == 0 and part == 0), stop=(h == H - 1 and part == 1))
                last.then_inc(W["scattered"], 1)
                yield
                pe.wait_ge(W["attnT"], b + 1)
                for t in range(NT):
                    last = mm(ps[0:TP, 0, 128 * t:128 * t + 128], attnT[:, TP * t:TP * t + TP], wo[:], start=True, stop=True)
                last.then_inc(W["oproj"], 1)
                yield

            def rest(i):
                pe.wait_ge(W["xn1"], i + 1)
                if later(i):
                    pe.wait_ge(W["gateT"], i)
                for t in range(NT):
                    last = tr(ps[:, 3, TP * t:TP * t + TP], xn[0:TP, t, :], ident[0:TP, 0:TP])
                last.then_inc(W["x1_turned"], 1)
                yield
                pe.wait_ge(W["x1T"], i + 1)
                for f in range(NF):
                    if f >= 2:
                        pe.wait_ge(W[f"g{f - 2}"], i + 1)
                    mm(ps[:, 4 - f % 2, 0:N], w1[:, 128 * f:128 * f + 128], x1T[:], start=True, stop=True).then_inc(W[f"f{f}"], 1)
                    if f % 2:
                        yield
                for f in range(NF):
                    pe.wait_ge(W[f"g{max(f, 2)}"], i + 1)
                    last = mm(ps[:, 4, 0:N], w2[:, f, :], hT[:, f, :], start=(f == 0), stop=(f == NF - 1))
                last.then_inc(W["ffn2"], 1)
                yield
                pe.wait_ge(W["yT"], i + 1)
                for t in range(NT):
                    last = tr(ps[0:TP, 3, 128 * t:128 * t + 128], yT[:, TP * t:TP * t + TP], ident)
                last.then_inc(W["y_turned"], 1)
                yield
                pe.wait_ge(W["xn2"], i + 1)
                for t in range(NT):
                    last = tr(ps[:, 4, TP * t:TP * t + TP], xn2[0:TP, t, :], ident[0:TP, 0:TP])
                last.then_inc(W["x2_turned"], 1)
                yield
                pe.wait_ge(W["x2T"], i + 1)
                for k in (1, 0, 2):
                    if k == 0:
                        pe.wait_ge(W["x2_edges"], i + 1)
                    last = mm(ps[:, 3, 0:N], cw[:, k, :], x2p[:, k:k + N], start=(k == 1), stop=(k == 2))
                last.then_inc(W["conv"], 1)
                yield
                pe.wait_ge(W["el"], i + 1)
                for t in range(PT_):
                    last = tr(ps[0:PR, 4, 128 * t:128 * t + 128], el[:, PR * t:PR * t + PR], ident)
                last.then_inc(W["el_turned"], 1)
                yield
                pe.wait_ge(W["hn"], i + 1)
                for t in range(PT_):
                    last = tr(ps[:, 3, PR * t:PR * t + PR], hn[0:PR, t, :], ident[0:PR, 0:PR])
                last.then_inc(W["hn_turned"], 1)
                yield
                pe.wait_ge(W["hnT"], i + 1)
                mm(ps[:, 4, 0:NP], wqq[:], hnT[:], start=True, stop=True)
                mm(ps[:, 4, 256:256 + NP], wkk[:], hnT[:], start=True, stop=True).then_inc(W["qk_proj"], 1)
                for t in range(PT_):
                    last = mm(ps[0:PR, 3, 128 * t:128 * t + 128], hnT[:, PR * t:PR * t + PR], wv2[:], start=True, stop=True)
                last.then_inc(W["v2_proj"], 1)
                yield
                pe.wait_ge(W["qa"], i + 1)
                pe.wait_ge(W["ka"], i + 1)
                for t in range(PT_):
                    o = ps[0:PR, 4, NP * t:NP * t + NP]
                    mm(o, qa[:, PR * t:PR * t + PR], ka[:], start=True, stop=False)
                    last = mm(o, ones_f[D2:128, :], kk[D2:128, :], start=False, stop=True)
                last.then_inc(W["dist"], 1)
                yield
                pe.wait_ge(W["v2"], i + 1)
                for t in range(PT_):
                    pe.wait_ge(W["e2x"], PT_ * i + t + 1)
                    for m in range(PT_):
                        last = tr(ps[0:PR, 3, NP * m + PR * t:NP * m + PR * t + PR], e2[0:PR, t, PR * m:PR * m + PR],
                                  ident[0:PR, 0:PR])
                last.then_inc(W["e2_turned"], 1)
                yield
                pe.wait_ge(W["e2T"], i + 1)
                for t in range(PT_):
                    for m in range(PT_):
                        last = mm(ps[0:PR, 4, 128 * t:128 * t + 128], e2T[0:PR, m, PR * t:PR * t + PR], v2[0:PR, m, :],
                                  start=(m == 0), stop=(m == PT_ - 1))
                last.then_inc(W["av2"], 1)
                yield
                pe.wait_ge(W["xn4"], i + 1)
                for t in range(PT_):
                    last = tr(ps[:, 3, PR * t:PR * t + PR], xn4[0:PR, t, :], ident[0:PR, 0:PR])
                last.then_inc(W["h2n_turned"], 1)
                yield
                pe.wait_ge(W["h2nT"], i + 1)
                for t in range(PT_):
                    last = mm(ps[0:PR, 4, E * t:E * t + E], h2nT[:, PR * t:PR * t + PR], wr[:], start=True, stop=True)
                last.then_inc(W["router"], 1)
                yield
                pe.wait_ge(W["gate"], i + 1)
                for t in range(PT_):
                    last = tr(ps[0:E, 3, PR * t:PR * t + PR], gate[0:PR, t, :], ident[0:PR, 0:PR])
                last.then_inc(W["gate_turned"], 1)
                yield

            def turn_out(b):
                pe.wait_ge(W["moeT"], b + 1)
                for t in range(PT_):
                    last = tr(ps[0:PR, 5, 256 + C * t:256 + C * t + C], moeT[:, PR * t:PR * t + PR], ident)
                last.then_inc(W["out_turned"], 1)

            def experts(b):
                def hidden(e):
                    if e == 0:
                        pe.wait_ge(W["h2nT_m"], b + 1)
                        if not later(b):
                            pe.wait_ge(T["idx_col"], 2)
                    for half in range(2):
                        if later(b) or e:
                            pe.wait_ge(m_relu, NF * (E * b + e) - 2 * (1 - half))
                        for k in range(2):
                            f = 2 * half + k
                            last = mm(ps[:, 6 + half, 256 * k:256 * k + NP], mw1[:, e, 128 * f:128 * f + 128], h2nT_m[:],
                                      start=True, stop=True)
                        last.then_inc(m_h[half], 1)

                def down(e):
                    if e == 0:
                        pe.wait_ge(W["gateT"], b + 1)
                        if later(b):
                            pe.wait_ge(W["out_ready"], b)
                        mm(ps[:, 5, 0:NP], mb2[:], gateT[:], start=True, stop=False).then_inc(W["bias2"], 1)
                    pe.wait_ge(m_gated, E * b + e + 1)
                    for f in range(NF):
                        last = mm(ps[:, 5, 0:NP], mw2[:, e, f, :], mh[e % 2][:, f, :],
                                  start=False, stop=(e == E - 1 and f == NF - 1))
                    last.then_inc(m_y, 1)

                hidden(0)
                if later(b):
                    turn_out(b - 1)
                yield
                for e in range(E):
                    if e + 1 < E:
                        hidden(e + 1)
                        yield
                    down(e)
                    yield

            all_batches(pe, no_steps, no_steps, head, tail, rest, experts, None, lambda: columns(1))
            turn_out(B - 1)

        @block.scalar
        def _(act):
            fn = nc.scalar.activation
            act.wait_ge(s_w0, 16 * EARLY)
            act.wait_ge(s_set, NSET)

            def a_evac(b):
                act.wait_ge(A["x_turned"], b + 1)
                if later(b):
                    act.wait_ge(A["q_proj"], b)
                fn(xTa[:], ps[:, 6, 0:N], ACT.Copy).then_inc(A["xT"], 1)
                act.wait_ge(A["k_proj"], b + 1)
                if later(b):
                    act.wait_ge(A["kc_ready"], b)
                fn(kTa[:], ps[:, 6, 0:N], ACT.Identity, bias=bqkT[:, 1:2], accum_out=ksum[:, 0:1]).then_inc(A["kT_ready"], 1)
                act.wait_ge(A["q_proj"], b + 1)
                if later(b):
                    act.wait_ge(A["qrem"], b)
                    act.wait_ge(A["q_out"], 16 * b)
                fn(qTa[:], ps[:, 7, 0:N], ACT.Identity, bias=bqkT[:, 0:1])
                fn(parts[0][:, 0, 0:N], ps[:, 7, 0:N], ACT.Identity, bias=bqkT[:, 0:1]).then_inc(A["qT_ready"], 1)
                act.wait_ge(A["mean_ready"], b + 1)
                if later(b):
                    act.wait_ge(A["krem"], b)
                    act.wait_ge(A["k_out"], 16 * b)
                fn(kca[:], kTa[:], ACT.Identity, bias=ksum[:, 1:2])
                fn(parts[1][:, 0, 0:N], kTa[:], ACT.Identity, bias=ksum[:, 1:2]).then_inc(A["kc_ready"], 1)
                for u, n in ((0, "q"), (1, "k")):
                    act.wait_ge(A[n + "rem"], b + 1)
                    fn(parts[u][:, 1, 0:N], rem[u][:], ACT.Copy).then_inc(A[n + "2"], 1)

            a_evac(0)
            with act.Fori(1, B) as b:
                a_evac(b)
            act.wait_ge(s_w, 16 * (len(loads) - EARLY))

            W = Bs

            def table_ahead(k, f):
                fn(unused[:, k:k + 1], kc[:, K_ID:K_ID + 1], f)

            def q_split(b):
                act.wait_ge(W["q_rows"], b + 1)
                fn(q_hi[0:TP], qrow[0:TP], ACT.Copy).then_inc(W["q_hi"], 1)
                yield

            def head(b):
                act.wait_ge(W["x_turned"], b + 1)
                fn(xT[:], ps[:, 2, 0:N], ACT.Identity, accum_out=xsum[:]).then_inc(W["xT"], 1)
                yield
                act.wait_ge(W["k_proj"], b + 1)
                fn(kT[:], ps[:, 2, 0:N], ACT.Identity, bias=bqkT[:, 1:2], accum_out=ksum_b[:, 0:1]).then_inc(W["kT"], 1)
                yield

            def tail(b):
                for t in range(NT):
                    act.wait_ge(W[f"s{t}"], b + 1)
                    fn(ex[0:TP, t, :].rearrange("p (a s) -> p a s", a=2), ps[0:TP, 0:2, 0:384],
                       ACT.Exp, scale=1.0 / float(np.sqrt(DK))).then_inc(W[f"e{t}"], 1)
                    yield
                yield
                act.wait_ge(W["scattered"], b + 1)
                fn(attnT[:], ps[:, 2, 0:N], ACT.Copy).then_inc(W["attnT"], 1)
                yield

            def rest(i):
                act.wait_ge(W["x1_turned"], i + 1)
                fn(x1T[:], ps[:, 3, 0:N], ACT.Identity, bias=vecs[:, 2:3], scale=vecs[:, 1:2]).then_inc(W["x1T"], 1)
                yield
                for f in range(NF):
                    act.wait_ge(W[f"f{f}"], i + 1)
                    fn(hT[:, f, :], ps[:, 4 - f % 2, 0:N], ACT.Gelu, bias=b1[:, f:f + 1]).then_inc(W[f"g{f}"], 1)
                    if f % 2:
                        yield
                table_ahead(1, ACT.Exp)
                yield
                yield
                act.wait_ge(W["x2_turned"], i + 1)
                fn(x2p[:, 1:N + 1], ps[:, 4, 0:N], ACT.Identity, bias=vecs[:, 4:5], scale=vecs[:, 3:4]).then_inc(W["x2T"], 1)
                fn(x2p[:, 0:1], ps[:, 4, N - 1:N], ACT.Identity, bias=vecs[:, 4:5], scale=vecs[:, 3:4])
                fn(x2p[:, N + 1:N + 2], ps[:, 4, 0:1], ACT.Identity, bias=vecs[:, 4:5], scale=vecs[:, 3:4]).then_inc(W["x2_edges"], 1)
                yield
                act.wait_ge(W["conv"], i + 1)
                fn(cp[:, 1:N + 1], ps[:, 3, 0:N], ACT.Identity, bias=vecs[:, 5:6]).then_inc(W["cp"], 1)
                act.wait_ge(W["mx"], i + 1)
                fn(emn[:], el[:], ACT.Exp).then_inc(W["emn"], 1)
                yield
                yield
                act.wait_ge(W["hn_turned"], i + 1)
                fn(hnT[:], ps[:, 3, 0:NP], ACT.Copy).then_inc(W["hnT"], 1)
                yield
                act.wait_ge(W["qk_proj"], i + 1)
                fn(qa[0:D2, :], ps[0:D2, 4, 0:NP], ACT.Copy)
                fn(qa[D2:128, :], ps[D2:128, 4, 0:NP], ACT.Square).then_inc(W["qa"], 1)
                fn(ka[0:D2, :], ps[0:D2, 4, 256:256 + NP], ACT.Copy, scale=-2.0)
                fn(kk[D2:128, :], ps[D2:128, 4, 256:256 + NP], ACT.Square).then_inc(W["ka"], 1)
                act.wait_ge(W["v2_proj"], i + 1)
                fn(v2[0:PR], ps[0:PR, 3, 0:256].rearrange("p (t c) -> p t c", t=PT_), ACT.Copy).then_inc(W["v2"], 1)
                yield
                act.wait_ge(W["dclip"], i + 1)
                for t in range(PT_):
                    last = fn(e2[0:PR, t, :], d2[0:PR, t, :], ACT.Exp, scale=lam[0:PR, 3:4], bias=dbias[0:PR, t:t + 1],
                              accum_out=rs2[0:PR, t:t + 1])
                    last.then_inc(W["e2x"], 1)
                yield
                act.wait_ge(W["e2_turned"], i + 1)
                fn(e2T[0:PR].rearrange("p m n -> p (m n)"), ps[0:PR, 3, 0:PT_ * NP], ACT.Copy).then_inc(W["e2T"], 1)
                yield
                yield
                act.wait_ge(W["h2n_turned"], i + 1)
                if later(i):
                    act.wait_ge(W["h2nT_m"], i)
                fn(h2nT[:], ps[:, 3, 0:NP], ACT.Copy).then_inc(W["h2nT"], 1)
                yield
                act.wait_ge(W["lg"], i + 1)
                fn(elg[0:PR], lgd[0:PR], ACT.Exp).then_inc(W["elg"], 1)
                yield
                table_ahead(0, ACT.Gelu)
                act.wait_ge(W["gate_turned"], i + 1)
                if later(i):
                    act.wait_ge(W["bias2"], i)
                    act.wait_ge(W["gate_out"], 16 * i)
                fn(gateT[:], ps[0:E, 3, 0:NP], ACT.Copy).then_inc(W["gateT"], 1)
                yield

            def store(b):
                act.wait_ge(W["out_ready"], b + 1)
                act.dma_start(od[bass.ds(b, 1)].rearrange("b p t c -> (b p) t c"), ostage[0:PR]).then_inc(W["out_stored"], 16)

            def experts(b):
                def relu(e):
                    if e >= 2:
                        act.wait_ge(m_y, E * b + e - 1)
                    for f in range(NF):
                        if f % 2 == 0:
                            act.wait_ge(m_h[f // 2], E * b + e + 1)
                        fn(mh[e % 2][:, f, :], ps[:, 6 + f // 2, 256 * (f % 2):256 * (f % 2) + NP], ACT.Relu,
                           bias=mb1[:, NF * e + f:NF * e + f + 1]).then_inc(m_relu, 1)

                relu(0)
                if later(b):
                    store(b - 1)
                yield
                for e in range(E):
                    if e + 1 < E:
                        relu(e + 1)
                        yield
                    yield
                act.wait_ge(m_y, E * (b + 1))
                if later(b):
                    act.wait_ge(W["out_turned"], b)
                fn(moeT[:], ps[:, 5, 0:NP], ACT.Copy).then_inc(W["moeT"], 1)
                yield

            all_batches(act, no_steps, q_split, head, tail, rest, experts)
            store(B - 1)

        @block.gpsimd
        def _(pool):
            g = nc.gpsimd
            g.memset(mean_w[:], 1.0 / N).then_inc(s_set, 1)
            for u in range(2):
                g.memset(kTc[u][:], 0.0).then_inc(s_set, 1)
            g.memset(ones_f[:], 1.0).then_inc(s_set, 1)
            g.memset(mhalf[:], -0.5).then_inc(s_set, 1)
            for u in range(2):
                g.memset(parts[u][:], 0.0).then_inc(s_set, 1)
            g.memset(qsel[:], 0.0).then_inc(s_set, 1)
            g.memset(opad[0][:].bitcast(F32), 0.0).then_inc(s_set, 1)
            g.memset(opad[1][:].bitcast(F32), 0.0).then_inc(s_set, 1)
            g.memset(cp[:], -BIG).then_inc(s_set, 1)
            g.memset(ka[:], 1.0).then_inc(s_set, 1)
            g.memset(v[:], 0.0).then_inc(s_set, 1)
            pool.wait_ge(s_set, 13)
            g.memset(kTc[0][64:65, :], 1.0).then_inc(s_set, 1)
            g.memset(kTc[1][0:1, :], 1.0).then_inc(s_set, 1)
            pool.wait_ge(s_set, 15)
            for t in range(NT):
                last = g.memset(v[:, t, 0:H * VW].rearrange("p (h c) -> p h c", c=VW)[:, :, DK:VW], 1.0)
            last.then_inc(s_set, 1)
            g.memset(euler[:], float(np.e)).then_inc(s_e, 1)
            pool.wait_ge(s_w0, 16 * EARLY)
            pool.wait_ge(s_e, 1)
            g.tensor_tensor(lam[:, 1:2], euler[:], lam[:, 0:1], ALU.pow).then_inc(s_lam, 1)

            def split(b):
                for u, n, whole, ready in ((0, "q", qTa, "qT_ready"), (1, "k", kca, "kc_ready")):
                    pool.wait_ge(A[ready], b + 1)
                    if later(b):
                        pool.wait_ge(A[n + "3"], b)
                    g.tensor_tensor(rem[u][:], whole[:], parts[u][:, 0, 0:N], ALU.subtract).then_inc(A[n + "rem"], 1)
                for u, n in ((0, "q"), (1, "k")):
                    pool.wait_ge(A[n + "2"], b + 1)
                    g.tensor_tensor(parts[u][:, 2, 0:N], rem[u][:], parts[u][:, 1, 0:N], ALU.subtract).then_inc(A[n + "3"], 1)

            split(0)
            with pool.Fori(1, B) as b:
                split(b)

            def root(k, u, b, rows, nt):
                pool.wait_ge(Bs[f"veps{k}"], b + 1)
                g.tensor_tensor(rstd[u][0:rows, 0:nt], veps[u][0:rows, 0:nt], mhalf[0:rows, 0:nt], ALU.pow).then_inc(Bs[f"rstd{k}"], 1)

            def q_split(b):
                pool.wait_ge(Bs["q_hi"], b + 1)
                g.tensor_tensor(q_lo[0:TP].rearrange("p t c -> p (t c)"), qrow[0:TP].rearrange("p t c -> p (t c)"),
                                q_hi[0:TP].bitcast(F32).rearrange("p t c -> p (t c)"), ALU.subtract).then_inc(Bs["q_lo"], 1)
                yield

            def tail(b):
                for _ in range(5):
                    yield
                root(1, 0, b, TP, NT)
                yield

            def rest(i):
                for slot in range(ORDER.count("K")):
                    if slot == 4:
                        root(2, 1, i, TP, NT)
                    if slot == 7:
                        root(3, 1, i, PR, PT_)
                        root(4, 1, i, PR, PT_)
                    if slot == 12:
                        root(5, 1, i, PR, PT_)
                    if slot == 17:
                        pool.wait_ge(Bs["h2nT"], i + 1)
                        if later(i):
                            for half in range(2):
                                pool.wait_ge(m_h[half], E * i)
                        pool.sem_inc(s_alone, 1)
                        g.tensor_copy(h2nT_m[:], h2nT[:]).then_inc(Bs["h2nT_m"], 1)
                    yield

            def experts(b):
                def weigh(e):
                    pool.wait_ge(m_relu, NF * (E * b + e + 1))
                    if e % 4 == 0:
                        pool.wait_ge(Bs[f"gates{e // 4}"], 16 * (b + 1))
                    g.tensor_tensor(mh[e % 2][:], mh[e % 2][:], gate_bc[:, e, None, :].to_broadcast([128, NF, NP]),
                                    ALU.mult).then_inc(m_gated, 1)

                weigh(0)
                yield
                for e in range(E):
                    if e + 1 < E:
                        weigh(e + 1)
                        yield
                    yield

            all_batches(pool, no_steps, q_split, no_steps, tail, rest, experts)

        @block.vector
        def _(dve):
            vv = nc.vector
            dve.wait_ge(s_w0, 16 * EARLY)
            cnt = [0]

            def setup(ins):
                cnt[0] += 1
                ins.then_inc(T["chain"], 1)
                dve.wait_ge(T["chain"], cnt[0])

            dve.wait_ge(s_lam, 1)
            setup(vv.tensor_scalar(lam[:, 1:2], lam[:, 1:2], 0.001, None, ALU.max))
            setup(vv.tensor_tensor(lam[:, 2:3], lam[:, 1:2], lam[:, 1:2], ALU.mult))
            setup(vv.tensor_scalar(lam[:, 1:2], lam[:, 2:3], 2.0, None, ALU.mult))
            setup(vv.reciprocal(lam[:, 2:3], lam[:, 1:2]))
            vv.tensor_scalar(lam[:, 3:4], lam[:, 2:3], -1.0, None, ALU.mult).then_inc(s_set, 1)
            dve.wait_ge(s_set, NSET)

            def a_batch(b):
                dve.wait_ge(A["kT_ready"], b + 1)
                vv.tensor_scalar(ksum[:, 1:2], ksum[:, 0:1], -1.0 / N, None, ALU.mult).then_inc(A["mean_ready"], 1)

            def a_max(b, ahead=None):
                for n in range(H):
                    if ahead is not None and n == 4:
                        a_batch(ahead)
                    dve.wait_ge(A["scores"], 8 * b + n + 1)
                    vv.tensor_reduce(maxes[0:TP, :, bass.ds(H * b + n, 1)].rearrange("p t k -> p (t k)"),
                                     ps[0:TP, 3 * (n % 2):3 * (n % 2) + 3, 0:N], AX.X, ALU.max).then_inc(A["maxed"], 1)

            a_batch(0)
            a_batch(1)
            a_max(0, 2)
            with dve.Fori(1, B - 2) as b:
                a_max(b, b + 2)
            a_max(B - 2)
            a_max(B - 1)

            def choose(gr):
                dve.wait_ge(T["turned"], gr + 1)
                if gr:
                    dve.wait_ge(T["stored"], 2 * 16)
                    dve.wait_ge(T["idx_turned"], 1)
                vv.tensor_copy(mrow[:], ps[:, 6, 0:N]).then_inc(T["rows"], 1)
                dve.wait_ge(T["rows"], gr + 1)
                src = mrow
                for r in range(S // 8):
                    t8 = top_v[:, 8 * r:8 * r + 8]
                    setup(vv.max(t8, src[:]))
                    setup(vv.max_index(top_i[:, 8 * r:8 * r + 8], t8, src[:]))
                    if r < S // 8 - 1:
                        dst = mwork if src is mrow else mrow
                        setup(vv.match_replace(dst[:], t8, src[:], -BIG))
                        src = dst
                    yield
                setup(vv.tensor_copy(top_if[:], top_i[:]))
                setup(vv.memset(top_if[:, TOP:S], -1.0))
                setup(vv.memset(top_v[:, TOP:S], 0.0))
                vv.tensor_scalar(top_r[:], top_v[:], -1.0, None, ALU.mult).then_inc(T["idx_ready"], 1)
                yield

            def columns(gr):
                dve.wait_ge(T["idx_turned"], gr + 1)
                vv.tensor_copy(idx_col[:, 128 * gr:128 * gr + 128], ps[0:S, 7, 0:128]).then_inc(T["idx_col"], 1)
                dve.wait_ge(T["idx_col"], gr + 1)

            for _ in choose(0):
                pass
            columns(0)
            dve.wait_ge(s_w, 16 * (len(loads) - EARLY))

            W = Bs

            def chained(b, sem_, per):
                k = [0]

                def link(ins, alone=False):
                    k[0] += 1
                    ins.then_inc(sem_, 1)
                    dve.wait_ge(sem_, b * per + k[0])
                    if alone:
                        dve.sem_inc(s_alone, 1)

                return link, k

            def moments(b, link, u, src, rows, nt, n):
                for t in range(nt):
                    last = vv.bn_stats(st[u][0:rows, t, :], src(t))
                link(last, alone=True)
                for t in range(nt):
                    last = vv.bn_aggr(mv[u][0:rows, t, :], st[u][0:rows, t, :])
                last.then_inc(W[f"aggr{n}"], 1)
                dve.wait_ge(W[f"aggr{n}"], b + 1)
                vv.tensor_scalar(veps[u][0:rows, 0:nt], mv[u][0:rows, 0:nt, 1], EPS, None, ALU.add).then_inc(W[f"veps{n}"], 1)

            def norm(b, link, u, src, dst, rows, nt, n):
                moments(b, link, u, src, rows, nt, n)
                dve.wait_ge(W[f"rstd{n}"], b + 1)
                for t in range(nt):
                    last = vv.tensor_scalar(dst(t), src(t), mv[u][0:rows, t, 0:1], rstd[u][0:rows, t:t + 1],
                                            ALU.subtract, ALU.mult)
                return last

            def row_picks(b):
                dve.wait_ge(W["idx_loaded"], 16 * (b + 1))
                if later(b):
                    dve.wait_ge(W["gathered"], b)
                for t in range(NT):
                    last = vv.tensor_scalar(pick[0:TP, t, :], idx_bc[0:TP, :], kc[0:TP, K_TOK + t:K_TOK + t + 1], None, ALU.is_equal)
                last.then_inc(W["pick"], 1)
                yield

            def head(b):
                yield
                dve.wait_ge(W["qv_proj"], b + 1)
                qv = ps[0:TP, 0:2, :].rearrange("p a c -> p (a c)")[:, 0:256 * NT].rearrange("p (t c) -> p t c", t=NT)
                vv.tensor_tensor(qrow[0:TP], qv[:, :, 0:C], bqv_bc[0:TP, None, 0:C].to_broadcast([TP, NT, C]), ALU.add).then_inc(W["q_rows"], 1)
                for t in range(NT):
                    last = vv.tensor_tensor(v[0:TP, t, 0:H * VW].rearrange("p (h c) -> p h c", c=VW)[:, :, 0:DK],
                                            qv[:, t, C:2 * C].rearrange("p (h c) -> p h c", c=DK),
                                            bqv_bc[0:TP, C:2 * C].rearrange("p (h c) -> p h c", c=DK), ALU.add)
                last.then_inc(W["v_rows"], 1)
                dve.wait_ge(W["kT"], b + 1)
                vv.tensor_scalar(ksum_b[:, 1:2], ksum_b[:, 0:1], -1.0 / N, None, ALU.mult).then_inc(W["kmean"], 1)
                dve.wait_ge(W["kmean"], b + 1)
                for u in range(2):
                    last = vv.tensor_scalar(kTc[u][64 * u:64 * u + 64], kT[64 * u:64 * u + 64], ksum_b[64 * u:64 * u + 64, 1:2],
                                            None, ALU.add)
                last.then_inc(W["kTc"], 1)
                dve.wait_ge(W["xT"], b + 1)
                vv.tensor_scalar(xmean[:], mean_w[:], xsum[:], None, ALU.mult).then_inc(W["xmean"], 1)
                yield
                dve.wait_ge(W["gathered"], b + 1)
                for u in range(2):
                    last = vv.tensor_tensor(qsel[64 * u:64 * u + 64, 384 * u:384 * u + 384], ps[64 * u:64 * u + 64, u, 0:384],
                                            kc[64 * u:64 * u + 64, K_BM + 384 * u:K_BM + 384 * u + 384], ALU.mult)
                last.then_inc(W["qsel"], 1)
                dve.wait_ge(W["x_loaded"], 16 * (b + 1))
                vv.tensor_tensor(xb[0:TP], x[0:TP], bo_bc[0:TP, None, :].to_broadcast([TP, NT, C]), ALU.add).then_inc(W["xb"], 1)
                yield

            def tail(b):
                link, k = chained(b, chain_f, CF)
                dve.wait_ge(W["vmean"], b + 1)
                link(vv.tensor_tensor(vrow[:], ps[0:S, 2, 0:C], bqv_bc[0:S, C:2 * C], ALU.add))
                vm = vrow[:].rearrange("p (h c) -> p h c", c=DK)
                if later(b):
                    dve.wait_ge(W["scattered"], b)
                vv.tensor_scalar(vmw[:], vm, kc[0:S, K_M + 1:K_M + 2], None, ALU.mult)
                link(vv.tensor_scalar(self_row[:].rearrange("p (h c) -> p h c", c=DK), vm, kc[0:S, K_M:K_M + 1], None, ALU.mult))
                link(vv.tensor_copy(opad[0][:, 0:C], self_row[:]))
                vv.tensor_tensor(opad[1][:, 0:C], self_row[:], opad[0][:, 0:C].bitcast(F32), ALU.subtract)
                yield
                vv.tensor_scalar(place[:, 0, :], kc[0:S, K_ROW:K_ROW + NE], idx_col[:, bass.ds(H * b, 1)],
                                 kc[0:S, K_M:K_M + 1], ALU.is_equal, ALU.max)
                for h in range(1, 4):
                    vv.tensor_scalar(place[:, h, :], kc[0:S, K_ROW:K_ROW + NE], idx_col[:, bass.ds(H * b + h, 1)],
                                     None, ALU.is_equal)
                yield
                for h in range(4, H):
                    last = vv.tensor_scalar(place[:, h, :], kc[0:S, K_ROW:K_ROW + NE], idx_col[:, bass.ds(H * b + h, 1)],
                                            None, ALU.is_equal)
                last.then_inc(W["place"], 1)
                yield
                dve.wait_ge(W["av"], b + 1)
                av = ps[0:S, 0:2, 0:384].rearrange("p a (h c) -> p a h c", c=S)
                link(vv.reciprocal(rden[:].rearrange("p (a h) -> p a h", a=2)[:, :, :, None], av[:, :, :, DK:VW]))
                for half in range(2):
                    last = vv.tensor_tensor(onorm[:, 4 * half:4 * half + 4, :], av[:, half, :, 0:DK],
                                            rden[:, 4 * half:4 * half + 4, None].to_broadcast([S, 4, DK]), ALU.mult)
                link(last)
                link(vv.tensor_tensor(on_all[:], onorm[:], vmw[:], ALU.subtract))
                hi, lo = (o[:].rearrange("p (h c) -> p h c", c=C + DK)[:, :, 0:DK] for o in opad)
                link(vv.tensor_copy(hi, on_all[:]))
                vv.tensor_tensor(lo, on_all[:], hi.bitcast(F32), ALU.subtract).then_inc(W["on"], 1)
                yield
                yield
                dve.wait_ge(W["oproj"], b + 1)
                dve.wait_ge(W["xb"], b + 1)
                vv.tensor_tensor(r1[0:TP].rearrange("p t c -> p (t c)"), ps[0:TP, 0, 0:NT * C],
                                 xb[0:TP].rearrange("p t c -> p (t c)"), ALU.add).then_inc(W["r1"], 1)
                dve.wait_ge(W["r1"], b + 1)
                if later(b):
                    dve.wait_ge(W["x1_turned"], b)
                norm(b, link, 0, lambda t: r1[0:TP, t, :], lambda t: xn[0:TP, t, :], TP, NT, 1).then_inc(W["xn1"], 1)
                assert k[0] == CF, ("CF", k[0])
                yield

            def rest(i):
                link, k = chained(i, chain_k, CK)
                yield
                yield
                yield
                dve.wait_ge(W["ffn2"], i + 1)
                vv.scalar_tensor_tensor(yT[:], ps[:, 4, 0:N], vecs[:, 0:1], x1T[:], ALU.add, ALU.add).then_inc(W["yT"], 1)
                yield
                dve.wait_ge(W["y_turned"], i + 1)
                norm(i, link, 1, lambda t: ps[0:TP, 3, C * t:C * t + C], lambda t: xn2[0:TP, t, :], TP, NT, 2).then_inc(W["xn2"], 1)
                yield
                yield
                dve.wait_ge(W["cp"], i + 1)
                link(vv.tensor_tensor(mx[:], cp[:, 0:2 * NP:2], cp[:, 1:2 * NP:2], ALU.max))
                link(vv.tensor_tensor(mx[:], mx[:], cp[:, 2:2 * NP + 1:2], ALU.max))
                vv.tensor_scalar(el[:], mx[:], 0.0, None, ALU.min).then_inc(W["mx"], 1)
                dve.wait_ge(W["emn"], i + 1)
                link(vv.tensor_scalar(emn[:], emn[:], -1.0, None, ALU.add))
                vv.scalar_tensor_tensor(el[:], mx[:], 0.0, emn[:], ALU.max, ALU.add).then_inc(W["el"], 1)
                yield
                dve.wait_ge(W["el_turned"], i + 1)
                moments(i, link, 1, lambda t: ps[0:PR, 4, C * t:C * t + C], PR, PT_, 3)
                for t in range(PT_):
                    last = vv.scalar_tensor_tensor(xn3[0:PR, t, :], ps[0:PR, 4, C * t:C * t + C], mv[1][0:PR, t, 0:1],
                                                   cng_bc[0:PR, :], ALU.subtract, ALU.mult)
                link(last)
                dve.wait_ge(W["rstd3"], i + 1)
                for t in range(PT_):
                    last = vv.scalar_tensor_tensor(hrow[0:PR, t, :], xn3[0:PR, t, :], rstd[1][0:PR, t:t + 1],
                                                   cnb_bc[0:PR, :], ALU.mult, ALU.add)
                link(last)
                norm(i, link, 1, lambda t: hrow[0:PR, t, :], lambda t: hn[0:PR, t, :], PR, PT_, 4).then_inc(W["hn"], 1)
                yield
                yield
                yield
                dve.wait_ge(W["dist"], i + 1)
                vv.tensor_reduce(dmin[0:PR], ps[0:PR, 4, 0:PT_ * NP].rearrange("p (t m) -> p t m", t=PT_), AX.X, ALU.min)
                link(vv.tensor_scalar(d2[0:PR].rearrange("p t m -> p (t m)"), ps[0:PR, 4, 0:PT_ * NP], 0.0, None, ALU.max))
                vv.tensor_scalar(dbias[0:PR], dmin[0:PR], 0.0, lam[0:PR, 2:3], ALU.max, ALU.mult).then_inc(W["dclip"], 1)
                yield
                dve.wait_ge(W["e2x"], PT_ * (i + 1))
                link(vv.reciprocal(rr2[0:PR], rs2[0:PR]))
                yield
                dve.wait_ge(W["av2"], i + 1)
                for t in range(PT_):
                    last = vv.scalar_tensor_tensor(h2[0:PR, t, :], ps[0:PR, 4, C * t:C * t + C], rr2[0:PR, t:t + 1],
                                                   hrow[0:PR, t, :], ALU.mult, ALU.add)
                link(last)
                norm(i, link, 1, lambda t: h2[0:PR, t, :], lambda t: xn4[0:PR, t, :], PR, PT_, 5).then_inc(W["xn4"], 1)
                yield
                yield
                dve.wait_ge(W["router"], i + 1)
                logits = vv.tensor_tensor(lg[0:PR], ps[0:PR, 4, 0:PT_ * E].rearrange("p (t e) -> p t e", t=PT_),
                                          br_bc[0:PR, None, :].to_broadcast([PR, PT_, E]), ALU.add)
                link(logits, alone=True)
                for t in range(PT_):
                    last = vv.max(m8[0:PR, t, :], lg[0:PR, t, :])
                link(last)
                vv.tensor_tensor(lgd[0:PR, :, 0:E], lg[0:PR], m8[0:PR, :, 0:1].to_broadcast([PR, PT_, E]), ALU.subtract)
                vv.tensor_tensor(lgd[0:PR, :, E:E + 2], m8[0:PR, :, 0:2], m8[0:PR, :, 0:1].to_broadcast([PR, PT_, 2]),
                                 ALU.subtract).then_inc(W["lg"], 1)
                for t in range(PT_):
                    last = vv.max_index(i8[0:PR, t, :], m8[0:PR, t, :], lg[0:PR, t, :])
                link(last)
                link(vv.tensor_copy(i8f[0:PR], i8[0:PR]))
                dve.wait_ge(W["elg"], i + 1)
                link(vv.tensor_reduce(rse[0:PR], elg[0:PR, :, 0:E], AX.X, ALU.add))
                link(vv.reciprocal(rre[0:PR], rse[0:PR]))
                link(vv.tensor_tensor(p12[0:PR], elg[0:PR, :, E:E + 2], rre[0:PR, :, None].to_broadcast([PR, PT_, 2]), ALU.mult))
                for t in range(PT_):
                    vv.tensor_scalar(gateA[0:PR, t, :], kc[0:PR, K_E8:K_E8 + E], i8f[0:PR, t, 0:1], p12[0:PR, t, 0:1],
                                     ALU.is_equal, ALU.mult)
                    last = vv.tensor_scalar(gateB[0:PR, t, :], kc[0:PR, K_E8:K_E8 + E], i8f[0:PR, t, 1:2], p12[0:PR, t, 1:2],
                                            ALU.is_equal, ALU.mult)
                link(last)
                vv.tensor_tensor(gate[0:PR], gateB[0:PR], gateA[0:PR], ALU.add).then_inc(W["gate"], 1)
                yield
                yield
                yield
                if later(i):
                    dve.wait_ge(W["h2_kept"], i)
                    if not isinstance(i, int) or i >= 2:
                        dve.wait_ge(W["out_stored"], 16 * (i - 1))
                    vv.tensor_copy(ostage[0:PR], h2_m[0:PR]).then_inc(W["h2_held"], 1)
                    dve.wait_ge(W["h2_held"], i)
                vv.tensor_copy(h2_m[0:PR], h2[0:PR]).then_inc(W["h2_kept"], 1)
                assert k[0] == CK, ("CK", k[0])
                yield

            def finish(b):
                dve.wait_ge(W["out_turned"], b + 1)
                dve.wait_ge(W["h2_held"], b + 1)
                vv.tensor_tensor(ostage[0:PR].rearrange("p t c -> p (t c)"), ps[0:PR, 5, 256:256 + PT_ * C],
                                 ostage[0:PR].rearrange("p t c -> p (t c)"), ALU.add).then_inc(W["out_ready"], 1)

            def experts(b):
                if later(b):
                    finish(b - 1)
                yield

            all_batches(dve, row_picks, no_steps, head, tail, rest, experts, choose(1), lambda: columns(1))
            dve.wait_ge(W["h2_kept"], B)
            dve.wait_ge(W["out_stored"], 16 * (B - 1))
            vv.tensor_copy(ostage[0:PR], h2_m[0:PR]).then_inc(W["h2_held"], 1)
            finish(B - 1)


def kernel(**inputs):
    import numpy as _np
    import concourse.bacc as _bacc
    from concourse import mybir as _mybir
    from concourse.bass_utils import run_bass_kernel_spmd as _run

    w = {k.split("_", 1)[1]: _np.asarray(v) for k, v in inputs.items() if k != "x"}
    tok = {k[4:]: v for k, v in w.items() if k.startswith("tok_")}
    att = {k[5:]: v for k, v in w.items() if k.startswith("attn_")}
    moe = {k[4:]: v for k, v in w.items() if k.startswith("ffn_")}
    laid = {
        "x": _np.asarray(inputs["x"]),
        "consts": shape_constants(),
        "qkv_w": tok["qkv_w"],
        "qkv_b": tok["qkv_b"].reshape(1, -1),
        "qk_bT": tok["qkv_b"][:2 * C].reshape(2, C).T,
        "out_w": tok["out_w"],
        "out_b": tok["out_b"].reshape(1, -1),
        "ffn_w1": tok["ffn_w1"],
        "ffn_b1": tok["ffn_b1"].reshape(NF, 128).T,
        "ffn_w2": tok["ffn_w2"],
        "vecs": _np.stack([tok[n] for n in ("ffn_b2", "n1_g", "n1_b", "n2_g", "n2_b", "conv_b")], axis=1),
        "conv_w": tok["conv_w"].transpose(1, 2, 0),
        "cn_g": tok["cn_g"].reshape(1, -1),
        "cn_b": tok["cn_b"].reshape(1, -1),
        "WqT": att["Wq"].T,
        "WkT": att["Wk"].T,
        "WvT": att["Wv"].T,
        "log_lambda": att["log_lambda"].reshape(1, 1),
        "Wr": moe["Wr"],
        "br": moe["br"].reshape(1, -1),
        "W1": moe["W1"],
        "mb1": moe["b1"].reshape(E * NF, 128).T,
        "W2": moe["W2"],
        "b2": moe["b2"],
    }
    nc = _bacc.Bacc("TRN2", target_bir_lowering=False, num_devices=1)
    arrays, aps = {}, {}
    for name, value in laid.items():
        value = _np.ascontiguousarray(value)
        arrays[f"in_{name}"] = value
        aps[name] = nc.dram_tensor(f"in_{name}", value.shape, _mybir.dt.from_np(value.dtype), kind="ExternalInput").ap()
    out = nc.dram_tensor("out_0", (B, NP, C), _mybir.dt.float32, kind="ExternalOutput").ap()
    audio_tower(nc, aps, out)
    r = _run(nc, [arrays], core_ids=[0])
    return r.results[0]["out_0"]
```
